# Optimizing a Trainium2 kernel written in Bass

```python
import numpy as np
import jax
import jax.numpy as jnp

def _softmax(x, axis=-1):
    return jax.nn.softmax(x, axis=axis)

def _gelu(x):
    return jax.nn.gelu(x, approximate=True)

def _silu(x):
    return jax.nn.silu(x)

def _sigmoid(x):
    return jax.nn.sigmoid(x)

def _layernorm(x, axis=-1, eps=1e-05):
    m = jnp.mean(x, axis=axis, keepdims=True)
    v = jnp.var(x, axis=axis, keepdims=True)
    return (x - m) / jnp.sqrt(v + eps)

def _scatter_add(tgt, idx, src, axis=0):
    return tgt.at[idx].add(src)

def _segment_sum(src, seg, n):
    return jax.ops.segment_sum(src, seg, n)
kernel_name = 'mk_pixart_resid_d1_seqx_r4_a49365'

def setup_inputs(seed: int=0):
    np.random.seed(seed)
    _w = jnp.asarray

    def _rec_inputs():
        import jax
        import jax.numpy as jnp
        _rk = jax.random.key(seed)
        x = 7.22e-05 + 1 * jax.random.normal(jax.random.fold_in(_rk, 1), (32, 128, 256), jnp.float32)
        _lenS = 128 - jax.random.randint(jax.random.fold_in(_rk, 7), (32,), 0, max(1, 128 // 4) + 1, jnp.int32)
        _lenS2 = 128 - jax.random.randint(jax.random.fold_in(_rk, 8), (32,), 0, max(1, 128 // 4) + 1, jnp.int32)
        _ctx_1024P = jax.random.normal(jax.random.fold_in(_rk, 11), (32, 16, 256), jnp.float32)
        _ctx_1024c = jax.random.dirichlet(jax.random.fold_in(_rk, 511), 0.3 * jnp.ones((16,), jnp.float32), (32, 128))
        _ctx_1024t = jnp.einsum('bsk,bkd->bsd', _ctx_1024c, _ctx_1024P)
        _ctx_1024t = _ctx_1024t * jax.lax.rsqrt(jnp.mean(jnp.square(_ctx_1024t)) + 1e-12) * 0.953939
        ctx_1024 = 4.13588e-05 + 0.999923 * (_ctx_1024t + 0.3 * jax.random.normal(jax.random.fold_in(_rk, 611), (32, 128, 256), jnp.float32))
        condB_tau = jax.random.uniform(jax.random.fold_in(_rk, 12), (32,), jnp.float32, 0.0, 1.45372)
        fside_BxS2_0 = 0.0088954 + 1.00633 * jax.random.normal(jax.random.fold_in(_rk, 13), (32, 128), jnp.float32)
        return (x, ctx_1024, condB_tau, fside_BxS2_0)
    x, ctx_1024, condB_tau, fside_BxS2_0 = _rec_inputs()

    def _L0_xcond_setup():
        import jax, jax.numpy as jnp
        import numpy as np
        D_MODEL = 256
        N_HEADS = 16
        key = jax.random.key(seed)
        ks = jax.random.split(key, 16)
        B, L, S, D = (4, 512, 512, D_MODEL)
        inp = {'q': jax.random.normal(ks[0], (B, L, D), jnp.float32), 'k': jax.random.normal(ks[1], (B, S, D), jnp.float32), 'v': jax.random.normal(ks[2], (B, S, D), jnp.float32), 'tau': jax.random.uniform(ks[3], (B, 1), jnp.float32, 0.5, 1.5), 'delta': jax.random.normal(ks[4], (B, S), jnp.float32)}
        s = 1.0 / np.sqrt(D)
        inp['Wq'] = jax.random.normal(ks[5], (D, D), jnp.float32) * s
        inp['bq'] = jnp.zeros((D,), jnp.float32)
        inp['Wk'] = jax.random.normal(ks[6], (D, D), jnp.float32) * s
        inp['bk'] = jnp.zeros((D,), jnp.float32)
        inp['Wv'] = jax.random.normal(ks[7], (D, D), jnp.float32) * s
        inp['bv'] = jnp.zeros((D,), jnp.float32)
        inp['Wo'] = jax.random.normal(ks[8], (D, D), jnp.float32) * s
        inp['bo'] = jnp.zeros((D,), jnp.float32)
        return inp
    _L0_xcond_all = _L0_xcond_setup()
    _L0_xcond_in = {k: v for k, v in _L0_xcond_all.items() if k in ('Wq', 'bq', 'Wk', 'bk', 'Wv', 'bv', 'Wo', 'bo')}
    del _L0_xcond_all

    def _L0_ffn_setup():
        import jax, jax.numpy as jnp
        import numpy as np
        TOP_K = 2
        key = jax.random.key(seed)
        k0, k1, k2, k3, k4 = jax.random.split(key, 5)
        B, S, D, H, E = (4, 512, 256, 512, 8)
        x = jax.random.normal(k0, (B, S, D), dtype=jnp.float32)
        router_w = jax.random.normal(k1, (E, D), dtype=jnp.float32) * D ** (-0.5)
        w_gate = jax.random.normal(k2, (E, D, H), dtype=jnp.float32) * D ** (-0.5)
        w_up = jax.random.normal(k3, (E, D, H), dtype=jnp.float32) * D ** (-0.5)
        w_down = jax.random.normal(k4, (E, H, D), dtype=jnp.float32) * H ** (-0.5)
        return {'x': x, 'router_w': router_w, 'w_gate': w_gate, 'w_up': w_up, 'w_down': w_down}
    _L0_ffn_all = _L0_ffn_setup()
    _L0_ffn_in = {k: v for k, v in _L0_ffn_all.items() if k in ('router_w', 'w_gate', 'w_up', 'w_down')}
    del _L0_ffn_all
    return {'x': x, 'ctx_1024': ctx_1024, 'condB_tau': condB_tau, 'fside_BxS2_0': fside_BxS2_0, 'L0_xcond_Wq': _L0_xcond_in['Wq'], 'L0_xcond_bq': _L0_xcond_in['bq'], 'L0_xcond_Wk': _L0_xcond_in['Wk'], 'L0_xcond_bk': _L0_xcond_in['bk'], 'L0_xcond_Wv': _L0_xcond_in['Wv'], 'L0_xcond_bv': _L0_xcond_in['bv'], 'L0_xcond_Wo': _L0_xcond_in['Wo'], 'L0_xcond_bo': _L0_xcond_in['bo'], 'L0_ffn_router_w': _L0_ffn_in['router_w'], 'L0_ffn_w_gate': _L0_ffn_in['w_gate'], 'L0_ffn_w_up': _L0_ffn_in['w_up'], 'L0_ffn_w_down': _L0_ffn_in['w_down']}

def reference(x, ctx_1024, condB_tau, fside_BxS2_0, L0_xcond_Wq, L0_xcond_bq, L0_xcond_Wk, L0_xcond_bk, L0_xcond_Wv, L0_xcond_bv, L0_xcond_Wo, L0_xcond_bo, L0_ffn_router_w, L0_ffn_w_gate, L0_ffn_w_up, L0_ffn_w_down):
    import jax
    import jax.numpy as jnp

    def _L0_xcond_ref(q, k, v, tau, delta, Wq, bq, Wk, bk, Wv, bv, Wo, bo):
        import jax, jax.numpy as jnp
        import numpy as np
        D_MODEL = 256
        N_HEADS = 16
        B, L, D = q.shape
        S = k.shape[1]
        H = N_HEADS
        E = D // H
        qh = (q @ Wq.T + bq).reshape(B, L, H, E)
        kh = (k @ Wk.T + bk).reshape(B, S, H, E)
        vh = (v @ Wv.T + bv).reshape(B, S, H, E)
        scale = 1.0 / np.sqrt(E).astype(np.float32)
        scores = jnp.einsum('blhe,bshe->bhls', qh, kh)
        scores = scores * tau[:, None, None, :] + delta[:, None, None, :]
        a = jax.nn.softmax(scale * scores, axis=-1)
        out = jnp.einsum('bhls,bshd->blhd', a, vh).reshape(B, L, D)
        return out @ Wo.T + bo

    def _L0_ffn_ref(x, router_w, w_gate, w_up, w_down):
        import jax, jax.numpy as jnp
        import numpy as np
        TOP_K = 2
        B, S, D = x.shape
        E = router_w.shape[0]
        xt = x.reshape(-1, D)
        logits = xt @ router_w.T
        topk_vals, topk_idx = jax.lax.top_k(logits, TOP_K)
        g = jax.nn.sigmoid(topk_vals)
        g = g / (g.sum(axis=-1, keepdims=True) + 1e-10)
        out = jnp.zeros_like(xt)
        for e in range(E):
            ge = jnp.sum(jnp.where(topk_idx == e, g, jnp.zeros_like(g)), axis=-1)
            h = jax.nn.silu(xt @ w_gate[e]) * (xt @ w_up[e])
            out = out + ge[:, None] * (h @ w_down[e])
        return out.reshape(B, S, D)
    x = x + _L0_xcond_ref(_layernorm(x, axis=-1), ctx_1024, ctx_1024, condB_tau[:, None], fside_BxS2_0, L0_xcond_Wq, L0_xcond_bq, L0_xcond_Wk, L0_xcond_bk, L0_xcond_Wv, L0_xcond_bv, L0_xcond_Wo, L0_xcond_bo)
    x = x + _L0_ffn_ref(_layernorm(x, axis=-1), L0_ffn_router_w, L0_ffn_w_gate, L0_ffn_w_up, L0_ffn_w_down)
    return x

_drawn_inputs = setup_inputs


def setup_inputs(seed=0):
    import zlib

    import numpy as np

    out = dict(_drawn_inputs(seed))
    spreads = {'L0_xcond_bq': (0.0, 0.1),
     'L0_xcond_bk': (0.0, 0.1),
     'L0_xcond_bv': (0.0, 0.1),
     'L0_xcond_bo': (0.0, 0.1)}
    factors = {}
    for name, (base, spread) in spreads.items():
        noise = np.random.default_rng([zlib.crc32(name.encode()), seed]).standard_normal(out[name].shape)
        drawn = base * np.exp(spread * noise) if base else spread * noise
        out[name] = jnp.asarray(drawn.astype(out[name].dtype))
    for name, factor in factors.items():
        out[name] = (out[name] * factor).astype(out[name].dtype)
    return out
```

```python
from contextlib import ExitStack

import concourse.bass as bass
from concourse import mybir

F32 = mybir.dt.float32
F32R = mybir.dt.float32r
BF16 = mybir.dt.bfloat16
I32 = mybir.dt.int32
U32 = mybir.dt.uint32
ALU = mybir.AluOpType
ACT = mybir.ActivationFunctionType
AX = mybir.AxisListType

P = 128
NB, L, D = 32, 128, 256
H, E = 16, 16
KC = D // P
G = 4
PADH = 32
NE, F = 8, 512
FC = F // P
TOK = NB * L
UB = 2
UT = UB * L
NU = NB // UB
NSTEP = NB * G
SPI = 16
BPI, UPI = SPI // G, SPI // G // UB
NIT = NSTEP // SPI
FILLS = 7
REG = TOK + P
NT = 2 * TOK // P + NE
ROWS = NE * REG + NE * P
PW = D + 2
SCALE = 0.25
TPI = 4
LN_EPS = 1e-5


def inside(it, per, c, total):
    return not isinstance(it, int) or 0 <= per * it + c < total


def build(nc, x, ctx_in, tau, delta, Wq, bq, Wk, bk, Wv, bv, Wo, bo, router, w_gate, w_up, w_down, out):
    routed = nc.dram_tensor("routed_rows", (ROWS, PW), F32, kind="Internal").ap()
    expert_out = nc.dram_tensor("expert_rows", (2 * TOK, D), F32, kind="Internal").ap()
    x_flat = x.rearrange("b l d -> l b d")
    c_flat = ctx_in.rearrange("b l d -> l b d")
    out_flat = out.rearrange("b l d -> l b d")
    delta_row = delta.rearrange("(o b) s -> o (b s)", o=1)

    with ExitStack() as stack:
        def sb(name, shape, dt=F32):
            return stack.enter_context(nc.sbuf_tensor(name, shape, dt))

        def sem(name):
            return stack.enter_context(nc.semaphore(name))

        X1 = sb("X1", [P, NB * D])
        WGU = sb("WGU", [P, NE * KC * 2 * F])
        WDN = sb("WDN", [P, NE * FC * D])
        ident = sb("ident", [P, P])
        WqT = sb("WqT", [P, KC, G, P])
        WkT = sb("WkT", [P, KC, G, P])
        WvT = sb("WvT", [P, KC, D])
        WoT = sb("WoT", [P, KC, D])
        WrT = sb("WrT", [P, KC, NE])
        ident_r = sb("ident_r", [P, P], F32R)
        before = sb("before", [P, P])
        before_b = sb("before_b", [P, P], BF16)
        ones_b = sb("ones_b", [P, P], BF16)
        bq_pad = sb("bq_pad", [P, G])
        bk_pad = sb("bk_pad", [P, G])
        bv_all = sb("bv_all", [P, D])
        bo_all = sb("bo_all", [P, D])
        tau_all = sb("tau_all", [P, NB])
        q_scale = sb("q_scale", [P, NB])
        row_i = sb("row_i", [P, 1], I32)
        row_f = sb("row_f", [P, 1])
        is_real = sb("is_real", [P, 1])
        is_delta = sb("is_delta", [P, 1])
        col_i = sb("col_i", [1, P], I32)
        col_f = sb("col_f", [1, P])
        delta_rows = sb("delta_rows", [1, P])
        minus_half = sb("minus_half", [P, UB])
        expert_i = sb("expert_i", [P, NE], I32)
        expert_f = sb("expert_f", [P, NE])
        base_i = sb("base_i", [P, NE], I32)
        counts = sb("counts", [P, NE])
        out_rows = sb("out_rows", [P, 2 * NB], I32)
        PAD = sb("PAD", [P, PW])
        CTX = sb("CTX", [P, 2, UB, D])
        DEL = sb("DEL", [1, 2, UT])
        ln_stats = sb("ln_stats", [P, UB, 6])
        ln_mv = sb("ln_mv", [P, UB, 2])
        ln_rstd = sb("ln_rstd", [P, UB])
        XN = sb("XN", [P, 2, UB, D])
        XNT = sb("XNT", [P, KC, UT])
        CT = sb("CT", [P, KC, UT])
        Q = sb("Q", [P, 2, G, UT])
        K = sb("K", [P, 2, G, UT])
        V = sb("V", [P, 2, UB, H, PADH])
        NM = sb("NM", [P, 2, G], F32R)
        AT = sb("AT", [P, 2, G * P])
        OT = sb("OT", [P, G * P])
        rden = sb("rden", [P, G, G])
        ON = sb("ON", [P, D])
        ONT = sb("ONT", [P, KC, P])
        st2 = sb("st2", [P, 6])
        mv2 = sb("mv2", [P, 2])
        rstd2 = sb("rstd2", [P, 1])
        XP = sb("XP", [P, 4, 2, PW])
        X2T = sb("X2T", [P, KC, P])
        lg = sb("lg", [P, NE])
        mx = sb("mx", [P, 8])
        mi = sb("mi", [P, 8], U32)
        mif = sb("mif", [P, 2])
        M = sb("M", [P, 2, NE])
        Mb = sb("Mb", [P, NE], BF16)
        ge = sb("ge", [P, 2])
        gp = sb("gp", [P, 2])
        gs = sb("gs", [P, 2])
        gsum = sb("gsum", [P, 1])
        grec = sb("grec", [P, 1])
        rank = sb("rank", [P, NE])
        rsel = sb("rsel", [P, 2, NE])
        slot_f = sb("slot_f", [P, 2])
        slot = [sb(f"slot{k}", [P, 1], I32) for k in range(2)]
        j_i = sb("j_i", [1, NB], I32)
        j_f = sb("j_f", [1, NB])
        t_i = sb("t_i", [1, NT], I32)
        t_f = sb("t_f", [1, NT])
        start_i = sb("start_i", [1, NE], I32)
        start_f = sb("start_f", [1, NE])
        cnt = sb("cnt", [1, NE])
        ntile = sb("ntile", [1, NE])
        ones8 = sb("ones8", [1, NE])
        upto = sb("upto", [1, NE])
        jump = sb("jump", [1, NE])
        te_f = sb("te_f", [1, NT])
        tr_f = sb("tr_f", [1, NT])
        end_i = sb("end_i", [1, NE], I32)
        te_i = sb("te_i", [1, NT], I32)
        tr_i = sb("tr_i", [1, NT], I32)

        PS = stack.enter_context(nc.psum_tensor("PS", [P, 8, 512], F32))

        setup_in = sem("setup_in")
        pool_const = sem("pool_const")
        dve_const = sem("dve_const")
        wt_turned = sem("wt_turned")
        wt_ready = sem("wt_ready")
        x_in = [sem(f"x_in{i}") for i in range(2)]
        c_in = [sem(f"c_in{i}") for i in range(2)]
        experts_in = sem("experts_in")
        ln1_stats = sem("ln1_stats")
        ln1_rstd = sem("ln1_rstd")
        xn_ready = sem("xn_ready")
        x_biased = sem("x_biased")
        pj_filled = sem("pj_filled")
        pj_free = sem("pj_free")
        s1_done = sem("s1_done")
        max_ready = sem("max_ready")
        s2_done = sem("s2_done")
        probs_ready = sem("probs_ready")
        av_done = sem("av_done")
        ot_ready = sem("ot_ready")
        ott_done = sem("ott_done")
        on_step = sem("on_step")
        ot2_done = sem("ot2_done")
        ont_ready = sem("ont_ready")
        wo_done = sem("wo_done")
        ln2_step = sem("ln2_step")
        ln2_rstd = sem("ln2_rstd")
        xp_ready = sem("xp_ready")
        xp_copied = sem("xp_copied")
        x2t_turned = sem("x2t_turned")
        x2t_ready = sem("x2t_ready")
        logits_done = sem("logits_done")
        gate_exp = sem("gate_exp")
        rank_done = sem("rank_done")
        route_step = sem("route_step")
        scattered = [sem(f"scattered{i}") for i in range(4)]
        dead_in = sem("dead_in")
        table_step = sem("table_step")
        pad_in = sem("pad_in")


        flat_q = Q[:, :, :, :].rearrange("p u g t -> p (u g t)")
        flat_k = K[:, :, :, :].rearrange("p u g t -> p (u g t)")
        flat_v = V[:, :, :, :, :].rearrange("p u b h r -> p (u b h r)")
        past = flat_v[0:1, 0:NT * NE].rearrange("p (t e) -> p t e", e=NE)
        pastj = flat_v[0:1, NT * NE:2 * NT * NE].rearrange("p (t e) -> p t e", e=NE)
        over = flat_v[0:1, 2 * NT * NE:2 * NT * NE + NE * NB].rearrange("p (e j) -> p e j", e=NE)
        XS = flat_v[:, 0:TPI * PW].rearrange("p (i w) -> p i w", i=TPI)
        XST = flat_q[:, 0:2 * D].rearrange("p (i w) -> p i w", i=2)
        SG = flat_q[:, 2 * D:2 * D + 2 * F].rearrange("p (i w) -> p i w", i=2)
        HS = flat_k[:, 0:2 * F].rearrange("p (i w) -> p i w", i=2)
        HST = flat_k[:, 2 * F:4 * F].rearrange("p (i w) -> p i w", i=2)
        YS = XN[:, :, :, :].rearrange("p u b d -> p (u b) d")
        META = sb("META", [P, TPI, 2])
        xs_in = [sem(f"xs_in{i}") for i in range(TPI)]
        xs_turned = sem("xs_turned")
        xst_ready = sem("xst_ready")
        meta_ready = sem("meta_ready")
        gu_done = sem("gu_done")
        silu_ready = sem("silu_ready")
        h_ready = sem("h_ready")
        h_turned = sem("h_turned")
        ht_ready = sem("ht_ready")
        down_done = sem("down_done")
        y_ready = sem("y_ready")
        y_out = [sem(f"y_out{i}") for i in range(TPI)]
        parts_in = [sem(f"parts_in{i}") for i in range(8)]
        sum_step = sem("sum_step")
        stored = sem("stored")

        def tile_blocks(eng, step):
            for it in (-1, 0):
                for loc in range(TPI):
                    step(it, loc)
            with eng.Fori(1, NT // TPI - 1) as it:
                for loc in range(TPI):
                    step(it, loc)
            for it in (NT // TPI - 1, NT // TPI):
                for loc in range(TPI):
                    step(it, loc)

        BQ = 4

        def part(q, k):
            return WGU[:, (k * NB + BQ * q) * D:(k * NB + BQ * (q + 1)) * D]

        def experts_sync(sp):
            for i in range(4):
                sp.wait_ge(scattered[i], 32 * NB // 4)
            sp.wait_ge(dead_in, 16 * NE)
            sp.wait_ge(pad_in, 16 * NE)
            sp.wait_ge(table_step, 12)

            def step(it, loc):
                t = loc + 2
                if inside(it, TPI, t, NT):
                    if inside(it, TPI, t - 4, NT):
                        sp.wait_ge(xs_turned, it * TPI + t - 3)
                        sp.wait_ge(meta_ready, it * TPI + t - 3)
                    row = sp.value_load(tr_i[0:1, bass.ds(it * TPI + t, 1)], min_val=0, max_val=ROWS - P)
                    sp.dma_start(XS[:, t % TPI, :], routed[bass.ds(row, P), :]).then_inc(xs_in[t % TPI], 16)

            tile_blocks(sp, step)
            sp.wait_ge(down_done, NT)
            for i in range(TPI):
                sp.wait_ge(y_out[i], 16 * NT // TPI)
            for q in range(NB // BQ):
                for k in range(2):
                    rows = expert_out[k * TOK + q * BQ * L:k * TOK + (q + 1) * BQ * L, :]
                    sp.dma_start(part(q, k).rearrange("p (b d) -> p b d", b=BQ),
                                 rows.rearrange("(b l) d -> l b d", b=BQ)).then_inc(parts_in[q], 16)
            for q in range(NB // BQ):
                sp.wait_ge(sum_step, 2 * (q + 1))
                sp.dma_start(out_flat[:, q * BQ:(q + 1) * BQ, :],
                             X1[:, q * BQ * D:(q + 1) * BQ * D].rearrange("p (b d) -> p b d", b=BQ)
                             ).then_inc(stored, 16)
            sp.wait_ge(stored, 16 * NB // BQ)

        def experts_pool(pool):
            def step(it, loc):
                t = loc + 1
                if inside(it, TPI, t, NT):
                    pool.wait_ge(xs_in[t % TPI], it * 16 + 16 * (t // TPI + 1))
                    if inside(it, TPI, t - 4, NT):
                        pool.wait_ge(y_out[t % TPI], it * 16 + 16 * (t // TPI))
                    pass_waits(pool)
                    pool.tensor_copy(META[:, t % TPI, :].bitcast(I32), XS[:, t % TPI, D:PW].bitcast(I32)
                                     ).then_inc(meta_ready, 1)
                t = loc - 2
                if inside(it, TPI, t, NT):
                    pool.wait_ge(y_ready, it * TPI + t + 1)
                    pass_waits(pool)
                    pool.indirect_dma_start(
                        expert_out[:, :], bass.IndirectOffsetOnAxis(ap=META[:, t % TPI, 1:2].bitcast(U32), axis=0),
                        YS[:, t % TPI, :], None, bounds_check=2 * TOK - 1, oob_is_err=False).then_inc(y_out[t % TPI], 16)

            tile_blocks(pool, step)

        def experts_scalar(act):
            def step(it, loc):
                t = loc
                if inside(it, TPI, t, NT):
                    act.wait_ge(gu_done, it * TPI + t + 1)
                    if inside(it, TPI, t - 2, NT):
                        act.wait_ge(h_ready, it * TPI + t - 1)
                    act.activation(SG[:, t % 2, :], bank(2 * (t % 2)), ACT.Silu).then_inc(silu_ready, 1)
                t = loc + 1
                if inside(it, TPI, t, NT):
                    act.wait_ge(xs_turned, it * TPI + t + 1)
                    if inside(it, TPI, t - 2, NT):
                        act.wait_ge(gu_done, it * TPI + t - 1)
                    act.activation(XST[:, t % 2, :], bank(4)[:, 0:D], ACT.Copy).then_inc(xst_ready, 1)
                t = loc - 1
                if inside(it, TPI, t, NT):
                    act.wait_ge(h_turned, it * TPI + t + 1)
                    if inside(it, TPI, t - 2, NT):
                        act.wait_ge(down_done, it * TPI + t - 1)
                    act.activation(HST[:, t % 2, :], bank(5), ACT.Copy).then_inc(ht_ready, 1)

            tile_blocks(act, step)

        def experts_vector(dve):
            def step(it, loc):
                t = loc
                if inside(it, TPI, t, NT):
                    dve.wait_ge(silu_ready, it * TPI + t + 1)
                    if inside(it, TPI, t - 2, NT):
                        dve.wait_ge(h_turned, it * TPI + t - 1)
                    dve.tensor_tensor(HS[:, t % 2, :], bank(2 * (t % 2) + 1), SG[:, t % 2, :], ALU.mult
                                      ).then_inc(h_ready, 1)
                t = loc - 2
                if inside(it, TPI, t, NT):
                    dve.wait_ge(down_done, it * TPI + t + 1)
                    dve.wait_ge(meta_ready, it * TPI + t + 1)
                    if inside(it, TPI, t - 4, NT):
                        dve.wait_ge(y_out[t % TPI], it * 16 + 16 * (t // TPI))
                    dve.tensor_scalar(YS[:, t % TPI, :], bank(6)[:, 0:D], META[:, t % TPI, 0:1], None, ALU.mult
                                      ).then_inc(y_ready, 1)

            tile_blocks(dve, step)
            for q in range(NB // BQ):
                dve.wait_ge(parts_in[q], 32)
                xq = X1[:, q * BQ * D:(q + 1) * BQ * D]
                dve.tensor_tensor(xq, xq, part(q, 0), ALU.add).then_inc(sum_step, 1)
                dve.wait_ge(sum_step, 2 * q + 1)
                dve.tensor_tensor(xq, xq, part(q, 1), ALU.add).then_inc(sum_step, 1)

        def experts_tensor(pe):
            pe.wait_ge(experts_in, 16 * 3 * NE)
            pe.wait_ge(table_step, 12)

            def step(it, loc):
                t = loc
                if inside(it, TPI, t, NT):
                    e = pe.value_load(te_i[0:1, bass.ds(it * TPI + t, 1)], min_val=0, max_val=NE - 1)
                    pe.wait_ge(xst_ready, it * TPI + t + 1)
                    if inside(it, TPI, t - 2, NT):
                        pe.wait_ge(h_ready, it * TPI + t - 1)
                    for n in range(2):
                        for k in range(KC):
                            ins = pe.matmul(bank(2 * (t % 2) + n), XST[:, t % 2, k * P:(k + 1) * P],
                                            WGU[:, bass.ds(e * (KC * 2 * F) + (2 * k + n) * F, F)],
                                            start=(k == 0), stop=(k == KC - 1))
                    ins.then_inc(gu_done, 1)
                t = loc + 1
                if inside(it, TPI, t, NT):
                    pe.wait_ge(xs_in[t % TPI], it * 16 + 16 * (t // TPI + 1))
                    if inside(it, TPI, t - 1, NT):
                        pe.wait_ge(xst_ready, it * TPI + t)
                    for k in range(KC):
                        ins = pe.transpose(bank(4)[:, k * P:(k + 1) * P], XS[:, t % TPI, k * P:(k + 1) * P], ident[:, :])
                    ins.then_inc(xs_turned, 1)
                t = loc - 1
                if inside(it, TPI, t, NT):
                    pe.wait_ge(h_ready, it * TPI + t + 1)
                    if inside(it, TPI, t - 1, NT):
                        pe.wait_ge(ht_ready, it * TPI + t)
                    for c in range(FC):
                        ins = pe.transpose(bank(5)[:, c * P:(c + 1) * P], HS[:, t % 2, c * P:(c + 1) * P], ident[:, :])
                    ins.then_inc(h_turned, 1)
                t = loc - 2
                if inside(it, TPI, t, NT):
                    e = pe.value_load(te_i[0:1, bass.ds(it * TPI + t, 1)], min_val=0, max_val=NE - 1)
                    pe.wait_ge(ht_ready, it * TPI + t + 1)
                    if inside(it, TPI, t - 1, NT):
                        pe.wait_ge(y_ready, it * TPI + t)
                    for c in range(FC):
                        ins = pe.matmul(bank(6)[:, 0:D], HST[:, t % 2, c * P:(c + 1) * P],
                                        WDN[:, bass.ds(e * (FC * D) + c * D, D)],
                                        start=(c == 0), stop=(c == FC - 1))
                    ins.then_inc(down_done, 1)

            tile_blocks(pe, step)

        waits_met = {nc.vector: sem("dve_waits_met"), nc.gpsimd: sem("pool_waits_met")}

        def pass_waits(eng):
            eng.sem_inc(waits_met[eng], 1)

        block = stack.enter_context(nc.Block())

        def bank(i):
            return PS[:, i, :]

        def weights_of(w):
            return w.rearrange("(c p) d -> p c d", p=P)

        N_SETUP = 5 + 8 + 3

        def attention_blocks(eng, step):
            for it in (-1, 0):
                for loc in range(SPI):
                    step(it, loc)
            with eng.Fori(1, NIT - 1) as it:
                for loc in range(SPI):
                    step(it, loc)
            for it in (NIT - 1, NIT):
                for loc in range(SPI):
                    step(it, loc)

        W_in = [Q[:, :, :, :].rearrange("p u g t -> p (u g t)")[:, i * KC * D:(i + 1) * KC * D]
                .rearrange("p (c d) -> p c d", c=KC) for i in range(4)]
        Wr_in = K[0:NE, 0, 0, 0:D]

        @block.sync
        def _(sp):
            for w, t in zip((Wq, Wk, Wv, Wo), W_in):
                sp.dma_start(t, weights_of(w)).then_inc(setup_in, 16)
            sp.dma_start(Wr_in, router).then_inc(setup_in, 16)
            for v, t in ((bv, bv_all), (bo, bo_all), (tau, tau_all)):
                sp.dma_start(t[:, :], v.partition_broadcast(P)).then_inc(setup_in, 16)
            sp.wait_ge(dve_const, 9)
            for b, t in ((bq, bq_pad), (bk, bk_pad)):
                by_row = b.rearrange("(g j r) -> j r g", g=G, j=G)
                for j in range(G):
                    sp.dma_start(t[PADH * j:PADH * j + E, :], by_row[j], allow_slow_non_contiguous=True).then_inc(setup_in, 16)

            def step(it, loc):
                if loc % 8:
                    return
                ul = loc // 8
                if inside(it, UPI, ul + 2, NU):
                    if inside(it, UPI, ul, NU):
                        sp.wait_ge(ln1_stats, it * UPI * 4 + 4 * (ul + 1))
                    b = it * (UPI * UB) + UB * (ul + 2)
                    dst = X1[:, bass.ds(b * D, UB * D)].rearrange("p (b d) -> p b d", b=UB)
                    sp.dma_start(dst, x_flat[:, bass.ds(b, UB), :]).then_inc(x_in[ul % 2], 16)
                if inside(it, UPI, ul + 2, NU):
                    if inside(it, UPI, ul, NU):
                        sp.wait_ge(pj_filled, it * UPI * FILLS + FILLS * ul + 6)
                    b = it * (UPI * UB) + UB * (ul + 2)
                    sp.dma_start(CTX[:, ul % 2, :, :], c_flat[:, bass.ds(b, UB), :]).then_inc(c_in[ul % 2], 16)
                    sp.dma_start(DEL[:, ul % 2, :], delta_row[:, bass.ds(b * L, UT)]).then_inc(c_in[ul % 2], 16)
                if ul == 0 and inside(it, 1, 0, NE):
                    for n, w in enumerate((w_gate, w_up)):
                        dst = WGU[:, bass.ds(it * (KC * 2 * F), KC * 2 * F)].rearrange("p (k n f) -> p k n f", k=KC, n=2)
                        src = w[bass.ds(it, 1), :, :].rearrange("o (k p) f -> p (o k) f", p=P)
                        sp.dma_start(dst[:, :, n, :], src).then_inc(experts_in, 16)
                    dst = WDN[:, bass.ds(it * (FC * D), FC * D)].rearrange("p (c d) -> p c d", c=FC)
                    src = w_down[bass.ds(it, 1), :, :].rearrange("o (c p) d -> p (o c) d", p=P)
                    sp.dma_start(dst, src).then_inc(experts_in, 16)

            attention_blocks(sp, step)

            sp.wait_ge(pool_const, 17)
            for t in range(NE):
                sp.dma_start(routed[NE * REG + t * P:NE * REG + (t + 1) * P, :], PAD[:, :]).then_inc(dead_in, 16)
            sp.wait_ge(table_step, 1)
            for e in range(NE):
                row = sp.value_load(end_i[0:1, e:e + 1], min_val=e * REG, max_val=e * REG + TOK)
                sp.dma_start(routed[bass.ds(row, P), :], PAD[:, :]).then_inc(pad_in, 16)
            experts_sync(sp)

        @block.gpsimd
        def _(pool):
            def const(ins):
                ins.then_inc(pool_const, 1)

            const(pool.memset(ident[:, :], 0.0))
            const(pool.memset(before[:, :], 1.0))
            const(pool.memset(minus_half[:, :], -0.5))
            const(pool.memset(PAD[:, :], 0.0))
            const(pool.iota(row_i[:, :], [[0, 1]], base=0, channel_multiplier=1))
            const(pool.iota(col_i[:, :], [[1, P]], base=0, channel_multiplier=0))
            const(pool.iota(expert_i[:, :], [[1, NE]], base=0, channel_multiplier=0))
            const(pool.iota(base_i[:, :], [[REG, NE]], base=0, channel_multiplier=0))
            const(pool.iota(out_rows[:, :], [[TOK, 2], [L, NB]], base=0, channel_multiplier=1))
            const(pool.iota(j_i[:, :], [[P, NB]], base=0, channel_multiplier=0))
            const(pool.iota(t_i[:, :], [[1, NT]], base=0, channel_multiplier=0))
            pool.wait_ge(pool_const, 11)
            const(pool.affine_select(out=ident[:, :], in_=ident[:, :], compare_op=ALU.not_equal, fill=1.0,
                                     base=0, pattern=[[-1, P]], channel_multiplier=1))
            const(pool.affine_select(out=before[:, :], in_=before[:, :], compare_op=ALU.is_gt, fill=0.0,
                                     base=0, pattern=[[1, P]], channel_multiplier=-1))
            const(pool.iota(PAD[:, D + 1:D + 2].bitcast(I32), [[0, 1]], base=2 * TOK, channel_multiplier=1))
            const(pool.memset(WqT[:, :, :, :], 0.0))
            const(pool.memset(WkT[:, :, :, :], 0.0))
            const(pool.memset(V[:, :, :, :, :], 0.0))
            pool.wait_ge(pool_const, 17)
            const(pool.memset(V[:, :, :, :, E:E + 1], 1.0))

            def step(it, loc):
                ul, s, j = loc // 8, loc % 8, loc % G
                if s == 3 and inside(it, UPI, ul + 2, NU):
                    pool.wait_ge(ln1_stats, it * UPI * 4 + 4 * (ul + 3))
                    if inside(it, UPI, ul + 1, NU):
                        pool.wait_ge(xn_ready, it * UPI * UB + UB * (ul + 2))
                    pass_waits(pool)
                    pool.tensor_scalar(ln_rstd[:, :], ln_mv[:, :, 1], LN_EPS, None, ALU.add).then_inc(ln1_rstd, 1)
                    pool.wait_ge(ln1_rstd, it * UPI * 2 + 2 * (ul + 2) + 1)
                    pool.tensor_tensor(ln_rstd[:, :], ln_rstd[:, :], minus_half[:, :], ALU.pow).then_inc(ln1_rstd, 1)
                if s == 7 and inside(it, UPI, ul + 2, NU):
                    pool.wait_ge(xn_ready, it * UPI * UB + UB * (ul + 3))
                    if isinstance(it, int) and it * UPI + ul + 2 == 0:
                        pool.wait_ge(setup_in, 16 * N_SETUP)
                    for b in range(UB):
                        xb = X1[:, bass.ds((it * (UPI * UB) + UB * (ul + 2) + b) * D, D)]
                        pool.tensor_tensor(xb, xb, bo_all[:, :], ALU.add).then_inc(x_biased, 1)
                if j == 0:
                    bl = (loc - 8) // G
                    if inside(it, BPI, bl, NB):
                        pool.wait_ge(ln2_step, it * BPI * 3 + 3 * (bl + 1))
                        if inside(it, BPI, bl - 1, NB):
                            pool.wait_ge(xp_ready, it * BPI + bl)
                        pass_waits(pool)
                        pool.tensor_scalar(rstd2[:, :], mv2[:, 1:2], LN_EPS, None, ALU.add).then_inc(ln2_rstd, 1)
                        pool.wait_ge(ln2_rstd, it * BPI * 2 + 2 * bl + 1)
                        pool.tensor_tensor(rstd2[:, :], rstd2[:, :], minus_half[:, 0:1], ALU.pow).then_inc(ln2_rstd, 1)
                if j == 1:
                    bl = (loc - 9) // G
                    if inside(it, BPI, bl, NB):
                        if inside(it, BPI, bl - 4, NB):
                            pool.wait_ge(scattered[bl % 4], it * 32 + 32 * (bl // 4))
                        pool.wait_ge(xp_ready, it * BPI + bl + 1)
                        pass_waits(pool)
                        pool.tensor_copy(XP[:, bl % 4, 1, 0:D], XP[:, bl % 4, 0, 0:D]).then_inc(xp_copied, 1)
                        for k in range(2):
                            pool.tensor_copy(XP[:, bl % 4, k, D + 1:D + 2].bitcast(I32),
                                             out_rows[:, bass.ds(it * BPI + bl + k * NB, 1)]).then_inc(xp_copied, 1)
                if j == 1:
                    bl = (loc - 17) // G
                    if inside(it, BPI, bl, NB):
                        pool.wait_ge(route_step, it * BPI * 17 + 17 * (bl + 1))
                        pool.wait_ge(xp_copied, it * BPI * 3 + 3 * (bl + 1))
                        pass_waits(pool)
                        for k in range(2):
                            pool.indirect_dma_start(
                                routed[:, :], bass.IndirectOffsetOnAxis(ap=slot[k][:, 0:1].bitcast(U32), axis=0),
                                XP[:, bl % 4, k, :], None).then_inc(scattered[bl % 4], 16)

            attention_blocks(pool, step)
            experts_pool(pool)

        @block.vector
        def _(dve):
            dve.memset(bq_pad[:, :], 0.0).then_inc(dve_const, 1)
            dve.memset(bk_pad[:, :], 0.0).then_inc(dve_const, 1)
            dve.memset(ones_b[:, :], 1.0).then_inc(dve_const, 1)
            dve.wait_ge(pool_const, 11)
            dve.tensor_scalar(row_i[:, :], row_i[:, :], 31, None, ALU.bitwise_and).then_inc(dve_const, 1)
            dve.wait_ge(dve_const, 4)
            dve.tensor_copy(row_f[:, :], row_i[:, :]).then_inc(dve_const, 1)
            dve.wait_ge(dve_const, 5)
            dve.tensor_scalar(is_real[:, :], row_f[:, :], float(E), None, ALU.is_lt).then_inc(dve_const, 1)
            dve.tensor_scalar(is_delta[:, :], row_f[:, :], float(E), None, ALU.is_equal).then_inc(dve_const, 1)
            dve.wait_ge(dve_const, 7)
            dve.tensor_copy(bq_pad[:, :], is_delta[:, 0:1].to_broadcast([P, G])).then_inc(dve_const, 1)
            dve.wait_ge(dve_const, 8)
            dve.tensor_scalar(col_i[:, :], col_i[:, :], 31, None, ALU.bitwise_and).then_inc(dve_const, 1)
            dve.wait_ge(dve_const, 9)
            dve.tensor_copy(col_f[:, :], col_i[:, :]).then_inc(dve_const, 1)
            dve.wait_ge(dve_const, 10)
            dve.tensor_scalar(delta_rows[:, :], col_f[:, :], float(E), None, ALU.is_equal).then_inc(dve_const, 1)
            dve.tensor_copy(expert_f[:, :], expert_i[:, :]).then_inc(dve_const, 1)
            dve.tensor_copy(counts[:, :], base_i[:, :]).then_inc(dve_const, 1)
            dve.tensor_copy(start_f[:, :], base_i[0:1, :]).then_inc(dve_const, 1)
            dve.tensor_copy(j_f[:, :], j_i[:, :]).then_inc(dve_const, 1)
            dve.tensor_copy(t_f[:, :], t_i[:, :]).then_inc(dve_const, 1)
            dve.memset(ones8[:, :], 1.0).then_inc(dve_const, 1)
            dve.wait_ge(pool_const, 13)
            dve.tensor_copy(ident_r[:, :], ident[:, :]).then_inc(dve_const, 1)
            dve.tensor_copy(before_b[:, :], before[:, :]).then_inc(dve_const, 1)
            dve.wait_ge(setup_in, 16 * N_SETUP)
            dve.tensor_scalar(q_scale[:, :], tau_all[:, :], is_real[:, 0:1], is_delta[:, 0:1], ALU.mult, ALU.add
                              ).then_inc(dve_const, 1)
            dve.wait_ge(pool_const, 17)
            for n, w in enumerate((WqT, WkT)):
                dve.wait_ge(wt_turned, n + 1)
                for k in range(KC):
                    dve.tensor_copy(w[:, k, :, :].rearrange("p g (j r) -> p (g j) r", r=PADH)[:, :, 0:E],
                                    bank(n)[:, k * D:(k + 1) * D].rearrange("p (h r) -> p h r", r=E)
                                    ).then_inc(wt_ready, 1)
            for n, w in ((2, WvT), (3, WoT)):
                dve.wait_ge(wt_turned, n + 1)
                dve.tensor_copy(w[:, :, :].rearrange("p k d -> p (k d)"), bank(n)).then_inc(wt_ready, 1)
            dve.wait_ge(wt_turned, 5)
            dve.tensor_copy(WrT[:, :, :].rearrange("p k e -> p (k e)"), bank(4)[:, 0:KC * NE]).then_inc(wt_ready, 1)

            def route(k, ins):
                ins.then_inc(route_step, 1)

            def step(it, loc):
                ul, s, j = loc // 8, loc % 8, loc % G
                u = it * UPI
                if inside(it, SPI, loc, NSTEP):
                    dve.wait_ge(s1_done, it * SPI + loc + 1)
                    if inside(it, SPI, loc - 2, NSTEP):
                        dve.wait_ge(s2_done, it * SPI + loc - 1)
                    dve.tensor_reduce(NM[:, loc % 2, :], bank(loc % 2).rearrange("p (g s) -> p g s", g=G),
                                      AX.X, ALU.max, negate=True).then_inc(max_ready, 1)
                if s == 3 and inside(it, UPI, ul + 2, NU):
                    dve.wait_ge(x_in[ul % 2], it * 16 * UPI // 2 + 16 * ((ul + 2) // 2 + 1))
                    if inside(it, UPI, ul + 1, NU):
                        dve.wait_ge(ln1_rstd, it * UPI * 2 + 2 * (ul + 2))
                        dve.wait_ge(xn_ready, it * UPI * UB + UB * (ul + 2))
                    base = it * (UPI * UB * D) + UB * (ul + 2) * D
                    pass_waits(dve)
                    for b in range(UB):
                        dve.bn_stats(ln_stats[:, b, :], X1[:, bass.ds(base + b * D, D)]).then_inc(ln1_stats, 1)
                    dve.wait_ge(ln1_stats, it * UPI * 4 + 4 * (ul + 2) + 2)
                    pass_waits(dve)
                    for b in range(UB):
                        dve.bn_aggr(ln_mv[:, b, :], ln_stats[:, b, :]).then_inc(ln1_stats, 1)
                if s == 6 and inside(it, UPI, ul + 2, NU):
                    dve.wait_ge(ln1_rstd, it * UPI * 2 + 2 * (ul + 3))
                    if inside(it, UPI, ul, NU):
                        dve.wait_ge(pj_filled, it * UPI * FILLS + FILLS * ul + 1)
                    base = it * (UPI * UB * D) + UB * (ul + 2) * D
                    for b in range(UB):
                        dve.tensor_scalar(XN[:, ul % 2, b, :], X1[:, bass.ds(base + b * D, D)], ln_mv[:, b, 0:1],
                                          ln_rstd[:, b:b + 1], ALU.subtract, ALU.mult).then_inc(xn_ready, 1)
                if s in (2, 3) and inside(it, UPI, ul + 1, NU):
                    dve.wait_ge(pj_filled, it * UPI * FILLS + FILLS * (ul + 1) + s + 1)
                    if inside(it, UPI, ul - 1, NU):
                        dve.wait_ge(s2_done, it * SPI + 8 * ul)
                    for h in range(2):
                        g = 2 * (s - 2) + h
                        qs = q_scale[:, bass.ds(it * (UPI * UB) + UB * (ul + 1), UB)]
                        ins = dve.scalar_tensor_tensor(
                            out=Q[:, (ul + 1) % 2, g, :].rearrange("p (b l) -> p b l", b=UB),
                            in0=bank(5)[:, h * UT:(h + 1) * UT].rearrange("p (b l) -> p b l", b=UB),
                            scalar=bq_pad[:, g:g + 1], in1=qs.unsqueeze(2).to_broadcast([P, UB, L]),
                            op0=ALU.add, op1=ALU.mult)
                    ins.then_inc(pj_free, 1)
                if s == 6 and inside(it, UPI, ul + 1, NU):
                    dve.wait_ge(pj_filled, it * UPI * FILLS + FILLS * (ul + 1) + s + 1)
                    if isinstance(it, int) and it * UPI + ul + 1 == 0:
                        dve.wait_ge(pool_const, 18)
                    if inside(it, UPI, ul - 1, NU):
                        dve.wait_ge(av_done, it * SPI + 8 * ul)
                    for b in range(UB):
                        ins = dve.tensor_tensor(
                            V[:, (ul + 1) % 2, b, :, 0:E],
                            bank(5)[:, b * D:(b + 1) * D].rearrange("p (h e) -> p h e", h=H),
                            bv_all[:, :].rearrange("p (h e) -> p h e", h=H), ALU.add)
                    ins.then_inc(pj_free, 1)
                if j == 2:
                    bl = (loc - 6) // G
                    if inside(it, BPI, bl, NB):
                        dve.wait_ge(ott_done, it * BPI + bl + 1)
                        by_head = bank(7).rearrange("p (j g r) -> p j g r", j=G, g=G)
                        if inside(it, BPI, bl - 1, NB):
                            dve.wait_ge(on_step, it * BPI * 2 + 2 * bl)
                        dve.reciprocal(rden[:, :, :], by_head[:, :, :, E]).then_inc(on_step, 1)
                        dve.wait_ge(on_step, it * BPI * 2 + 2 * bl + 1)
                        if inside(it, BPI, bl - 1, NB):
                            dve.wait_ge(ot2_done, it * BPI + bl)
                        dve.tensor_tensor(ON[:, :].rearrange("p (g j r) -> p j g r", g=G, j=G),
                                          by_head[:, :, :, 0:E],
                                          rden[:, :, :].unsqueeze(3).to_broadcast([P, G, G, E]), ALU.mult
                                          ).then_inc(on_step, 1)
                if j == 0:
                    bl = (loc - 8) // G
                    if inside(it, BPI, bl, NB):
                        dve.wait_ge(wo_done, it * BPI + bl + 1)
                        dve.wait_ge(x_biased, it * BPI + bl + 1)
                        xb = X1[:, bass.ds((it * BPI + bl) * D, D)]
                        dve.tensor_tensor(xb, bank(7)[:, 0:D], xb, ALU.add).then_inc(ln2_step, 1)
                        dve.wait_ge(ln2_step, it * BPI * 3 + 3 * bl + 1)
                        pass_waits(dve)
                        dve.bn_stats(st2[:, :], xb).then_inc(ln2_step, 1)
                        dve.wait_ge(ln2_step, it * BPI * 3 + 3 * bl + 2)
                        if inside(it, BPI, bl - 1, NB):
                            dve.wait_ge(ln2_rstd, it * BPI * 2 + 2 * bl)
                            dve.wait_ge(xp_ready, it * BPI + bl)
                        pass_waits(dve)
                        dve.bn_aggr(mv2[:, :], st2[:, :]).then_inc(ln2_step, 1)
                if j == 1:
                    bl = (loc - 9) // G
                    if inside(it, BPI, bl, NB):
                        dve.wait_ge(ln2_rstd, it * BPI * 2 + 2 * (bl + 1))
                        if inside(it, BPI, bl - 4, NB):
                            dve.wait_ge(scattered[bl % 4], it * 32 + 32 * (bl // 4))
                        dve.tensor_scalar(XP[:, bl % 4, 0, 0:D], X1[:, bass.ds((it * BPI + bl) * D, D)], mv2[:, 0:1],
                                          rstd2[:, 0:1], ALU.subtract, ALU.mult).then_inc(xp_ready, 1)
                if j == 1:
                    bl = (loc - 13) // G
                    if inside(it, BPI, bl, NB):
                        r0 = it * BPI * 17 + 17 * bl
                        if inside(it, BPI, bl - 1, NB):
                            dve.wait_ge(route_step, r0)
                        dve.wait_ge(logits_done, it * BPI + bl + 1)
                        route(1, dve.tensor_copy(lg[:, :], bank(7)[:, 0:NE]))
                        dve.wait_ge(route_step, r0 + 1)
                        pass_waits(dve)
                        route(2, dve.max(mx[:, :], lg[:, :]))
                        dve.wait_ge(route_step, r0 + 2)
                        pass_waits(dve)
                        route(3, dve.max_index(mi[:, :], mx[:, :], lg[:, :]))
                        dve.wait_ge(route_step, r0 + 3)
                        route(4, dve.tensor_copy(mif[:, :], mi[:, 0:2]))
                        dve.wait_ge(route_step, r0 + 4)
                        for k in range(2):
                            route(5 + k, dve.tensor_scalar(M[:, k, :], expert_f[:, :], mif[:, k:k + 1], None, ALU.is_equal))
                        dve.wait_ge(route_step, r0 + 6)
                        route(7, dve.tensor_tensor(Mb[:, :], M[:, 0, :], M[:, 1, :], ALU.add))
                if j == 2:
                    bl = (loc - 14) // G
                    if inside(it, BPI, bl, NB):
                        r0 = it * BPI * 17 + 17 * bl
                        dve.wait_ge(gate_exp, it * BPI + bl + 1)
                        route(8, dve.tensor_scalar(gp[:, :], ge[:, :], 1.0, None, ALU.add))
                        dve.wait_ge(route_step, r0 + 8)
                        route(9, dve.reciprocal(gs[:, :], gp[:, :]))
                        dve.wait_ge(route_step, r0 + 9)
                        route(10, dve.scalar_tensor_tensor(out=gsum[:, :], in0=gs[:, 0:1], scalar=1e-10,
                                                           in1=gs[:, 1:2], op0=ALU.add, op1=ALU.add))
                        dve.wait_ge(route_step, r0 + 10)
                        route(11, dve.reciprocal(grec[:, :], gsum[:, :]))
                        dve.wait_ge(route_step, r0 + 11)
                        route(12, dve.tensor_scalar(XP[:, bl % 4, :, D], gs[:, :], grec[:, 0:1], None, ALU.mult))
                if j == 0:
                    bl = (loc - 16) // G
                    if inside(it, BPI, bl, NB):
                        r0 = it * BPI * 17 + 17 * bl
                        dve.wait_ge(rank_done, it * BPI + bl + 1)
                        dve.wait_ge(route_step, r0 + 12)
                        route(13, dve.tensor_tensor(rank[:, :], bank(6)[:, 0:NE], counts[:, :], ALU.add))
                        dve.wait_ge(route_step, r0 + 13)
                        route(14, dve.tensor_tensor(counts[:, :], bank(6)[:, NE:2 * NE], counts[:, :], ALU.add))
                        route(15, dve.tensor_tensor(rsel[:, :, :], M[:, :, :],
                                                    rank[:, :].unsqueeze(1).to_broadcast([P, 2, NE]), ALU.mult))
                        dve.wait_ge(route_step, r0 + 15)
                        route(16, dve.tensor_reduce(slot_f[:, :], rsel[:, :, :], AX.X, ALU.add))
                        dve.wait_ge(route_step, r0 + 16)
                        if inside(it, BPI, bl - 1, NB):
                            dve.wait_ge(scattered[(bl - 1) % 4], it * 32 + 32 * ((bl - 1) // 4 + 1))
                        dve.tensor_copy(slot[0][:, :], slot_f[:, 0:1])
                        route(17, dve.tensor_copy(slot[1][:, :], slot_f[:, 1:2]))

            attention_blocks(dve, step)

            dve.wait_ge(route_step, 17 * NB)
            dve.tensor_copy(end_i[:, :], counts[0:1, :]).then_inc(table_step, 1)
            dve.tensor_tensor(cnt[:, :], counts[0:1, :], start_f[:, :], ALU.subtract).then_inc(table_step, 1)
            dve.wait_ge(table_step, 2)
            dve.tensor_tensor(over, cnt[:, :].unsqueeze(2).to_broadcast([1, NE, NB]),
                              j_f[:, :].unsqueeze(1).to_broadcast([1, NE, NB]), ALU.is_gt).then_inc(table_step, 1)
            dve.wait_ge(table_step, 3)
            dve.tensor_reduce(ntile[:, :], over, AX.X, ALU.add).then_inc(table_step, 1)
            dve.wait_ge(table_step, 4)
            dve.tensor_tensor_scan(upto[:, :], ones8[:, :], ntile[:, :], 0.0, ALU.mult, ALU.add).then_inc(table_step, 1)
            dve.tensor_scalar(jump[:, :], ntile[:, :], -float(P), float(REG), ALU.mult, ALU.add).then_inc(table_step, 1)
            dve.wait_ge(table_step, 6)
            dve.tensor_tensor(past, t_f[:, :].unsqueeze(2).to_broadcast([1, NT, NE]),
                              upto[:, :].unsqueeze(1).to_broadcast([1, NT, NE]), ALU.is_ge).then_inc(table_step, 1)
            dve.wait_ge(table_step, 7)
            dve.tensor_tensor(pastj, past, jump[:, :].unsqueeze(1).to_broadcast([1, NT, NE]),
                              ALU.mult).then_inc(table_step, 1)
            dve.tensor_reduce(te_f[:, :], past, AX.X, ALU.add).then_inc(table_step, 1)
            dve.wait_ge(table_step, 9)
            dve.tensor_reduce(tr_f[:, :], pastj, AX.X, ALU.add).then_inc(table_step, 1)
            dve.tensor_scalar(te_i[:, :], te_f[:, :], float(NE - 1), None, ALU.min).then_inc(table_step, 1)
            dve.wait_ge(table_step, 11)
            dve.scalar_tensor_tensor(out=tr_i[:, :], in0=t_f[:, :], scalar=float(P), in1=tr_f[:, :],
                                     op0=ALU.mult, op1=ALU.add).then_inc(table_step, 1)
            experts_vector(dve)

        @block.scalar
        def _(act):
            def step(it, loc):
                ul, s, j = loc // 8, loc % 8, loc % G
                if inside(it, SPI, loc - 1, NSTEP):
                    act.wait_ge(s2_done, it * SPI + loc)
                    if inside(it, SPI, loc - 3, NSTEP):
                        act.wait_ge(av_done, it * SPI + loc - 2)
                    k = (loc - 1) % 2
                    act.activation(AT[:, k, :], bank(2 + k), ACT.Exp, scale=SCALE).then_inc(probs_ready, 1)
                if s in (0, 1) and inside(it, UPI, ul + 1, NU):
                    act.wait_ge(pj_filled, it * UPI * FILLS + FILLS * (ul + 1) + s + 1)
                    dst = (XNT, CT)[s]
                    act.activation(dst[:, :, :].rearrange("p k t -> p (k t)"), bank(5), ACT.Copy).then_inc(pj_free, 1)
                if s in (4, 5) and inside(it, UPI, ul + 1, NU):
                    if isinstance(it, int) and it * UPI + ul + 1 == 0:
                        act.wait_ge(setup_in, 16 * N_SETUP)
                    act.wait_ge(pj_filled, it * UPI * FILLS + FILLS * (ul + 1) + s + 1)
                    if inside(it, UPI, ul - 1, NU):
                        act.wait_ge(s2_done, it * SPI + 8 * ul)
                    for h in range(2):
                        g = 2 * (s - 4) + h
                        ins = act.activation(K[:, (ul + 1) % 2, g, :], bank(5)[:, h * UT:(h + 1) * UT], ACT.Identity,
                                             bias=bk_pad[:, g:g + 1])
                    ins.then_inc(pj_free, 1)
                if j == 1:
                    bl = (loc - 5) // G
                    if inside(it, BPI, bl, NB):
                        act.wait_ge(av_done, it * SPI + G * (bl + 1))
                        if inside(it, BPI, bl - 1, NB):
                            act.wait_ge(ott_done, it * BPI + bl)
                        act.activation(OT[:, :], bank(4), ACT.Copy).then_inc(ot_ready, 1)
                if j == 3:
                    bl = (loc - 7) // G
                    if inside(it, BPI, bl, NB):
                        act.wait_ge(ot2_done, it * BPI + bl + 1)
                        if inside(it, BPI, bl - 1, NB):
                            act.wait_ge(wo_done, it * BPI + bl)
                        act.activation(ONT[:, :, :].rearrange("p k l -> p (k l)"), bank(7)[:, 0:KC * P], ACT.Copy
                                       ).then_inc(ont_ready, 1)
                if j == 2:
                    bl = (loc - 10) // G
                    if inside(it, BPI, bl, NB):
                        act.wait_ge(x2t_turned, it * BPI + bl + 1)
                        if inside(it, BPI, bl - 1, NB):
                            act.wait_ge(logits_done, it * BPI + bl)
                        act.activation(X2T[:, :, :].rearrange("p k l -> p (k l)"), bank(6)[:, 0:KC * P], ACT.Copy
                                       ).then_inc(x2t_ready, 1)
                if j == 2:
                    bl = (loc - 14) // G
                    if inside(it, BPI, bl, NB):
                        act.wait_ge(route_step, it * BPI * 17 + 17 * bl + 2)
                        act.activation(ge[:, :], mx[:, 0:2], ACT.Exp, scale=-1.0).then_inc(gate_exp, 1)

            attention_blocks(act, step)
            experts_scalar(act)

        @block.tensor
        def _(pe):
            pe.wait_ge(setup_in, 16 * N_SETUP)
            pe.wait_ge(pool_const, 13)
            for n in range(4):
                for k in range(KC):
                    for c in range(KC):
                        ins = pe.transpose(bank(n)[:, k * D + c * P:k * D + (c + 1) * P],
                                           W_in[n][:, c, k * P:(k + 1) * P], ident[:, :])
                ins.then_inc(wt_turned, 1)
            for k in range(KC):
                ins = pe.transpose(bank(4)[:, k * NE:(k + 1) * NE], Wr_in[:, k * P:(k + 1) * P], ident[0:NE, 0:NE])
            ins.then_inc(wt_turned, 1)
            pe.wait_ge(wt_ready, 7)
            pe.wait_ge(dve_const, 20)

            def step(it, loc):
                ul, s, j = loc // 8, loc % 8, loc % G
                if inside(it, SPI, loc, NSTEP):
                    if s == 0:
                        pe.wait_ge(pj_free, it * UPI * FILLS + FILLS * ul + 6)
                    if inside(it, SPI, loc - 2, NSTEP):
                        pe.wait_ge(max_ready, it * SPI + loc - 1)
                    b = (s // G) * L
                    rows = slice(PADH * j, PADH * (j + 1))
                    for g in range(G):
                        ins = pe.matmul(bank(loc % 2)[:, g * P:(g + 1) * P], Q[rows, ul % 2, g, b:b + L],
                                        K[rows, ul % 2, g, b:b + L], start=True, stop=True)
                    ins.then_inc(s1_done, 1)
                if inside(it, SPI, loc - 2, NSTEP):
                    k = loc - 2
                    kj, ku, kb = k % G, (k // 8) % 2, (k % 8) // G
                    pe.wait_ge(probs_ready, it * SPI + k + 1)
                    if k % 8 == 0:
                        pe.wait_ge(pj_free, it * UPI * FILLS + FILLS * (k // 8 + 1))
                    if kj == 0 and inside(it, BPI, k // G - 1, NB):
                        pe.wait_ge(ot_ready, it * BPI + k // G)
                    for g in range(G):
                        ins = pe.matmul(PS[PADH * g:PADH * (g + 1), 4, kj * P:(kj + 1) * P],
                                        V[:, ku, kb, G * g + kj, :], AT[:, k % 2, g * P:(g + 1) * P],
                                        start=True, stop=True)
                    ins.then_inc(av_done, 1)
                if inside(it, SPI, loc - 1, NSTEP):
                    k = loc - 1
                    kj, ku, kb = k % G, (k // 8) % 2, ((k % 8) // G) * L
                    pe.wait_ge(max_ready, it * SPI + k + 1)
                    if inside(it, SPI, k - 2, NSTEP):
                        pe.wait_ge(probs_ready, it * SPI + k - 1)
                    rows = slice(PADH * kj, PADH * (kj + 1))
                    for g in range(G):
                        dst = bank(2 + k % 2)[:, g * P:(g + 1) * P]
                        pe.matmul(dst, K[rows, ku, g, kb:kb + L], Q[rows, ku, g, kb:kb + L], start=True, stop=False)
                        ins = pe.matmul(dst, NM[:, k % 2, g:g + 1].to_broadcast([P, P]), ident_r[:, :],
                                        start=False, stop=True)
                    ins.then_inc(s2_done, 1)
                if s < FILLS and inside(it, UPI, ul + 1, NU):
                    f = it * UPI * FILLS + FILLS * (ul + 1) + s
                    if not (isinstance(it, int) and it * UPI + ul + 1 == 0 and s == 0):
                        pe.wait_ge(pj_free, f)
                    ub = (ul + 1) % 2
                    if s == 0:
                        pe.wait_ge(xn_ready, it * UPI * UB + UB * (ul + 2))
                    if s == 1:
                        pe.wait_ge(c_in[ub], it * 32 + 32 * ((ul + 1) // 2 + 1))
                    if s in (0, 1):
                        src = (XN, CTX)[s]
                        for k in range(KC):
                            for b in range(UB):
                                ins = pe.transpose(bank(5)[:, k * UT + b * L:k * UT + (b + 1) * L],
                                                   src[:, ub, b, k * P:(k + 1) * P], ident[:, :])
                    elif s < 6:
                        is_k = s >= 4
                        w, src = ((WqT, XNT), (WkT, CT))[is_k]
                        for h in range(2):
                            g = 2 * (s % 2) + h
                            dst = bank(5)[:, h * UT:(h + 1) * UT]
                            for k in range(KC):
                                ins = pe.matmul(dst, w[:, k, g, :], src[:, k, :], start=(k == 0),
                                                stop=(k == KC - 1 and not is_k))
                            if is_k:
                                ins = pe.matmul(dst, delta_rows[:, :], DEL[:, ub, :], start=False, stop=True)
                    else:
                        for b in range(UB):
                            for k in range(KC):
                                ins = pe.matmul(bank(5)[:, b * D:(b + 1) * D], CT[:, k, b * L:(b + 1) * L],
                                                WvT[:, k, :], start=(k == 0), stop=(k == KC - 1))
                    ins.then_inc(pj_filled, 1)
                if j == 2:
                    bl = (loc - 6) // G
                    if inside(it, BPI, bl, NB):
                        pe.wait_ge(ot_ready, it * BPI + bl + 1)
                        if inside(it, BPI, bl - 1, NB):
                            pe.wait_ge(ln2_step, it * BPI * 3 + 3 * (bl - 1) + 1)
                        if inside(it, BPI, bl - 2, NB):
                            pe.wait_ge(route_step, it * BPI * 17 + 17 * (bl - 2) + 1)
                        for q in range(G):
                            ins = pe.transpose(bank(7)[:, q * P:(q + 1) * P], OT[:, q * P:(q + 1) * P], ident[:, :])
                        ins.then_inc(ott_done, 1)
                if j == 3:
                    bl = (loc - 7) // G
                    if inside(it, BPI, bl, NB):
                        pe.wait_ge(on_step, it * BPI * 2 + 2 * (bl + 1))
                        for k in range(KC):
                            ins = pe.transpose(bank(7)[:, k * P:(k + 1) * P], ON[:, k * P:(k + 1) * P], ident[:, :])
                        ins.then_inc(ot2_done, 1)
                if j == 0:
                    bl = (loc - 8) // G
                    if inside(it, BPI, bl, NB):
                        pe.wait_ge(ont_ready, it * BPI + bl + 1)
                        for k in range(KC):
                            ins = pe.matmul(bank(7)[:, 0:D], ONT[:, k, :], WoT[:, k, :], start=(k == 0),
                                            stop=(k == KC - 1))
                        ins.then_inc(wo_done, 1)
                if j == 1:
                    bl = (loc - 13) // G
                    if inside(it, BPI, bl, NB):
                        pe.wait_ge(x2t_ready, it * BPI + bl + 1)
                        if inside(it, BPI, bl + 1, NB):
                            pe.wait_ge(ln2_step, it * BPI * 3 + 3 * (bl + 1) + 1)
                        for k in range(KC):
                            ins = pe.matmul(bank(7)[:, 0:NE], X2T[:, k, :], WrT[:, k, :], start=(k == 0),
                                            stop=(k == KC - 1))
                        ins.then_inc(logits_done, 1)
                if j == 2:
                    bl = (loc - 10) // G
                    if inside(it, BPI, bl, NB):
                        pe.wait_ge(xp_ready, it * BPI + bl + 1)
                        if inside(it, BPI, bl - 2, NB):
                            pe.wait_ge(route_step, it * BPI * 17 + 17 * (bl - 2) + 14)
                        for k in range(KC):
                            ins = pe.transpose(bank(6)[:, k * P:(k + 1) * P], XP[:, bl % 4, 0, k * P:(k + 1) * P],
                                               ident[:, :])
                        ins.then_inc(x2t_turned, 1)
                if j == 0:
                    bl = (loc - 16) // G
                    if inside(it, BPI, bl, NB):
                        pe.wait_ge(route_step, it * BPI * 17 + 17 * bl + 7)
                        if inside(it, BPI, bl + 1, NB):
                            pe.wait_ge(x2t_ready, it * BPI + bl + 2)
                        pe.matmul(bank(6)[:, 0:NE], before_b[:, :], Mb[:, :], start=True, stop=True)
                        pe.matmul(bank(6)[:, NE:2 * NE], ones_b[:, :], Mb[:, :], start=True, stop=True
                                  ).then_inc(rank_done, 1)

            attention_blocks(pe, step)
            experts_tensor(pe)


_INS = ['x', 'ctx_1024', 'condB_tau', 'fside_BxS2_0', 'L0_xcond_Wq', 'L0_xcond_bq', 'L0_xcond_Wk', 'L0_xcond_bk',
        'L0_xcond_Wv', 'L0_xcond_bv', 'L0_xcond_Wo', 'L0_xcond_bo', 'L0_ffn_router_w', 'L0_ffn_w_gate',
        'L0_ffn_w_up', 'L0_ffn_w_down']
_OUTS = [((NB, L, D), 'float32')]


def kernel(**inputs):
    import numpy as _np
    import concourse.bacc as _bacc
    from concourse import mybir as _mybir
    from concourse.bass_utils import run_bass_kernel_spmd as _run

    nc = _bacc.Bacc("TRN2", target_bir_lowering=False, num_devices=1)
    arrays, args = {}, []
    for name in _INS:
        a = _np.ascontiguousarray(inputs[name])
        arrays[f"in_{name}_dram"] = a
        args.append(nc.dram_tensor(f"in_{name}_dram", a.shape, _mybir.dt.from_np(a.dtype), kind="ExternalInput").ap())
    for i, (shape, dtype) in enumerate(_OUTS):
        dt = _mybir.dt.from_np(_np.dtype(dtype))
        args.append(nc.dram_tensor(f"out_{i}_dram", shape, dt, kind="ExternalOutput").ap())
    build(nc, *args)
    r = _run(nc, [arrays], core_ids=[0])
    got = tuple(r.results[0][f"out_{i}_dram"] for i in range(len(_OUTS)))
    return got[0]
```

```python
from contextlib import ExitStack

import concourse.bass as bass
from concourse import mybir

F32 = mybir.dt.float32
F32R = mybir.dt.float32r
BF16 = mybir.dt.bfloat16
I32 = mybir.dt.int32
U32 = mybir.dt.uint32
ALU = mybir.AluOpType
ACT = mybir.ActivationFunctionType
AX = mybir.AxisListType

P = 128
NB, L, D = 32, 128, 256
H, E = 16, 16
KC = D // P
G = 4
PADH = 32
NE, F = 8, 512
FC = F // P
TOK = NB * L
UB = 2
UT = UB * L
NU = NB // UB
NSTEP = NB * G
SPI = 16
BPI, UPI = SPI // G, SPI // G // UB
NIT = NSTEP // SPI
FILLS = 7
REG = TOK + P
NT = 2 * TOK // P + NE
ROWS = NE * REG + NE * P
PW = D + 2
SCALE = 0.25
TPI = 8
GUW, DNW = KC * 2 * F, FC * D
EW = GUW + DNW
SLOTS = 3
CHW = EW // 6
LN_EPS = 1e-5


SPLIT = ((0, 0), (0, 1), (1, 0))
TABLE = 25


def expert_at(place):
    return (place + NE - 1) % NE


def inside(it, per, c, total):
    return not isinstance(it, int) or 0 <= per * it + c < total


def build(nc, x, ctx_in, tau, delta, Wq, bq, Wk, bk, Wv, bv, Wo, bo, router, w_gate, w_up, w_down, out):
    routed = nc.dram_tensor("routed_rows", (ROWS, PW), F32, kind="Internal").ap()
    expert_out = nc.dram_tensor("expert_rows", (2 * TOK, D), F32, kind="Internal").ap()
    split_w = nc.dram_tensor("split_weights", (NE * P, 2 * EW), F32, kind="Internal").ap()
    x_flat = x.rearrange("b l d -> l b d")
    c_flat = ctx_in.rearrange("b l d -> l b d")
    out_flat = out.rearrange("b l d -> l b d")
    delta_row = delta.rearrange("(o b) s -> o (b s)", o=1)

    with ExitStack() as stack:
        def sb(name, shape, dt=F32):
            return stack.enter_context(nc.sbuf_tensor(name, shape, dt))

        def sem(name):
            return stack.enter_context(nc.semaphore(name))

        X1 = sb("X1", [P, NB * D])
        W = sb("W", [P, SLOTS * 2 * EW], F32R)
        w_raw = sb("w_raw", [P, EW])
        ident = sb("ident", [P, P])
        WrT = sb("WrT", [P, KC, NE])
        ones_r = sb("ones_r", [P, P], F32R)
        before_b = sb("before_b", [P, P], BF16)
        ones_b = sb("ones_b", [P, P], BF16)
        bq_pad = sb("bq_pad", [P, G])
        bk_pad = sb("bk_pad", [P, G])
        bv_all = sb("bv_all", [P, D])
        bo_all = sb("bo_all", [P, D])
        tau_all = sb("tau_all", [P, NB])
        q_scale = sb("q_scale", [P, NB])
        row_i = sb("row_i", [P, 1], I32)
        row_f = sb("row_f", [P, 1])
        is_real = sb("is_real", [P, 1])
        is_delta = sb("is_delta", [P, 1])
        col_i = sb("col_i", [1, P], I32)
        col_f = sb("col_f", [1, P])
        delta_rows = sb("delta_rows", [1, P], F32R)
        delta_high = sb("delta_high", [P, NB], F32R)
        delta_low = sb("delta_low", [P, NB])
        minus_half = sb("minus_half", [P, UB])
        expert_i = sb("expert_i", [P, NE], I32)
        expert_f = sb("expert_f", [P, NE])
        base_i = sb("base_i", [P, NE], I32)
        counts = sb("counts", [P, NE])
        out_rows = sb("out_rows", [P, 2 * NB], I32)
        PAD = sb("PAD", [P, PW])
        CTX = sb("CTX", [P, 2, UB, D])
        DEL = sb("DEL", [1, 2, UT])
        ln_stats = sb("ln_stats", [P, UB, 6])
        ln_mv = sb("ln_mv", [P, UB, 2])
        ln_rstd = sb("ln_rstd", [P, UB])
        XN = sb("XN", [P, 2, UB, D])
        Q = sb("Q", [P, 2, G, UT])
        K = sb("K", [P, 2, G, UT])
        QKW = 2 * G * UT
        QR, KR = (W[:, 2 * EW + i * QKW:2 * EW + (i + 1) * QKW].rearrange("p (u g t) -> p u g t", u=2, g=G)
                  for i in range(2))
        at = 2 * EW + 2 * QKW
        XNT, CT = ([W[:, at + (2 * i + n) * KC * UT:at + (2 * i + n + 1) * KC * UT]
                    .rearrange("p (k t) -> p k t", k=KC) for n in range(2)] for i in range(2))
        at += 4 * KC * UT
        WqT, WkT = ([W[:, at + (2 * i + n) * KC * G * P:at + (2 * i + n + 1) * KC * G * P]
                     .rearrange("p (k g r) -> p k g r", k=KC, g=G) for n in range(2)] for i in range(2))
        at += 4 * KC * G * P
        WvT, WoT = ([W[:, at + (2 * i + n) * KC * D:at + (2 * i + n + 1) * KC * D]
                     .rearrange("p (k d) -> p k d", k=KC) for n in range(2)] for i in range(2))
        W_whole = [Q[:, i, :, :].rearrange("p g t -> p (g t)") for i in range(2)]
        DR = sb("DR", [1, UT], F32R)
        V = sb("V", [P, 2, UB, H, PADH])
        NM = sb("NM", [P, 2, G])
        NMD = sb("NMD", [P, 2, G, P], F32R)
        AT = sb("AT", [P, 2, G * P])
        before = AT[:, 0, 0:P]
        OT = sb("OT", [P, G * P])
        rden = sb("rden", [P, G, G])
        ON = sb("ON", [P, D])
        ONT = [sb(f"ONT_{n}", [P, KC, P], F32R) for n in ("high", "low")]
        st2 = sb("st2", [P, 6])
        mv2 = sb("mv2", [P, 2])
        rstd2 = sb("rstd2", [P, 1])
        XP = sb("XP", [P, 4, 2, PW])
        X2T = sb("X2T", [P, KC, P])
        lg = sb("lg", [P, NE])
        mx = sb("mx", [P, 8])
        mi = sb("mi", [P, 8], U32)
        mif = sb("mif", [P, 2])
        M = sb("M", [P, 2, NE])
        Mb = sb("Mb", [P, NE], BF16)
        ge = sb("ge", [P, 2])
        gp = sb("gp", [P, 2])
        gs = sb("gs", [P, 2])
        gsum = sb("gsum", [P, 1])
        grec = sb("grec", [P, 1])
        rank = sb("rank", [P, NE])
        rsel = sb("rsel", [P, 2, NE])
        slot_f = sb("slot_f", [P, 2])
        slot = sb("slot", [P, 4, 2], I32)
        j_i = sb("j_i", [1, NB], I32)
        j_f = sb("j_f", [1, NB])
        t_i = sb("t_i", [1, NT], I32)
        t_f = sb("t_f", [1, NT])
        start_i = sb("start_i", [1, NE], I32)
        start_f = sb("start_f", [1, NE])
        cnt = sb("cnt", [1, NE])
        ntile = sb("ntile", [1, NE])
        ones8 = sb("ones8", [1, NE])
        placed = sb("placed", [1, NE])
        upto = sb("upto", [1, NE])
        jump = sb("jump", [1, NE])
        te_f = sb("te_f", [1, NT])
        tr_f = sb("tr_f", [1, NT])
        tw_f = sb("tw_f", [1, NT])
        place = sb("place", [1, NT])
        turn1 = sb("turn1", [1, NT])
        turn2 = sb("turn2", [1, NT])
        end_i = sb("end_i", [1, NE], I32)
        te_i = sb("te_i", [1, NT], I32)
        tw_i = sb("tw_i", [1, NT], I32)
        upto_i = sb("upto_i", [1, NE], I32)
        tr_i = sb("tr_i", [1, NT], I32)

        PS = stack.enter_context(nc.psum_tensor("PS", [P, 8, 512], F32))

        setup_in = sem("setup_in")
        pool_const = sem("pool_const")
        dve_const = sem("dve_const")
        wt_turned = sem("wt_turned")
        wt_spread = sem("wt_spread")
        wt_rounded = sem("wt_rounded")
        wt_ready = sem("wt_ready")
        tokens_high = sem("tokens_high")
        ont_high = sem("ont_high")
        x_in = [sem(f"x_in{i}") for i in range(2)]
        c_in = [sem(f"c_in{i}") for i in range(2)]
        raw_in = sem("raw_in")
        high_ready = sem("high_ready")
        low_ready = sem("low_ready")
        split_out = sem("split_out")
        weights_in = sem("weights_in")
        ln1_stats = sem("ln1_stats")
        ln1_rstd = sem("ln1_rstd")
        xn_ready = sem("xn_ready")
        x_biased = sem("x_biased")
        pj_filled = sem("pj_filled")
        pj_free = sem("pj_free")
        q_rounded = sem("q_rounded")
        k_rounded = sem("k_rounded")
        max_found = sem("max_found")
        max_used = sem("max_used")
        delta_rounded = sem("delta_rounded")
        s1_done = sem("s1_done")
        max_ready = sem("max_ready")
        s2_done = sem("s2_done")
        probs_ready = sem("probs_ready")
        av_done = sem("av_done")
        ot_ready = sem("ot_ready")
        ott_done = sem("ott_done")
        on_step = sem("on_step")
        ot2_done = sem("ot2_done")
        ont_ready = sem("ont_ready")
        wo_done = sem("wo_done")
        ln2_step = sem("ln2_step")
        ln2_rstd = sem("ln2_rstd")
        xp_ready = sem("xp_ready")
        xp_copied = sem("xp_copied")
        x2t_turned = sem("x2t_turned")
        x2t_ready = sem("x2t_ready")
        logits_done = sem("logits_done")
        gate_exp = sem("gate_exp")
        rank_done = sem("rank_done")
        route_step = sem("route_step")
        scattered = [sem(f"scattered{i}") for i in range(4)]
        dead_in = sem("dead_in")
        rows_placed = sem("rows_placed")
        table_step = sem("table_step")
        pad_in = sem("pad_in")


        flat_v = V[:, :, :, :, :].rearrange("p u b h r -> p (u b h r)")
        past = flat_v[0:1, 0:NT * NE].rearrange("p (t e) -> p t e", e=NE)
        pastj = flat_v[0:1, NT * NE:2 * NT * NE].rearrange("p (t e) -> p t e", e=NE)
        over = flat_v[0:1, 2 * NT * NE:2 * NT * NE + NE * NB].rearrange("p (e j) -> p e j", e=NE)
        XS = XP[:, :, :, :].rearrange("p i k w -> p (i k) w")
        XST = [sb(f"XST_{n}", [P, 2, D], F32R) for n in ("high", "low")]
        HS = w_raw[:, 0:2 * F].rearrange("p (i w) -> p i w", i=2)
        SG = w_raw[:, 2 * F:4 * F].rearrange("p (i w) -> p i w", i=2)
        HST = [NMD[:, :, :, :].rearrange("p i g l -> p i (g l)"),
               sb("HST_low", [P, 2, F], F32R)]
        YS = flat_v.rearrange("p (i w) -> p i w", i=TPI)
        META = sb("META", [P, TPI, 2])
        xs_in = [sem(f"xs_in{i}") for i in range(TPI)]
        xs_turned = sem("xs_turned")
        xst_high = sem("xst_high")
        xst_ready = sem("xst_ready")
        meta_ready = sem("meta_ready")
        gu_done = sem("gu_done")
        silu_ready = sem("silu_ready")
        h_ready = sem("h_ready")
        h_turned = sem("h_turned")
        ht_high = sem("ht_high")
        ht_ready = sem("ht_ready")
        down_done = sem("down_done")
        y_ready = sem("y_ready")
        y_out = [sem(f"y_out{i}") for i in range(TPI)]
        parts_in = [sem(f"parts_in{i}") for i in range(8)]
        sum_step = sem("sum_step")
        stored = sem("stored")

        def tile_blocks(eng, step):
            for it in (-1, 0, 1):
                for loc in range(TPI):
                    step(it, loc)
            with eng.Fori(2, NT // TPI - 1) as it:
                for loc in range(TPI):
                    step(it, loc)
            for it in (NT // TPI - 1, NT // TPI):
                for loc in range(TPI):
                    step(it, loc)

        BQ = 4

        def part(q, k):
            return W[:, (k * NB + BQ * q) * D:(k * NB + BQ * (q + 1)) * D].bitcast(F32)

        def pad_regions(eng, experts):
            eng.wait_ge(table_step, 1)
            for e in experts:
                row = eng.value_load(end_i[0:1, e:e + 1], min_val=e * REG, max_val=e * REG + TOK)
                eng.dma_start(routed[bass.ds(row, P), :], PAD[:, :]).then_inc(pad_in, 16)

        def experts_sync(sp):
            for i in range(4):
                sp.wait_ge(scattered[i], 32 * NB // 4)
            sp.wait_ge(dead_in, 16 * NE)
            sp.wait_ge(pad_in, 16 * NE)
            sp.wait_ge(table_step, TABLE)
            sp.wait_ge(low_ready, 6 * NE)
            sp.wait_ge(split_out, 32 * (NE - 1))
            sp.sem_inc(rows_placed, 1)
            sp.sem_inc(weights_in, 32)
            sp.wait_ge(xs_in[3], 16)
            for p in range(1, NE):
                if p >= SLOTS:
                    done = sp.value_load(upto_i[0:1, p - SLOTS:p - SLOTS + 1], min_val=1, max_val=NT + 1)
                    sp.wait_ge(down_done, done)
                e = expert_at(p)
                w0 = (p % SLOTS) * 2 * EW
                for h in range(2):
                    c0, c1 = h * EW, (h + 1) * EW
                    sp.dma_start(W[:, w0 + c0:w0 + c1].bitcast(F32), split_w[e * P:(e + 1) * P, c0:c1]).then_inc(weights_in, 16)
                sp.wait_ge(weights_in, 32 * (p + 1))
            sp.wait_ge(down_done, NT + 1)
            for i in range(TPI):
                sp.wait_ge(y_out[i], 16 * NT // TPI)
            for q in range(NB // BQ):
                for k in range(2):
                    rows = expert_out[k * TOK + q * BQ * L:k * TOK + (q + 1) * BQ * L, :]
                    sp.dma_start(part(q, k).rearrange("p (b d) -> p b d", b=BQ),
                                 rows.rearrange("(b l) d -> l b d", b=BQ)).then_inc(parts_in[q], 16)
            for q in range(NB // BQ):
                sp.wait_ge(sum_step, 2 * (q + 1))
                sp.dma_start(out_flat[:, q * BQ:(q + 1) * BQ, :],
                             X1[:, q * BQ * D:(q + 1) * BQ * D].rearrange("p (b d) -> p b d", b=BQ)
                             ).then_inc(stored, 16)
            sp.wait_ge(stored, 16 * NB // BQ)

        def experts_pool(pool):
            def step(it, loc):
                t = loc + 1
                if inside(it, TPI, t, NT):
                    pool.wait_ge(xs_in[t % TPI], it * 16 + 16 * (t // TPI + 1))
                    if inside(it, TPI, t - TPI, NT):
                        pool.wait_ge(y_out[t % TPI], it * 16 + 16 * (t // TPI))
                    pass_waits(pool)
                    pool.tensor_copy(META[:, t % TPI, :].bitcast(I32), XS[:, t % TPI, D:PW].bitcast(I32)
                                     ).then_inc(meta_ready, 1)
                t = loc - 2
                if inside(it, TPI, t, NT):
                    pool.wait_ge(y_ready, it * TPI + t + 1)
                    pass_waits(pool)
                    pool.indirect_dma_start(
                        expert_out[:, :], bass.IndirectOffsetOnAxis(ap=META[:, t % TPI, 1:2].bitcast(U32), axis=0),
                        YS[:, t % TPI, :], None, bounds_check=2 * TOK - 1, oob_is_err=False).then_inc(y_out[t % TPI], 16)

            tile_blocks(pool, step)

        def experts_scalar(act):
            pad_regions(act, range(NE // 2, NE))
            act.wait_ge(rows_placed, 1)

            def step(it, loc):
                t = loc + 4
                if inside(it, TPI, t, NT):
                    if inside(it, TPI, t - TPI, NT):
                        act.wait_ge(xs_turned, it * TPI + t - TPI + 1)
                        act.wait_ge(meta_ready, it * TPI + t - TPI + 1)
                    row = act.value_load(tr_i[0:1, bass.ds(it * TPI + t, 1)], min_val=0, max_val=ROWS - P)
                    act.dma_start(XS[:, t % TPI, :], routed[bass.ds(row, P), :]).then_inc(xs_in[t % TPI], 16)
                t = loc + 1
                if inside(it, TPI, t, NT):
                    act.wait_ge(xs_turned, it * TPI + t + 1)
                    if inside(it, TPI, t - 2, NT):
                        act.wait_ge(gu_done, it * TPI + t - 1)
                    act.activation(XST[0][:, t % 2, :], bank(4)[:, 0:D], ACT.Copy).then_inc(xst_high, 1)
                t = loc
                if inside(it, TPI, t, NT):
                    act.wait_ge(gu_done, it * TPI + t + 1)
                    if inside(it, TPI, t - 2, NT):
                        act.wait_ge(h_ready, it * TPI + t - 1)
                    act.activation(SG[:, t % 2, :], bank(2 * (t % 2)), ACT.Silu).then_inc(silu_ready, 1)
                t = loc - 1
                if inside(it, TPI, t, NT):
                    act.wait_ge(h_turned, it * TPI + t + 1)
                    if inside(it, TPI, t - 2, NT):
                        act.wait_ge(down_done, it * TPI + t)
                    act.activation(HST[0][:, t % 2, :], bank(5), ACT.Copy).then_inc(ht_high, 1)

            tile_blocks(act, step)

        def experts_vector(dve):
            def step(it, loc):
                t = loc + 1
                if inside(it, TPI, t, NT):
                    dve.wait_ge(xst_high, it * TPI + t + 1)
                    dve.tensor_tensor(XST[1][:, t % 2, :], bank(4)[:, 0:D], XST[0][:, t % 2, :].bitcast(F32),
                                      ALU.subtract).then_inc(xst_ready, 1)
                t = loc
                if inside(it, TPI, t, NT):
                    dve.wait_ge(silu_ready, it * TPI + t + 1)
                    if inside(it, TPI, t - 2, NT):
                        dve.wait_ge(h_turned, it * TPI + t - 1)
                    dve.tensor_tensor(HS[:, t % 2, :], bank(2 * (t % 2) + 1), SG[:, t % 2, :], ALU.mult
                                      ).then_inc(h_ready, 1)
                t = loc - 1
                if inside(it, TPI, t, NT):
                    dve.wait_ge(ht_high, it * TPI + t + 1)
                    dve.tensor_tensor(HST[1][:, t % 2, :], bank(5), HST[0][:, t % 2, :].bitcast(F32),
                                      ALU.subtract).then_inc(ht_ready, 1)
                t = loc - 2
                if inside(it, TPI, t, NT):
                    dve.wait_ge(down_done, it * TPI + t + 2)
                    dve.wait_ge(meta_ready, it * TPI + t + 1)
                    if inside(it, TPI, t - TPI, NT):
                        dve.wait_ge(y_out[t % TPI], it * 16 + 16 * (t // TPI))
                    dve.tensor_scalar(YS[:, t % TPI, :], bank(6)[:, 0:D], META[:, t % TPI, 0:1], None, ALU.mult
                                      ).then_inc(y_ready, 1)

            tile_blocks(dve, step)
            for q in range(NB // BQ):
                dve.wait_ge(parts_in[q], 32)
                xq = X1[:, q * BQ * D:(q + 1) * BQ * D]
                dve.tensor_tensor(xq, xq, part(q, 0), ALU.add).then_inc(sum_step, 1)
                dve.wait_ge(sum_step, 2 * q + 1)
                dve.tensor_tensor(xq, xq, part(q, 1), ALU.add).then_inc(sum_step, 1)

        def experts_tensor(pe):
            pe.sem_inc(down_done, 1)
            pe.wait_ge(low_ready, 6 * NE)
            pe.wait_ge(table_step, TABLE)

            def ring_at(it, t):
                w0 = pe.value_load(te_i[0:1, bass.ds(it * TPI + t, 1)], min_val=0, max_val=(SLOTS - 1) * 2 * EW)
                loaded = pe.value_load(tw_i[0:1, bass.ds(it * TPI + t, 1)], min_val=32, max_val=32 * NE)
                return w0, loaded

            def column_at(it, t):
                if not inside(it, TPI, t, NT):
                    return None
                return pe.value_load(te_i[0:1, bass.ds(it * TPI + t, 1)], min_val=0, max_val=(SLOTS - 1) * 2 * EW),

            held = {}

            def step(it, loc):
                if loc == 0:
                    held[-2] = column_at(it, -2)
                    if inside(it, TPI, 0, NT):
                        held[0] = ring_at(it, 0)
                    else:
                        held[-1] = column_at(it, -1)
                t = loc + 1
                if inside(it, TPI, t, NT):
                    pe.wait_ge(xs_in[t % TPI], it * 16 + 16 * (t // TPI + 1))
                    if inside(it, TPI, t - 1, NT):
                        pe.wait_ge(xst_ready, it * TPI + t)
                    for k in range(KC):
                        ins = pe.transpose(bank(4)[:, k * P:(k + 1) * P], XS[:, t % TPI, k * P:(k + 1) * P], ident[:, :])
                    ins.then_inc(xs_turned, 1)
                t = loc
                if inside(it, TPI, t, NT):
                    w0, loaded = held[loc]
                    pe.wait_ge(weights_in, loaded)
                    pe.wait_ge(xst_ready, it * TPI + t + 1)
                    if inside(it, TPI, t - 2, NT):
                        pe.wait_ge(h_ready, it * TPI + t - 1)
                    for n in range(2):
                        for k in range(KC):
                            for i, (a, b) in enumerate(SPLIT):
                                ins = pe.matmul(bank(2 * (t % 2) + n), XST[a][:, t % 2, k * P:(k + 1) * P],
                                                W[:, bass.ds(w0 + (b * EW + (2 * k + n) * F), F)],
                                                start=(k == 0 and i == 0), stop=(k == KC - 1 and i == 2))
                    ins.then_inc(gu_done, 1)
                    if loc == 0:
                        held[-1] = column_at(it, -1)
                    if loc + 1 < TPI:
                        held[loc + 1] = ring_at(it, t + 1)
                t = loc - 1
                if inside(it, TPI, t, NT):
                    pe.wait_ge(h_ready, it * TPI + t + 1)
                    if inside(it, TPI, t - 1, NT):
                        pe.wait_ge(ht_ready, it * TPI + t)
                    for c in range(FC):
                        ins = pe.transpose(bank(5)[:, c * P:(c + 1) * P], HS[:, t % 2, c * P:(c + 1) * P], ident[:, :])
                    ins.then_inc(h_turned, 1)
                t = loc - 2
                if inside(it, TPI, t, NT):
                    w0 = held[t][0]
                    pe.wait_ge(ht_ready, it * TPI + t + 1)
                    if inside(it, TPI, t - 1, NT):
                        pe.wait_ge(y_ready, it * TPI + t)
                    for c in range(FC):
                        for i, (a, b) in enumerate(SPLIT):
                            ins = pe.matmul(bank(6)[:, 0:D], HST[a][:, t % 2, c * P:(c + 1) * P],
                                            W[:, bass.ds(w0 + (b * EW + GUW + c * D), D)],
                                            start=(c == 0 and i == 0), stop=(c == FC - 1 and i == 2))
                    ins.then_inc(down_done, 1)

            tile_blocks(pe, step)

        waits_met = {nc.vector: sem("dve_waits_met"), nc.gpsimd: sem("pool_waits_met"),
                     nc.scalar: sem("act_waits_met"), nc.sync: sem("sp_waits_met")}

        def pass_waits(eng):
            eng.sem_inc(waits_met[eng], 1)

        block = stack.enter_context(nc.Block())

        def bank(i):
            return PS[:, i, :]

        def split_chunk(part, i):
            return W[:, part * EW + i * CHW:part * EW + (i + 1) * CHW]

        def weights_of(w):
            return w.rearrange("(c p) d -> p c d", p=P)

        N_SETUP = 5 + 8 + 3 + 1

        def attention_blocks(eng, step):
            for it in (-1, 0, 1):
                for loc in range(SPI):
                    step(it, loc)
            with eng.Fori(2, NIT - 1) as it:
                for loc in range(SPI):
                    step(it, loc)
            for it in (NIT - 1, NIT):
                for loc in range(SPI):
                    step(it, loc)

        W_in = [w_raw[:, i * KC * D:(i + 1) * KC * D].rearrange("p (c d) -> p c d", c=KC) for i in range(4)]
        Wr_in = w_raw[0:NE, 4 * KC * D:4 * KC * D + D]
        delta_in = w_raw[0:NB, 4 * KC * D + D:4 * KC * D + D + L]

        @block.sync
        def _(sp):
            for w, t in zip((Wq, Wk, Wv, Wo), W_in):
                sp.dma_start(t, weights_of(w)).then_inc(setup_in, 16)
            sp.dma_start(Wr_in, router).then_inc(setup_in, 16)
            sp.dma_start(delta_in, delta).then_inc(setup_in, 16)
            for v, t in ((bv, bv_all), (bo, bo_all), (tau, tau_all)):
                sp.dma_start(t[:, :], v.partition_broadcast(P)).then_inc(setup_in, 16)
            sp.wait_ge(dve_const, 9)
            for b, t in ((bq, bq_pad), (bk, bk_pad)):
                by_row = b.rearrange("(g j r) -> j r g", g=G, j=G)
                for j in range(G):
                    sp.dma_start(t[PADH * j:PADH * j + E, :], by_row[j], allow_slow_non_contiguous=True).then_inc(setup_in, 16)

            def step(it, loc):
                weights_step(it, loc)
                if loc % 8 != 0:
                    return
                ul = loc // 8
                if inside(it, UPI, ul + 2, NU):
                    if inside(it, UPI, ul, NU):
                        sp.wait_ge(ln1_stats, it * UPI * 4 + 4 * (ul + 1))
                    b = it * (UPI * UB) + UB * (ul + 2)
                    dst = X1[:, bass.ds(b * D, UB * D)].rearrange("p (b d) -> p b d", b=UB)
                    sp.dma_start(dst, x_flat[:, bass.ds(b, UB), :]).then_inc(x_in[ul % 2], 16)
                if inside(it, UPI, ul + 2, NU):
                    if inside(it, UPI, ul, NU):
                        sp.wait_ge(pj_filled, it * UPI * FILLS + FILLS * ul + 6)
                    b = it * (UPI * UB) + UB * (ul + 2)
                    sp.dma_start(CTX[:, ul % 2, :, :], c_flat[:, bass.ds(b, UB), :]).then_inc(c_in[ul % 2], 16)
                    sp.dma_start(DEL[:, ul % 2, :], delta_row[:, bass.ds(b * L, UT)]).then_inc(c_in[ul % 2], 16)

            def weights_step(it, loc):
                if loc < 5 and inside(it, 1, 0, NE):
                    if not isinstance(it, int) or it * SPI + loc > 0:
                        sp.wait_ge(s1_done, it * SPI + loc)
                        pass_waits(sp)
                if loc < 2 and inside(it, 1, -1, NE - 1):
                    sp.wait_ge(low_ready, it * 6)
                    pass_waits(sp)
                    c0, c1 = loc * EW, (loc + 1) * EW
                    sp.dma_start(split_w[bass.ds((it - 1) * P, P), c0:c1], W[:, c0:c1].bitcast(F32)).then_inc(split_out, 16)
                if 2 <= loc < 5 and inside(it, 1, 0, NE):
                    if isinstance(it, int) and it == 0 and loc == 2:
                        sp.wait_ge(wt_turned, 5)
                    pass_waits(sp)
                    if loc < 4:
                        n = loc - 2
                        dst = w_raw[:, 0:GUW].rearrange("p (k n f) -> p k n f", k=KC, n=2)
                        src = (w_gate, w_up)[n][bass.ds(it, 1), :, :].rearrange("o (k p) f -> p (o k) f", p=P)
                        sp.dma_start(dst[:, :, n, :], src).then_inc(raw_in, 16)
                    else:
                        dst = w_raw[:, GUW:EW].rearrange("p (c d) -> p c d", c=FC)
                        src = w_down[bass.ds(it, 1), :, :].rearrange("o (c p) d -> p (o c) d", p=P)
                        sp.dma_start(dst, src).then_inc(raw_in, 16)

            attention_blocks(sp, step)

            sp.wait_ge(pool_const, 17)
            for t in range(NE):
                sp.dma_start(routed[NE * REG + t * P:NE * REG + (t + 1) * P, :], PAD[:, :]).then_inc(dead_in, 16)
            pad_regions(sp, range(0, NE // 2))
            experts_sync(sp)

        @block.gpsimd
        def _(pool):
            def const(ins):
                ins.then_inc(pool_const, 1)

            const(pool.memset(ident[:, :], 0.0))
            const(pool.memset(before, 1.0))
            const(pool.memset(minus_half[:, :], -0.5))
            const(pool.memset(PAD[:, :], 0.0))
            const(pool.iota(row_i[:, :], [[0, 1]], base=0, channel_multiplier=1))
            const(pool.iota(col_i[:, :], [[1, P]], base=0, channel_multiplier=0))
            const(pool.iota(expert_i[:, :], [[1, NE]], base=0, channel_multiplier=0))
            const(pool.iota(base_i[:, :], [[REG, NE]], base=0, channel_multiplier=0))
            const(pool.iota(out_rows[:, :], [[TOK, 2], [L, NB]], base=0, channel_multiplier=1))
            const(pool.iota(j_i[:, :], [[P, NB]], base=0, channel_multiplier=0))
            const(pool.iota(t_i[:, :], [[1, NT]], base=0, channel_multiplier=0))
            pool.wait_ge(pool_const, 11)
            const(pool.affine_select(out=ident[:, :], in_=ident[:, :], compare_op=ALU.not_equal, fill=1.0,
                                     base=0, pattern=[[-1, P]], channel_multiplier=1))
            const(pool.affine_select(out=before, in_=before, compare_op=ALU.is_gt, fill=0.0,
                                     base=0, pattern=[[1, P]], channel_multiplier=-1))
            const(pool.iota(PAD[:, D + 1:D + 2].bitcast(I32), [[0, 1]], base=2 * TOK, channel_multiplier=1))
            const(pool.memset(W_whole[0], 0.0))
            const(pool.memset(W_whole[1], 0.0))
            const(pool.memset(V[:, :, :, :, :], 0.0))
            pool.wait_ge(pool_const, 17)
            const(pool.memset(V[:, :, :, :, E:E + 1], 1.0))

            def step(it, loc):
                ul, s, j = loc // 8, loc % 8, loc % G
                if s == 2 and inside(it, UPI, ul + 1, NU):
                    pool.wait_ge(c_in[(ul + 1) % 2], it * 32 + 32 * ((ul + 1) // 2 + 1))
                    if inside(it, UPI, ul, NU):
                        pool.wait_ge(pj_filled, it * UPI * FILLS + FILLS * ul + 6)
                    pass_waits(pool)
                    pool.tensor_copy(DR[:, :], DEL[:, (ul + 1) % 2, :]).then_inc(delta_rounded, 1)
                if s == 3 and inside(it, UPI, ul + 2, NU):
                    pool.wait_ge(ln1_stats, it * UPI * 4 + 4 * (ul + 3))
                    if inside(it, UPI, ul + 1, NU):
                        pool.wait_ge(xn_ready, it * UPI * UB + UB * (ul + 2))
                    pass_waits(pool)
                    pool.tensor_scalar(ln_rstd[:, :], ln_mv[:, :, 1], LN_EPS, None, ALU.add).then_inc(ln1_rstd, 1)
                    pool.wait_ge(ln1_rstd, it * UPI * 2 + 2 * (ul + 2) + 1)
                    pool.tensor_tensor(ln_rstd[:, :], ln_rstd[:, :], minus_half[:, :], ALU.pow).then_inc(ln1_rstd, 1)
                if s == 7 and inside(it, UPI, ul + 2, NU):
                    pool.wait_ge(xn_ready, it * UPI * UB + UB * (ul + 3))
                    if isinstance(it, int) and it * UPI + ul + 2 == 0:
                        pool.wait_ge(setup_in, 16 * N_SETUP)
                    for b in range(UB):
                        xb = X1[:, bass.ds((it * (UPI * UB) + UB * (ul + 2) + b) * D, D)]
                        pool.tensor_tensor(xb, xb, bo_all[:, :], ALU.add).then_inc(x_biased, 1)
                if j == 1:
                    bl = (loc - 9) // G
                    if inside(it, BPI, bl, NB):
                        pool.wait_ge(ln2_step, it * BPI * 3 + 3 * (bl + 1))
                        if inside(it, BPI, bl - 1, NB):
                            pool.wait_ge(xp_ready, it * BPI + bl)
                        pass_waits(pool)
                        pool.tensor_scalar(rstd2[:, :], mv2[:, 1:2], LN_EPS, None, ALU.add).then_inc(ln2_rstd, 1)
                        pool.wait_ge(ln2_rstd, it * BPI * 2 + 2 * bl + 1)
                        pool.tensor_tensor(rstd2[:, :], rstd2[:, :], minus_half[:, 0:1], ALU.pow).then_inc(ln2_rstd, 1)
                if j == 2:
                    bl = (loc - 10) // G
                    if inside(it, BPI, bl, NB):
                        if inside(it, BPI, bl - 4, NB):
                            pool.wait_ge(scattered[bl % 4], it * 32 + 32 * (bl // 4))
                        pool.wait_ge(xp_ready, it * BPI + bl + 1)
                        pass_waits(pool)
                        pool.tensor_copy(XP[:, bl % 4, 1, 0:D], XP[:, bl % 4, 0, 0:D]).then_inc(xp_copied, 1)
                        for k in range(2):
                            pool.tensor_copy(XP[:, bl % 4, k, D + 1:D + 2].bitcast(I32),
                                             out_rows[:, bass.ds(it * BPI + bl + k * NB, 1)]).then_inc(xp_copied, 1)
                if j == 2:
                    bl = (loc - 18) // G
                    if inside(it, BPI, bl, NB):
                        pool.wait_ge(route_step, it * BPI * 17 + 17 * (bl + 1))
                        pool.wait_ge(xp_copied, it * BPI * 3 + 3 * (bl + 1))
                        pass_waits(pool)
                        for k in range(2):
                            pool.indirect_dma_start(
                                routed[:, :], bass.IndirectOffsetOnAxis(ap=slot[:, bl % 4, k:k + 1].bitcast(U32), axis=0),
                                XP[:, bl % 4, k, :], None).then_inc(scattered[bl % 4], 16)

                if 10 <= loc and inside(it, 1, 0, NE):
                    i = loc - 10
                    pool.wait_ge(high_ready, it * 6 + i + 1)
                    pool.tensor_tensor(split_chunk(1, i), w_raw[:, i * CHW:(i + 1) * CHW],
                                       split_chunk(0, i).bitcast(F32), ALU.subtract).then_inc(low_ready, 1)

            attention_blocks(pool, step)
            experts_pool(pool)

        @block.vector
        def _(dve):
            dve.memset(bq_pad[:, :], 0.0).then_inc(dve_const, 1)
            dve.memset(bk_pad[:, :], 0.0).then_inc(dve_const, 1)
            dve.memset(ones_b[:, :], 1.0).then_inc(dve_const, 1)
            dve.wait_ge(pool_const, 11)
            dve.tensor_scalar(row_i[:, :], row_i[:, :], 31, None, ALU.bitwise_and).then_inc(dve_const, 1)
            dve.wait_ge(dve_const, 4)
            dve.tensor_copy(row_f[:, :], row_i[:, :]).then_inc(dve_const, 1)
            dve.wait_ge(dve_const, 5)
            dve.tensor_scalar(is_real[:, :], row_f[:, :], float(E), None, ALU.is_lt).then_inc(dve_const, 1)
            dve.tensor_scalar(is_delta[:, :], row_f[:, :], float(E), None, ALU.is_equal).then_inc(dve_const, 1)
            dve.wait_ge(dve_const, 7)
            dve.tensor_copy(bq_pad[:, :], is_delta[:, 0:1].to_broadcast([P, G])).then_inc(dve_const, 1)
            dve.wait_ge(dve_const, 8)
            dve.tensor_scalar(col_i[:, :], col_i[:, :], 31, None, ALU.bitwise_and).then_inc(dve_const, 1)
            dve.wait_ge(dve_const, 9)
            dve.tensor_copy(col_f[:, :], col_i[:, :]).then_inc(dve_const, 1)
            dve.wait_ge(dve_const, 10)
            dve.tensor_scalar(delta_rows[:, :], col_f[:, :], float(E), None, ALU.is_equal).then_inc(dve_const, 1)
            dve.tensor_copy(expert_f[:, :], expert_i[:, :]).then_inc(dve_const, 1)
            dve.tensor_copy(counts[:, :], base_i[:, :]).then_inc(dve_const, 1)
            dve.tensor_copy(start_f[:, :], base_i[0:1, :]).then_inc(dve_const, 1)
            dve.tensor_copy(j_f[:, :], j_i[:, :]).then_inc(dve_const, 1)
            dve.tensor_copy(t_f[:, :], t_i[:, :]).then_inc(dve_const, 1)
            dve.memset(ones8[:, :], 1.0).then_inc(dve_const, 1)
            dve.wait_ge(pool_const, 13)
            dve.tensor_scalar(ones_r[:, :], ident[:, :], 0.0, 1.0, ALU.mult, ALU.add).then_inc(dve_const, 1)
            dve.tensor_copy(before_b[:, :], before).then_inc(dve_const, 1)
            dve.wait_ge(setup_in, 16 * N_SETUP)
            dve.tensor_scalar(q_scale[:, :], tau_all[:, :], is_real[:, 0:1], is_delta[:, 0:1], ALU.mult, ALU.add
                              ).then_inc(dve_const, 1)
            dve.wait_ge(pool_const, 17)
            for n, w in enumerate((WqT, WkT)):
                dve.wait_ge(wt_turned, n + 1)
                for k in range(KC):
                    dve.tensor_copy(W_whole[n][:, k * G * P:(k + 1) * G * P].rearrange("p (h r) -> p h r", r=PADH)[:, :, 0:E],
                                    bank(n)[:, k * D:(k + 1) * D].rearrange("p (h r) -> p h r", r=E)
                                    ).then_inc(wt_spread, 1)
            for n, w in enumerate((WqT, WkT)):
                dve.wait_ge(wt_rounded, n + 1)
                high, low = (t[:, :, :, :].rearrange("p k g r -> p (k g r)") for t in w)
                dve.tensor_tensor(low, W_whole[n], high.bitcast(F32), ALU.subtract).then_inc(wt_ready, 1)
            for n, w in ((2, WvT), (3, WoT)):
                dve.wait_ge(wt_rounded, n + 1)
                high, low = (t[:, :, :].rearrange("p k d -> p (k d)") for t in w)
                dve.tensor_tensor(low, bank(n), high.bitcast(F32), ALU.subtract).then_inc(wt_ready, 1)
            dve.wait_ge(wt_turned, 5)
            dve.tensor_copy(WrT[:, :, :].rearrange("p k e -> p (k e)"), bank(4)[:, 0:KC * NE]).then_inc(wt_ready, 1)
            dve.tensor_copy(delta_high[:, :], bank(4)[:, P:P + NB]).then_inc(wt_ready, 1)
            dve.wait_ge(wt_ready, 6)
            dve.tensor_tensor(delta_low[:, :], bank(4)[:, P:P + NB], delta_high[:, :].bitcast(F32), ALU.subtract
                              ).then_inc(wt_ready, 1)
            dve.wait_ge(wt_ready, 7)
            dve.tensor_scalar(delta_low[:, :], delta_low[:, :], SCALE, None, ALU.mult).then_inc(wt_ready, 1)

            def route(k, ins):
                ins.then_inc(route_step, 1)

            def step(it, loc):
                ul, s, j = loc // 8, loc % 8, loc % G
                u = it * UPI
                if inside(it, SPI, loc, NSTEP):
                    dve.wait_ge(s1_done, it * SPI + loc + 1)
                    if inside(it, SPI, loc - 2, NSTEP):
                        dve.wait_ge(max_ready, it * SPI + loc - 1)
                    dve.tensor_reduce(NM[:, loc % 2, :], bank(loc % 2).rearrange("p (g s) -> p g s", g=G),
                                      AX.X, ALU.max, negate=True).then_inc(max_found, 1)
                if s == 3 and inside(it, UPI, ul + 2, NU):
                    dve.wait_ge(x_in[ul % 2], it * 16 * UPI // 2 + 16 * ((ul + 2) // 2 + 1))
                    if inside(it, UPI, ul + 1, NU):
                        dve.wait_ge(ln1_rstd, it * UPI * 2 + 2 * (ul + 2))
                        dve.wait_ge(xn_ready, it * UPI * UB + UB * (ul + 2))
                    base = it * (UPI * UB * D) + UB * (ul + 2) * D
                    pass_waits(dve)
                    for b in range(UB):
                        dve.bn_stats(ln_stats[:, b, :], X1[:, bass.ds(base + b * D, D)]).then_inc(ln1_stats, 1)
                    dve.wait_ge(ln1_stats, it * UPI * 4 + 4 * (ul + 2) + 2)
                    pass_waits(dve)
                    for b in range(UB):
                        dve.bn_aggr(ln_mv[:, b, :], ln_stats[:, b, :]).then_inc(ln1_stats, 1)
                if s == 6 and inside(it, UPI, ul + 2, NU):
                    dve.wait_ge(ln1_rstd, it * UPI * 2 + 2 * (ul + 3))
                    if inside(it, UPI, ul, NU):
                        dve.wait_ge(pj_filled, it * UPI * FILLS + FILLS * ul + 1)
                    base = it * (UPI * UB * D) + UB * (ul + 2) * D
                    for b in range(UB):
                        dve.tensor_scalar(XN[:, ul % 2, b, :], X1[:, bass.ds(base + b * D, D)], ln_mv[:, b, 0:1],
                                          ln_rstd[:, b:b + 1], ALU.subtract, ALU.mult).then_inc(xn_ready, 1)
                if s in (0, 1) and inside(it, UPI, ul + 1, NU):
                    dve.wait_ge(tokens_high, it * UPI * 2 + 2 * (ul + 1) + s + 1)
                    high, low = (t[:, :, :].rearrange("p k t -> p (k t)") for t in (XNT, CT)[s])
                    dve.tensor_tensor(low, bank(5), high.bitcast(F32), ALU.subtract).then_inc(pj_free, 1)
                if s in (2, 3) and inside(it, UPI, ul + 1, NU):
                    dve.wait_ge(pj_filled, it * UPI * FILLS + FILLS * (ul + 1) + s + 1)
                    if inside(it, UPI, ul - 1, NU):
                        dve.wait_ge(s2_done, it * SPI + 8 * ul)
                        dve.wait_ge(q_rounded, it * UPI * 2 + 2 * ul)
                    for h in range(2):
                        g = 2 * (s - 2) + h
                        qs = q_scale[:, bass.ds(it * (UPI * UB) + UB * (ul + 1), UB)]
                        ins = dve.scalar_tensor_tensor(
                            out=Q[:, (ul + 1) % 2, g, :].rearrange("p (b l) -> p b l", b=UB),
                            in0=bank(5)[:, h * UT:(h + 1) * UT].rearrange("p (b l) -> p b l", b=UB),
                            scalar=bq_pad[:, g:g + 1], in1=qs.unsqueeze(2).to_broadcast([P, UB, L]),
                            op0=ALU.add, op1=ALU.mult)
                    ins.then_inc(pj_free, 1)
                if s == 6 and inside(it, UPI, ul + 1, NU):
                    dve.wait_ge(pj_filled, it * UPI * FILLS + FILLS * (ul + 1) + s + 1)
                    if isinstance(it, int) and it * UPI + ul + 1 == 0:
                        dve.wait_ge(pool_const, 18)
                    if inside(it, UPI, ul - 1, NU):
                        dve.wait_ge(av_done, it * SPI + 8 * ul)
                    for b in range(UB):
                        ins = dve.tensor_tensor(
                            V[:, (ul + 1) % 2, b, :, 0:E],
                            bank(5)[:, b * D:(b + 1) * D].rearrange("p (h e) -> p h e", h=H),
                            bv_all[:, :].rearrange("p (h e) -> p h e", h=H), ALU.add)
                    ins.then_inc(pj_free, 1)
                if j == 3:
                    bl = (loc - 7) // G
                    if inside(it, BPI, bl, NB):
                        dve.wait_ge(ott_done, it * BPI + bl + 1)
                        by_head = bank(7).rearrange("p (j g r) -> p j g r", j=G, g=G)
                        if inside(it, BPI, bl - 1, NB):
                            dve.wait_ge(on_step, it * BPI * 2 + 2 * bl)
                        dve.reciprocal(rden[:, :, :], by_head[:, :, :, E]).then_inc(on_step, 1)
                        dve.wait_ge(on_step, it * BPI * 2 + 2 * bl + 1)
                        if inside(it, BPI, bl - 1, NB):
                            dve.wait_ge(ot2_done, it * BPI + bl)
                        dve.tensor_tensor(ON[:, :].rearrange("p (g j r) -> p j g r", g=G, j=G),
                                          by_head[:, :, :, 0:E],
                                          rden[:, :, :].unsqueeze(3).to_broadcast([P, G, G, E]), ALU.mult
                                          ).then_inc(on_step, 1)
                if j == 0:
                    bl = (loc - 8) // G
                    if inside(it, BPI, bl, NB):
                        dve.wait_ge(ont_high, it * BPI + bl + 1)
                        high, low = (t[:, :, :].rearrange("p k l -> p (k l)") for t in ONT)
                        dve.tensor_tensor(low, bank(7)[:, 0:KC * P], high.bitcast(F32), ALU.subtract
                                          ).then_inc(ont_ready, 1)
                if j == 1:
                    bl = (loc - 9) // G
                    if inside(it, BPI, bl, NB):
                        dve.wait_ge(wo_done, it * BPI + bl + 1)
                        dve.wait_ge(x_biased, it * BPI + bl + 1)
                        xb = X1[:, bass.ds((it * BPI + bl) * D, D)]
                        dve.tensor_tensor(xb, bank(7)[:, 0:D], xb, ALU.add).then_inc(ln2_step, 1)
                        dve.wait_ge(ln2_step, it * BPI * 3 + 3 * bl + 1)
                        pass_waits(dve)
                        dve.bn_stats(st2[:, :], xb).then_inc(ln2_step, 1)
                        dve.wait_ge(ln2_step, it * BPI * 3 + 3 * bl + 2)
                        if inside(it, BPI, bl - 1, NB):
                            dve.wait_ge(ln2_rstd, it * BPI * 2 + 2 * bl)
                            dve.wait_ge(xp_ready, it * BPI + bl)
                        pass_waits(dve)
                        dve.bn_aggr(mv2[:, :], st2[:, :]).then_inc(ln2_step, 1)
                if j == 2:
                    bl = (loc - 10) // G
                    if inside(it, BPI, bl, NB):
                        dve.wait_ge(ln2_rstd, it * BPI * 2 + 2 * (bl + 1))
                        if inside(it, BPI, bl - 4, NB):
                            dve.wait_ge(scattered[bl % 4], it * 32 + 32 * (bl // 4))
                        dve.tensor_scalar(XP[:, bl % 4, 0, 0:D], X1[:, bass.ds((it * BPI + bl) * D, D)], mv2[:, 0:1],
                                          rstd2[:, 0:1], ALU.subtract, ALU.mult).then_inc(xp_ready, 1)
                if j == 2:
                    bl = (loc - 14) // G
                    if inside(it, BPI, bl, NB):
                        r0 = it * BPI * 17 + 17 * bl
                        if inside(it, BPI, bl - 1, NB):
                            dve.wait_ge(route_step, r0)
                        dve.wait_ge(logits_done, it * BPI + bl + 1)
                        route(1, dve.tensor_copy(lg[:, :], bank(7)[:, 0:NE]))
                        dve.wait_ge(route_step, r0 + 1)
                        pass_waits(dve)
                        route(2, dve.max(mx[:, :], lg[:, :]))
                        dve.wait_ge(route_step, r0 + 2)
                        pass_waits(dve)
                        route(3, dve.max_index(mi[:, :], mx[:, :], lg[:, :]))
                        dve.wait_ge(route_step, r0 + 3)
                        route(4, dve.tensor_copy(mif[:, :], mi[:, 0:2]))
                        dve.wait_ge(route_step, r0 + 4)
                        for k in range(2):
                            route(5 + k, dve.tensor_scalar(M[:, k, :], expert_f[:, :], mif[:, k:k + 1], None, ALU.is_equal))
                        dve.wait_ge(route_step, r0 + 6)
                        route(7, dve.tensor_tensor(Mb[:, :], M[:, 0, :], M[:, 1, :], ALU.add))
                if j == 3:
                    bl = (loc - 15) // G
                    if inside(it, BPI, bl, NB):
                        r0 = it * BPI * 17 + 17 * bl
                        dve.wait_ge(gate_exp, it * BPI + bl + 1)
                        route(8, dve.tensor_scalar(gp[:, :], ge[:, :], 1.0, None, ALU.add))
                        dve.wait_ge(route_step, r0 + 8)
                        route(9, dve.reciprocal(gs[:, :], gp[:, :]))
                        dve.wait_ge(route_step, r0 + 9)
                        route(10, dve.scalar_tensor_tensor(out=gsum[:, :], in0=gs[:, 0:1], scalar=1e-10,
                                                           in1=gs[:, 1:2], op0=ALU.add, op1=ALU.add))
                        dve.wait_ge(route_step, r0 + 10)
                        route(11, dve.reciprocal(grec[:, :], gsum[:, :]))
                        dve.wait_ge(route_step, r0 + 11)
                        route(12, dve.tensor_scalar(XP[:, bl % 4, :, D], gs[:, :], grec[:, 0:1], None, ALU.mult))
                if j == 1:
                    bl = (loc - 17) // G
                    if inside(it, BPI, bl, NB):
                        r0 = it * BPI * 17 + 17 * bl
                        dve.wait_ge(rank_done, it * BPI + bl + 1)
                        dve.wait_ge(route_step, r0 + 12)
                        route(13, dve.tensor_tensor(rank[:, :], bank(6)[:, 0:NE], counts[:, :], ALU.add))
                        dve.wait_ge(route_step, r0 + 13)
                        route(14, dve.tensor_tensor(counts[:, :], bank(6)[:, NE:2 * NE], counts[:, :], ALU.add))
                        route(15, dve.tensor_tensor(rsel[:, :, :], M[:, :, :],
                                                    rank[:, :].unsqueeze(1).to_broadcast([P, 2, NE]), ALU.mult))
                        dve.wait_ge(route_step, r0 + 15)
                        route(16, dve.tensor_reduce(slot_f[:, :], rsel[:, :, :], AX.X, ALU.add))
                        dve.wait_ge(route_step, r0 + 16)
                        route(17, dve.tensor_copy(slot[:, bl % 4, :], slot_f[:, :]))

            attention_blocks(dve, step)

            dve.wait_ge(route_step, 17 * NB)
            dve.tensor_copy(end_i[:, :], counts[0:1, :]).then_inc(table_step, 1)
            dve.tensor_tensor(cnt[:, :], counts[0:1, :], start_f[:, :], ALU.subtract).then_inc(table_step, 1)
            dve.wait_ge(table_step, 2)
            dve.tensor_tensor(over, cnt[:, :].unsqueeze(2).to_broadcast([1, NE, NB]),
                              j_f[:, :].unsqueeze(1).to_broadcast([1, NE, NB]), ALU.is_gt).then_inc(table_step, 1)
            dve.wait_ge(table_step, 3)
            dve.tensor_reduce(ntile[:, :], over, AX.X, ALU.add).then_inc(table_step, 1)
            dve.wait_ge(table_step, 4)
            dve.tensor_copy(placed[:, 0:1], ntile[:, NE - 1:NE]).then_inc(table_step, 1)
            dve.tensor_copy(placed[:, 1:NE], ntile[:, 0:NE - 1]).then_inc(table_step, 1)
            dve.wait_ge(table_step, 6)
            dve.tensor_tensor_scan(upto[:, :], ones8[:, :], placed[:, :], 0.0, ALU.mult, ALU.add).then_inc(table_step, 1)
            dve.tensor_scalar(jump[:, :], placed[:, :], -float(P), float(REG), ALU.mult, ALU.add).then_inc(table_step, 1)
            dve.wait_ge(table_step, 8)
            dve.tensor_scalar(jump[:, 0:1], jump[:, 0:1], -float(NE * REG), None, ALU.add).then_inc(table_step, 1)
            dve.tensor_scalar(jump[:, NE - 1:NE], jump[:, NE - 1:NE], float(REG), None, ALU.add).then_inc(table_step, 1)
            dve.tensor_tensor(past, t_f[:, :].unsqueeze(2).to_broadcast([1, NT, NE]),
                              upto[:, :].unsqueeze(1).to_broadcast([1, NT, NE]), ALU.is_ge).then_inc(table_step, 1)
            dve.tensor_scalar(upto_i[:, :], upto[:, :], 1.0, None, ALU.add).then_inc(table_step, 1)
            dve.wait_ge(table_step, 12)
            dve.tensor_tensor(pastj, past, jump[:, :].unsqueeze(1).to_broadcast([1, NT, NE]),
                              ALU.mult).then_inc(table_step, 1)
            dve.tensor_reduce(te_f[:, :], past, AX.X, ALU.add).then_inc(table_step, 1)
            dve.wait_ge(table_step, 14)
            dve.tensor_reduce(tr_f[:, :], pastj, AX.X, ALU.add).then_inc(table_step, 1)
            dve.tensor_scalar(place[:, :], te_f[:, :], float(NE - 1), None, ALU.min).then_inc(table_step, 1)
            dve.wait_ge(table_step, 16)
            dve.tensor_scalar(tr_f[:, :], tr_f[:, :], float(expert_at(0) * REG), None, ALU.add).then_inc(table_step, 1)
            dve.tensor_scalar(turn1[:, :], place[:, :], float(SLOTS), None, ALU.is_ge).then_inc(table_step, 1)
            dve.tensor_scalar(turn2[:, :], place[:, :], float(2 * SLOTS), None, ALU.is_ge).then_inc(table_step, 1)
            dve.tensor_scalar(tw_f[:, :], place[:, :], 1.0, None, ALU.add).then_inc(table_step, 1)
            dve.wait_ge(table_step, 20)
            dve.scalar_tensor_tensor(out=tr_i[:, :], in0=t_f[:, :], scalar=float(P), in1=tr_f[:, :],
                                     op0=ALU.mult, op1=ALU.add).then_inc(table_step, 1)
            dve.tensor_scalar(tw_i[:, :], tw_f[:, :], 32.0, None, ALU.mult).then_inc(table_step, 1)
            dve.tensor_tensor(turn1[:, :], turn1[:, :], turn2[:, :], ALU.add).then_inc(table_step, 1)
            dve.wait_ge(table_step, 23)
            dve.scalar_tensor_tensor(out=place[:, :], in0=turn1[:, :], scalar=-float(SLOTS), in1=place[:, :],
                                     op0=ALU.mult, op1=ALU.add).then_inc(table_step, 1)
            dve.wait_ge(table_step, 24)
            dve.tensor_scalar(te_i[:, :], place[:, :], float(2 * EW), None, ALU.mult).then_inc(table_step, 1)
            experts_vector(dve)

        @block.scalar
        def _(act):
            for n, w in enumerate((WqT, WkT)):
                act.wait_ge(wt_spread, 2 * (n + 1))
                act.activation(w[0][:, :, :, :].rearrange("p k g r -> p (k g r)"), W_whole[n], ACT.Copy
                               ).then_inc(wt_rounded, 1)
            for n, w in ((2, WvT), (3, WoT)):
                act.wait_ge(wt_turned, n + 1)
                act.activation(w[0][:, :, :].rearrange("p k d -> p (k d)"), bank(n), ACT.Copy).then_inc(wt_rounded, 1)

            def step(it, loc):
                ul, s, j = loc // 8, loc % 8, loc % G
                if inside(it, SPI, loc - 1, NSTEP):
                    act.wait_ge(max_found, it * SPI + loc)
                    if inside(it, SPI, loc - 3, NSTEP):
                        act.wait_ge(max_used, it * SPI + loc - 2)
                    k = (loc - 1) % 2
                    for g in range(G):
                        ins = act.activation(NMD[:, k, g, :], ident[:, :], ACT.Copy, scale=NM[:, k, g:g + 1])
                    ins.then_inc(max_ready, 1)
                if inside(it, SPI, loc - 2, NSTEP):
                    act.wait_ge(s2_done, it * SPI + loc - 1)
                    if inside(it, SPI, loc - 4, NSTEP):
                        act.wait_ge(av_done, it * SPI + loc - 3)
                    k = loc % 2
                    pass_waits(act)
                    act.activation(AT[:, k, :], bank(2 + k), ACT.Exp, scale=SCALE,
                                   bias=delta_low[:, bass.ds(it * BPI + (loc - 2) // G, 1)]).then_inc(probs_ready, 1)
                if s in (0, 1) and inside(it, UPI, ul + 1, NU):
                    act.wait_ge(pj_filled, it * UPI * FILLS + FILLS * (ul + 1) + s + 1)
                    dst = (XNT, CT)[s]
                    act.activation(dst[0][:, :, :].rearrange("p k t -> p (k t)"), bank(5), ACT.Copy
                                   ).then_inc(tokens_high, 1)
                if s in (2, 3) and inside(it, UPI, ul + 1, NU):
                    act.wait_ge(pj_free, it * UPI * FILLS + FILLS * (ul + 1) + s + 1)
                    if inside(it, UPI, ul - 1, NU):
                        act.wait_ge(s1_done, it * SPI + 8 * ul)
                    g = 2 * (s - 2)
                    act.activation(QR[:, (ul + 1) % 2, g:g + 2, :], Q[:, (ul + 1) % 2, g:g + 2, :],
                                   ACT.Copy).then_inc(q_rounded, 1)
                if s in (4, 5) and inside(it, UPI, ul + 1, NU):
                    act.wait_ge(pj_filled, it * UPI * FILLS + FILLS * (ul + 1) + s + 1)
                    if inside(it, UPI, ul - 1, NU):
                        act.wait_ge(s2_done, it * SPI + 8 * ul)
                    for h in range(2):
                        g = 2 * (s - 4) + h
                        ins = act.activation(K[:, (ul + 1) % 2, g, :], bank(5)[:, h * UT:(h + 1) * UT], ACT.Identity,
                                             bias=bk_pad[:, g:g + 1])
                    ins.then_inc(pj_free, 1)
                    act.wait_ge(pj_free, it * UPI * FILLS + FILLS * (ul + 1) + s + 1)
                    g = 2 * (s - 4)
                    act.activation(KR[:, (ul + 1) % 2, g:g + 2, :], K[:, (ul + 1) % 2, g:g + 2, :],
                                   ACT.Copy).then_inc(k_rounded, 1)
                if j == 2:
                    bl = (loc - 6) // G
                    if inside(it, BPI, bl, NB):
                        act.wait_ge(av_done, it * SPI + G * (bl + 1))
                        if inside(it, BPI, bl - 1, NB):
                            act.wait_ge(ott_done, it * BPI + bl)
                        act.activation(OT[:, :], bank(4), ACT.Copy).then_inc(ot_ready, 1)
                if j == 0:
                    bl = (loc - 8) // G
                    if inside(it, BPI, bl, NB):
                        act.wait_ge(ot2_done, it * BPI + bl + 1)
                        if inside(it, BPI, bl - 1, NB):
                            act.wait_ge(wo_done, it * BPI + bl)
                        act.activation(ONT[0][:, :, :].rearrange("p k l -> p (k l)"), bank(7)[:, 0:KC * P], ACT.Copy
                                       ).then_inc(ont_high, 1)
                if j == 3:
                    bl = (loc - 11) // G
                    if inside(it, BPI, bl, NB):
                        act.wait_ge(x2t_turned, it * BPI + bl + 1)
                        if inside(it, BPI, bl - 1, NB):
                            act.wait_ge(logits_done, it * BPI + bl)
                        act.activation(X2T[:, :, :].rearrange("p k l -> p (k l)"), bank(6)[:, 0:KC * P], ACT.Copy
                                       ).then_inc(x2t_ready, 1)
                if j == 3:
                    bl = (loc - 15) // G
                    if inside(it, BPI, bl, NB):
                        act.wait_ge(route_step, it * BPI * 17 + 17 * bl + 2)
                        act.activation(ge[:, :], mx[:, 0:2], ACT.Exp, scale=-1.0).then_inc(gate_exp, 1)

                if 9 <= loc < 15 and inside(it, 1, 0, NE):
                    i = loc - 9
                    if i == 0:
                        act.wait_ge(raw_in, it * 48 + 48)
                        if inside(it, 1, -1, NE):
                            act.wait_ge(split_out, it * 32)
                    act.activation(split_chunk(0, i), w_raw[:, i * CHW:(i + 1) * CHW], ACT.Copy).then_inc(high_ready, 1)

            attention_blocks(act, step)
            experts_scalar(act)

        @block.tensor
        def _(pe):
            pe.wait_ge(setup_in, 16 * N_SETUP)
            pe.wait_ge(pool_const, 13)
            for n in range(4):
                for k in range(KC):
                    for c in range(KC):
                        ins = pe.transpose(bank(n)[:, k * D + c * P:k * D + (c + 1) * P],
                                           W_in[n][:, c, k * P:(k + 1) * P], ident[:, :])
                ins.then_inc(wt_turned, 1)
            for k in range(KC):
                pe.transpose(bank(4)[:, k * NE:(k + 1) * NE], Wr_in[:, k * P:(k + 1) * P], ident[0:NE, 0:NE])
            ins = pe.transpose(bank(4)[:, P:P + NB], delta_in, ident[0:NB, 0:NB])
            ins.then_inc(wt_turned, 1)
            pe.wait_ge(wt_ready, 8)
            pe.wait_ge(dve_const, 20)

            def step(it, loc):
                ul, s, j = loc // 8, loc % 8, loc % G
                if inside(it, SPI, loc, NSTEP):
                    if s == 0:
                        pe.wait_ge(pj_free, it * UPI * FILLS + FILLS * ul + 6)
                        pe.wait_ge(q_rounded, it * UPI * 2 + 2 * (ul + 1))
                        pe.wait_ge(k_rounded, it * UPI * 2 + 2 * (ul + 1))
                    if inside(it, SPI, loc - 2, NSTEP):
                        pe.wait_ge(max_ready, it * SPI + loc - 1)
                    b = (s // G) * L
                    rows = slice(PADH * j, PADH * (j + 1))
                    for g in range(G):
                        ins = pe.matmul(bank(loc % 2)[:, g * P:(g + 1) * P], QR[rows, ul % 2, g, b:b + L],
                                        KR[rows, ul % 2, g, b:b + L], start=True, stop=True)
                    ins.then_inc(s1_done, 1)
                if inside(it, SPI, loc - 2, NSTEP):
                    k = loc - 2
                    kj, ku, kb = k % G, (k // 8) % 2, ((k % 8) // G) * L
                    pe.wait_ge(max_ready, it * SPI + k + 1)
                    if inside(it, SPI, k - 2, NSTEP):
                        pe.wait_ge(probs_ready, it * SPI + k - 1)
                    pe.matmul(bank(2 + k % 2), ones_r[:, :], NMD[:, k % 2, :, :].rearrange("p g l -> p (g l)"),
                              start=True, stop=False).then_inc(max_used, 1)
                    rows = slice(PADH * kj, PADH * (kj + 1))
                    for g in range(G):
                        ins = pe.matmul(bank(2 + k % 2)[:, g * P:(g + 1) * P], K[rows, ku, g, kb:kb + L],
                                        Q[rows, ku, g, kb:kb + L], start=False, stop=(g == G - 1))
                    ins.then_inc(s2_done, 1)
                if inside(it, SPI, loc - 3, NSTEP):
                    k = loc - 3
                    kj, ku, kb = k % G, (k // 8) % 2, (k % 8) // G
                    pe.wait_ge(probs_ready, it * SPI + k + 1)
                    if k % 8 == 0:
                        pe.wait_ge(pj_free, it * UPI * FILLS + FILLS * (k // 8 + 1))
                    if kj == 0 and inside(it, BPI, k // G - 1, NB):
                        pe.wait_ge(ot_ready, it * BPI + k // G)
                    for g in range(G):
                        ins = pe.matmul(PS[PADH * g:PADH * (g + 1), 4, kj * P:(kj + 1) * P],
                                        V[:, ku, kb, G * g + kj, :], AT[:, k % 2, g * P:(g + 1) * P],
                                        start=True, stop=True)
                    ins.then_inc(av_done, 1)
                if s < FILLS and inside(it, UPI, ul + 1, NU):
                    f = it * UPI * FILLS + FILLS * (ul + 1) + s
                    if not (isinstance(it, int) and it * UPI + ul + 1 == 0 and s == 0):
                        pe.wait_ge(pj_free, f)
                    ub = (ul + 1) % 2
                    if s == 0:
                        pe.wait_ge(xn_ready, it * UPI * UB + UB * (ul + 2))
                    if s == 1:
                        pe.wait_ge(c_in[ub], it * 32 + 32 * ((ul + 1) // 2 + 1))
                    if s in (0, 1):
                        src = (XN, CTX)[s]
                        for k in range(KC):
                            for b in range(UB):
                                ins = pe.transpose(bank(5)[:, k * UT + b * L:k * UT + (b + 1) * L],
                                                   src[:, ub, b, k * P:(k + 1) * P], ident[:, :])
                    elif s < 6:
                        is_k = s >= 4
                        w, src = ((WqT, XNT), (WkT, CT))[is_k]
                        for h in range(2):
                            g = 2 * (s % 2) + h
                            dst = bank(5)[:, h * UT:(h + 1) * UT]
                            for k in range(KC):
                                for i, (a, c) in enumerate(SPLIT):
                                    ins = pe.matmul(dst, w[a][:, k, g, :], src[c][:, k, :], start=(k == 0 and i == 0),
                                                    stop=(k == KC - 1 and i == 2 and not is_k))
                            if is_k:
                                if s == 4 and h == 0:
                                    pe.wait_ge(delta_rounded, it * UPI + ul + 2)
                                ins = pe.matmul(dst, delta_rows[:, :], DR[:, :], start=False, stop=True)
                    else:
                        for b in range(UB):
                            for k in range(KC):
                                for i, (a, c) in enumerate(SPLIT):
                                    ins = pe.matmul(bank(5)[:, b * D:(b + 1) * D], CT[a][:, k, b * L:(b + 1) * L],
                                                    WvT[c][:, k, :], start=(k == 0 and i == 0),
                                                    stop=(k == KC - 1 and i == 2))
                    ins.then_inc(pj_filled, 1)
                if j == 3:
                    bl = (loc - 7) // G
                    if inside(it, BPI, bl, NB):
                        pe.wait_ge(ot_ready, it * BPI + bl + 1)
                        if inside(it, BPI, bl - 1, NB):
                            pe.wait_ge(ln2_step, it * BPI * 3 + 3 * (bl - 1) + 1)
                        if inside(it, BPI, bl - 2, NB):
                            pe.wait_ge(route_step, it * BPI * 17 + 17 * (bl - 2) + 1)
                        for q in range(G):
                            ins = pe.transpose(bank(7)[:, q * P:(q + 1) * P], OT[:, q * P:(q + 1) * P], ident[:, :])
                        ins.then_inc(ott_done, 1)
                if j == 0:
                    bl = (loc - 8) // G
                    if inside(it, BPI, bl, NB):
                        pe.wait_ge(on_step, it * BPI * 2 + 2 * (bl + 1))
                        for k in range(KC):
                            ins = pe.transpose(bank(7)[:, k * P:(k + 1) * P], ON[:, k * P:(k + 1) * P], ident[:, :])
                        ins.then_inc(ot2_done, 1)
                if j == 1:
                    bl = (loc - 9) // G
                    if inside(it, BPI, bl, NB):
                        pe.wait_ge(ont_ready, it * BPI + bl + 1)
                        for k in range(KC):
                            for i, (a, c) in enumerate(SPLIT):
                                ins = pe.matmul(bank(7)[:, 0:D], ONT[a][:, k, :], WoT[c][:, k, :],
                                                start=(k == 0 and i == 0), stop=(k == KC - 1 and i == 2))
                        ins.then_inc(wo_done, 1)
                if j == 2:
                    bl = (loc - 14) // G
                    if inside(it, BPI, bl, NB):
                        pe.wait_ge(x2t_ready, it * BPI + bl + 1)
                        if inside(it, BPI, bl + 1, NB):
                            pe.wait_ge(ln2_step, it * BPI * 3 + 3 * (bl + 1) + 1)
                        for k in range(KC):
                            ins = pe.matmul(bank(7)[:, 0:NE], X2T[:, k, :], WrT[:, k, :], start=(k == 0),
                                            stop=(k == KC - 1))
                        ins.then_inc(logits_done, 1)
                if j == 3:
                    bl = (loc - 11) // G
                    if inside(it, BPI, bl, NB):
                        pe.wait_ge(xp_ready, it * BPI + bl + 1)
                        if inside(it, BPI, bl - 2, NB):
                            pe.wait_ge(route_step, it * BPI * 17 + 17 * (bl - 2) + 14)
                        for k in range(KC):
                            ins = pe.transpose(bank(6)[:, k * P:(k + 1) * P], XP[:, bl % 4, 0, k * P:(k + 1) * P],
                                               ident[:, :])
                        ins.then_inc(x2t_turned, 1)
                if j == 1:
                    bl = (loc - 17) // G
                    if inside(it, BPI, bl, NB):
                        pe.wait_ge(route_step, it * BPI * 17 + 17 * bl + 7)
                        if inside(it, BPI, bl + 1, NB):
                            pe.wait_ge(x2t_ready, it * BPI + bl + 2)
                        pe.matmul(bank(6)[:, 0:NE], before_b[:, :], Mb[:, :], start=True, stop=True)
                        pe.matmul(bank(6)[:, NE:2 * NE], ones_b[:, :], Mb[:, :], start=True, stop=True
                                  ).then_inc(rank_done, 1)

            attention_blocks(pe, step)
            experts_tensor(pe)


_INS = ['x', 'ctx_1024', 'condB_tau', 'fside_BxS2_0', 'L0_xcond_Wq', 'L0_xcond_bq', 'L0_xcond_Wk', 'L0_xcond_bk',
        'L0_xcond_Wv', 'L0_xcond_bv', 'L0_xcond_Wo', 'L0_xcond_bo', 'L0_ffn_router_w', 'L0_ffn_w_gate',
        'L0_ffn_w_up', 'L0_ffn_w_down']
_OUTS = [((NB, L, D), 'float32')]


def kernel(**inputs):
    import numpy as _np
    import concourse.bacc as _bacc
    from concourse import mybir as _mybir
    from concourse.bass_utils import run_bass_kernel_spmd as _run

    nc = _bacc.Bacc("TRN2", target_bir_lowering=False, num_devices=1)
    arrays, args = {}, []
    for name in _INS:
        a = _np.ascontiguousarray(inputs[name])
        arrays[f"in_{name}_dram"] = a
        args.append(nc.dram_tensor(f"in_{name}_dram", a.shape, _mybir.dt.from_np(a.dtype), kind="ExternalInput").ap())
    for i, (shape, dtype) in enumerate(_OUTS):
        dt = _mybir.dt.from_np(_np.dtype(dtype))
        args.append(nc.dram_tensor(f"out_{i}_dram", shape, dt, kind="ExternalOutput").ap())
    build(nc, *args)
    r = _run(nc, [arrays], core_ids=[0])
    got = tuple(r.results[0][f"out_{i}_dram"] for i in range(len(_OUTS)))
    return got[0]
```

```python
from contextlib import ExitStack

import concourse.bass as bass
from concourse import mybir

F32 = mybir.dt.float32
F32R = mybir.dt.float32r
BF16 = mybir.dt.bfloat16
I32 = mybir.dt.int32
U32 = mybir.dt.uint32
ALU = mybir.AluOpType
ACT = mybir.ActivationFunctionType
AX = mybir.AxisListType

P = 128
NB, L, D = 32, 128, 256
H, E = 16, 16
KC = D // P
G = 4
HC = H // KC
PADH = 32
NE, F = 8, 512
FC = F // P
TOK = NB * L
UB = 2
UT = UB * L
NU = NB // UB
NSTEP = NB * G
SPI = 16
BPI, UPI = SPI // G, SPI // G // UB
NIT = NSTEP // SPI
FILLS = 5
REG = TOK + P
NT = 2 * TOK // P + NE
ROWS = NE * REG + NE * P
PW = D + 2
SCALE = 0.25
TPI = 8
GUW, DNW = KC * 2 * F, FC * D
EW = GUW + DNW
SLOTS = 3
CHW = EW // 6
LN_EPS = 1e-5


SPLIT = ((0, 0), (0, 1), (1, 0))
TABLE = 25


def expert_at(place):
    return (place + NE - 1) % NE


def inside(it, per, c, total):
    return not isinstance(it, int) or 0 <= per * it + c < total


def build(nc, x, ctx_in, tau, delta, Wq, bq, Wk, bk, Wv, bv, Wo, bo, router, w_gate, w_up, w_down, out):
    routed = nc.dram_tensor("routed_rows", (ROWS, PW), F32, kind="Internal").ap()
    expert_out = nc.dram_tensor("expert_rows", (2 * TOK, D), F32, kind="Internal").ap()
    split_w = nc.dram_tensor("split_weights", (NE * P, 2 * EW), F32, kind="Internal").ap()
    x_flat = x.rearrange("b l d -> l b d")
    c_flat = ctx_in.rearrange("b l d -> l b d")
    out_flat = out.rearrange("b l d -> l b d")
    delta_round = nc.dram_tensor("delta_rounded", (NB, L), F32, kind="Internal").ap()

    with ExitStack() as stack:
        def sb(name, shape, dt=F32):
            return stack.enter_context(nc.sbuf_tensor(name, shape, dt))

        def sem(name):
            return stack.enter_context(nc.semaphore(name))

        X1 = sb("X1", [P, NB * D])
        W = sb("W", [P, SLOTS * 2 * EW], F32R)
        w_raw = sb("w_raw", [P, EW])
        ident = sb("ident", [P, P])
        WrT = sb("WrT", [P, KC, NE])
        ones_r = sb("ones_r", [P, P], F32R)
        before_b = sb("before_b", [P, P], BF16)
        ones_b = sb("ones_b", [P, P], BF16)
        bq_col = sb("bq_col", [P, KC])
        bk_col = sb("bk_col", [P, KC])
        bv_all = sb("bv_all", [P, D])
        bo_all = sb("bo_all", [P, D])
        tau_all = sb("tau_all", [P, NB])
        delta_col = sb("delta_col", [P, NB])
        delta_in = sb("delta_in", [NB, L])
        delta_r = sb("delta_r", [NB, L], F32R)
        minus_half = sb("minus_half", [P, UB])
        expert_i = sb("expert_i", [P, NE], I32)
        expert_f = sb("expert_f", [P, NE])
        base_i = sb("base_i", [P, NE], I32)
        counts = sb("counts", [P, NE])
        out_rows = sb("out_rows", [P, 2 * NB], I32)
        PAD = sb("PAD", [P, PW])
        CTX = sb("CTX", [P, 2, UB, D])
        ln_stats = sb("ln_stats", [P, UB, 6])
        ln_mv = sb("ln_mv", [P, UB, 2])
        ln_rstd = sb("ln_rstd", [P, UB])
        XN = sb("XN", [P, 2, UB, D])
        tight = sb("tight", [P, 2, 3, KC, UT])
        QR = sb("QR", [P, 2, KC, UT], F32R)
        BW = UB * 2 * KC * HC * L
        blocks = W[:, 2 * EW:2 * EW + BW].rearrange("p (b n c i l) -> p b n c i l", b=UB, n=2, c=KC, i=HC)
        DR = sb("DR", [1, 2, UT], F32R)
        at = 2 * EW + BW
        XNT, CT = ([W[:, at + (2 * i + n) * KC * UT:at + (2 * i + n + 1) * KC * UT]
                    .rearrange("p (k t) -> p k t", k=KC) for n in range(2)] for i in range(2))
        at += 4 * KC * UT
        WvT, WoT = ([W[:, at + (2 * i + n) * KC * D:at + (2 * i + n + 1) * KC * D]
                     .rearrange("p (k d) -> p k d", k=KC) for n in range(2)] for i in range(2))
        WqT, WkT = ([sb(f"{w}_{n}", [P, KC, D], F32R) for n in ("high", "low")] for w in ("WqT", "WkT"))
        V = sb("V", [P, 2, UB, H, PADH])
        NM = sb("NM", [P, 2, G])
        NMD = sb("NMD", [P, 2, G, P], F32R)
        AT = sb("AT", [P, 2, G * P])
        before = AT[:, 0, 0:P]
        OT = sb("OT", [P, G * P])
        rden = sb("rden", [P, H])
        ON = sb("ON", [P, D])
        ONT = [sb(f"ONT_{n}", [P, KC, P], F32R) for n in ("high", "low")]
        st2 = sb("st2", [P, 6])
        mv2 = sb("mv2", [P, 2])
        rstd2 = sb("rstd2", [P, 1])
        XP = sb("XP", [P, 4, 2, PW])
        X2T = sb("X2T", [P, KC, P])
        lg = sb("lg", [P, NE])
        mx = sb("mx", [P, 8])
        mi = sb("mi", [P, 8], U32)
        mif = sb("mif", [P, 2])
        M = sb("M", [P, 2, NE])
        Mb = sb("Mb", [P, NE], BF16)
        ge = sb("ge", [P, 2])
        gp = sb("gp", [P, 2])
        gs = sb("gs", [P, 2])
        gsum = sb("gsum", [P, 1])
        grec = sb("grec", [P, 1])
        rank = sb("rank", [P, NE])
        rsel = sb("rsel", [P, 2, NE])
        slot_f = sb("slot_f", [P, 2])
        slot = sb("slot", [P, 4, 2], I32)
        j_i = sb("j_i", [1, NB], I32)
        j_f = sb("j_f", [1, NB])
        t_i = sb("t_i", [1, NT], I32)
        t_f = sb("t_f", [1, NT])
        start_i = sb("start_i", [1, NE], I32)
        start_f = sb("start_f", [1, NE])
        cnt = sb("cnt", [1, NE])
        ntile = sb("ntile", [1, NE])
        ones8 = sb("ones8", [1, NE])
        tiles_placed = sb("tiles_placed", [1, NE])
        upto = sb("upto", [1, NE])
        jump = sb("jump", [1, NE])
        te_f = sb("te_f", [1, NT])
        tr_f = sb("tr_f", [1, NT])
        tw_f = sb("tw_f", [1, NT])
        place = sb("place", [1, NT])
        turn1 = sb("turn1", [1, NT])
        turn2 = sb("turn2", [1, NT])
        end_i = sb("end_i", [1, NE], I32)
        te_i = sb("te_i", [1, NT], I32)
        tw_i = sb("tw_i", [1, NT], I32)
        upto_i = sb("upto_i", [1, NE], I32)
        tr_i = sb("tr_i", [1, NT], I32)

        PS = stack.enter_context(nc.psum_tensor("PS", [P, 8, 512], F32))

        setup_in = sem("setup_in")
        pool_const = sem("pool_const")
        dve_const = sem("dve_const")
        wt_turned = sem("wt_turned")
        setup_weights = sem("setup_weights")
        blocks_cleared = sem("blocks_cleared")
        delta_high = sem("delta_high")
        delta_out = sem("delta_out")
        queries_in = [sem(f"queries_in{b}") for b in range(UB)]
        keys_in = [sem(f"keys_in{b}") for b in range(UB)]
        delta_row_in = [sem(f"delta_row_in{i}") for i in range(2)]
        wt_rounded = sem("wt_rounded")
        wt_ready = sem("wt_ready")
        tokens_high = sem("tokens_high")
        ont_high = sem("ont_high")
        x_in = [sem(f"x_in{i}") for i in range(2)]
        c_in = [sem(f"c_in{i}") for i in range(2)]
        raw_in = sem("raw_in")
        high_ready = sem("high_ready")
        low_ready = sem("low_ready")
        split_out = sem("split_out")
        weights_in = sem("weights_in")
        ln1_stats = sem("ln1_stats")
        ln1_rstd = sem("ln1_rstd")
        xn_ready = sem("xn_ready")
        x_biased = sem("x_biased")
        pj_filled = sem("pj_filled")
        pj_free = sem("pj_free")
        q_rounded = sem("q_rounded")
        k_rounded = sem("k_rounded")
        max_found = sem("max_found")
        max_used = sem("max_used")
        s1_done = sem("s1_done")
        max_ready = sem("max_ready")
        s2_done = sem("s2_done")
        probs_ready = sem("probs_ready")
        av_done = sem("av_done")
        ot_ready = sem("ot_ready")
        ott_done = sem("ott_done")
        on_step = sem("on_step")
        ot2_done = sem("ot2_done")
        ont_ready = sem("ont_ready")
        wo_done = sem("wo_done")
        ln2_step = sem("ln2_step")
        ln2_rstd = sem("ln2_rstd")
        xp_ready = sem("xp_ready")
        xp_copied = sem("xp_copied")
        x2t_turned = sem("x2t_turned")
        x2t_ready = sem("x2t_ready")
        logits_done = sem("logits_done")
        gate_exp = sem("gate_exp")
        rank_done = sem("rank_done")
        route_step = sem("route_step")
        scattered = [sem(f"scattered{i}") for i in range(4)]
        dead_in = sem("dead_in")
        rows_placed = sem("rows_placed")
        table_step = sem("table_step")
        pad_in = sem("pad_in")


        flat_v = V[:, :, :, :, :].rearrange("p u b h r -> p (u b h r)")
        past = flat_v[0:1, 0:NT * NE].rearrange("p (t e) -> p t e", e=NE)
        pastj = flat_v[0:1, NT * NE:2 * NT * NE].rearrange("p (t e) -> p t e", e=NE)
        over = flat_v[0:1, 2 * NT * NE:2 * NT * NE + NE * NB].rearrange("p (e j) -> p e j", e=NE)
        XS = XP[:, :, :, :].rearrange("p i k w -> p (i k) w")
        XST = [sb(f"XST_{n}", [P, 2, D], F32R) for n in ("high", "low")]
        HS = w_raw[:, 0:2 * F].rearrange("p (i w) -> p i w", i=2)
        SG = w_raw[:, 2 * F:4 * F].rearrange("p (i w) -> p i w", i=2)
        HST = [NMD[:, :, :, :].rearrange("p i g l -> p i (g l)"),
               sb("HST_low", [P, 2, F], F32R)]
        YS = flat_v.rearrange("p (i w) -> p i w", i=TPI)
        META = sb("META", [P, TPI, 2])
        xs_in = [sem(f"xs_in{i}") for i in range(TPI)]
        xs_turned = sem("xs_turned")
        xst_high = sem("xst_high")
        xst_ready = sem("xst_ready")
        meta_ready = sem("meta_ready")
        gu_done = sem("gu_done")
        silu_ready = sem("silu_ready")
        h_ready = sem("h_ready")
        h_turned = sem("h_turned")
        ht_high = sem("ht_high")
        ht_ready = sem("ht_ready")
        down_done = sem("down_done")
        y_ready = sem("y_ready")
        y_out = [sem(f"y_out{i}") for i in range(TPI)]
        parts_in = [sem(f"parts_in{i}") for i in range(8)]
        sum_step = sem("sum_step")
        stored = sem("stored")

        def tile_blocks(eng, step):
            for it in (-1, 0, 1):
                for loc in range(TPI):
                    step(it, loc)
            with eng.Fori(2, NT // TPI - 1) as it:
                for loc in range(TPI):
                    step(it, loc)
            for it in (NT // TPI - 1, NT // TPI):
                for loc in range(TPI):
                    step(it, loc)

        BQ = 4

        def part(q, k):
            return W[:, (k * NB + BQ * q) * D:(k * NB + BQ * (q + 1)) * D].bitcast(F32)

        def pad_regions(eng, experts):
            eng.wait_ge(table_step, 1)
            for e in experts:
                row = eng.value_load(end_i[0:1, e:e + 1], min_val=e * REG, max_val=e * REG + TOK)
                eng.dma_start(routed[bass.ds(row, P), :], PAD[:, :]).then_inc(pad_in, 16)

        def experts_sync(sp):
            for i in range(4):
                sp.wait_ge(scattered[i], 32 * NB // 4)
            sp.wait_ge(dead_in, 16 * NE)
            sp.wait_ge(pad_in, 16 * NE)
            sp.wait_ge(table_step, TABLE)
            sp.wait_ge(low_ready, 6 * NE)
            sp.wait_ge(split_out, 32 * (NE - 1))
            sp.sem_inc(rows_placed, 1)
            sp.sem_inc(weights_in, 32)
            sp.wait_ge(xs_in[3], 16)
            for p in range(1, NE):
                if p >= SLOTS:
                    done = sp.value_load(upto_i[0:1, p - SLOTS:p - SLOTS + 1], min_val=1, max_val=NT + 1)
                    sp.wait_ge(down_done, done)
                e = expert_at(p)
                w0 = (p % SLOTS) * 2 * EW
                for h in range(2):
                    c0, c1 = h * EW, (h + 1) * EW
                    sp.dma_start(W[:, w0 + c0:w0 + c1].bitcast(F32), split_w[e * P:(e + 1) * P, c0:c1]).then_inc(weights_in, 16)
                sp.wait_ge(weights_in, 32 * (p + 1))
            sp.wait_ge(down_done, NT + 1)
            for i in range(TPI):
                sp.wait_ge(y_out[i], 16 * NT // TPI)
            for q in range(NB // BQ):
                for k in range(2):
                    rows = expert_out[k * TOK + q * BQ * L:k * TOK + (q + 1) * BQ * L, :]
                    sp.dma_start(part(q, k).rearrange("p (b d) -> p b d", b=BQ),
                                 rows.rearrange("(b l) d -> l b d", b=BQ)).then_inc(parts_in[q], 16)
            for q in range(NB // BQ):
                sp.wait_ge(sum_step, 2 * (q + 1))
                sp.dma_start(out_flat[:, q * BQ:(q + 1) * BQ, :],
                             X1[:, q * BQ * D:(q + 1) * BQ * D].rearrange("p (b d) -> p b d", b=BQ)
                             ).then_inc(stored, 16)
            sp.wait_ge(stored, 16 * NB // BQ)

        def experts_pool(pool):
            def step(it, loc):
                t = loc + 1
                if inside(it, TPI, t, NT):
                    pool.wait_ge(xs_in[t % TPI], it * 16 + 16 * (t // TPI + 1))
                    if inside(it, TPI, t - TPI, NT):
                        pool.wait_ge(y_out[t % TPI], it * 16 + 16 * (t // TPI))
                    pass_waits(pool)
                    pool.tensor_copy(META[:, t % TPI, :].bitcast(I32), XS[:, t % TPI, D:PW].bitcast(I32)
                                     ).then_inc(meta_ready, 1)
                t = loc - 2
                if inside(it, TPI, t, NT):
                    pool.wait_ge(y_ready, it * TPI + t + 1)
                    pass_waits(pool)
                    pool.indirect_dma_start(
                        expert_out[:, :], bass.IndirectOffsetOnAxis(ap=META[:, t % TPI, 1:2].bitcast(U32), axis=0),
                        YS[:, t % TPI, :], None, bounds_check=2 * TOK - 1, oob_is_err=False).then_inc(y_out[t % TPI], 16)

            tile_blocks(pool, step)

        def experts_scalar(act):
            pad_regions(act, range(NE // 2, NE))
            act.wait_ge(rows_placed, 1)

            def step(it, loc):
                t = loc + 4
                if inside(it, TPI, t, NT):
                    if inside(it, TPI, t - TPI, NT):
                        act.wait_ge(xs_turned, it * TPI + t - TPI + 1)
                        act.wait_ge(meta_ready, it * TPI + t - TPI + 1)
                    row = act.value_load(tr_i[0:1, bass.ds(it * TPI + t, 1)], min_val=0, max_val=ROWS - P)
                    act.dma_start(XS[:, t % TPI, :], routed[bass.ds(row, P), :]).then_inc(xs_in[t % TPI], 16)
                t = loc + 1
                if inside(it, TPI, t, NT):
                    act.wait_ge(xs_turned, it * TPI + t + 1)
                    if inside(it, TPI, t - 2, NT):
                        act.wait_ge(gu_done, it * TPI + t - 1)
                    act.activation(XST[0][:, t % 2, :], bank(4)[:, 0:D], ACT.Copy).then_inc(xst_high, 1)
                t = loc
                if inside(it, TPI, t, NT):
                    act.wait_ge(gu_done, it * TPI + t + 1)
                    if inside(it, TPI, t - 2, NT):
                        act.wait_ge(h_ready, it * TPI + t - 1)
                    act.activation(SG[:, t % 2, :], bank(2 * (t % 2)), ACT.Silu).then_inc(silu_ready, 1)
                t = loc - 1
                if inside(it, TPI, t, NT):
                    act.wait_ge(h_turned, it * TPI + t + 1)
                    if inside(it, TPI, t - 2, NT):
                        act.wait_ge(down_done, it * TPI + t)
                    act.activation(HST[0][:, t % 2, :], bank(5), ACT.Copy).then_inc(ht_high, 1)

            tile_blocks(act, step)

        def experts_vector(dve):
            def step(it, loc):
                t = loc + 1
                if inside(it, TPI, t, NT):
                    dve.wait_ge(xst_high, it * TPI + t + 1)
                    dve.tensor_tensor(XST[1][:, t % 2, :], bank(4)[:, 0:D], XST[0][:, t % 2, :].bitcast(F32),
                                      ALU.subtract).then_inc(xst_ready, 1)
                t = loc
                if inside(it, TPI, t, NT):
                    dve.wait_ge(silu_ready, it * TPI + t + 1)
                    if inside(it, TPI, t - 2, NT):
                        dve.wait_ge(h_turned, it * TPI + t - 1)
                    dve.tensor_tensor(HS[:, t % 2, :], bank(2 * (t % 2) + 1), SG[:, t % 2, :], ALU.mult
                                      ).then_inc(h_ready, 1)
                t = loc - 1
                if inside(it, TPI, t, NT):
                    dve.wait_ge(ht_high, it * TPI + t + 1)
                    dve.tensor_tensor(HST[1][:, t % 2, :], bank(5), HST[0][:, t % 2, :].bitcast(F32),
                                      ALU.subtract).then_inc(ht_ready, 1)
                t = loc - 2
                if inside(it, TPI, t, NT):
                    dve.wait_ge(down_done, it * TPI + t + 2)
                    dve.wait_ge(meta_ready, it * TPI + t + 1)
                    if inside(it, TPI, t - TPI, NT):
                        dve.wait_ge(y_out[t % TPI], it * 16 + 16 * (t // TPI))
                    dve.tensor_scalar(YS[:, t % TPI, :], bank(6)[:, 0:D], META[:, t % TPI, 0:1], None, ALU.mult
                                      ).then_inc(y_ready, 1)

            tile_blocks(dve, step)
            for q in range(NB // BQ):
                dve.wait_ge(parts_in[q], 32)
                xq = X1[:, q * BQ * D:(q + 1) * BQ * D]
                dve.tensor_tensor(xq, xq, part(q, 0), ALU.add).then_inc(sum_step, 1)
                dve.wait_ge(sum_step, 2 * q + 1)
                dve.tensor_tensor(xq, xq, part(q, 1), ALU.add).then_inc(sum_step, 1)

        def experts_tensor(pe):
            pe.sem_inc(down_done, 1)
            pe.wait_ge(low_ready, 6 * NE)
            pe.wait_ge(table_step, TABLE)

            def ring_at(it, t):
                w0 = pe.value_load(te_i[0:1, bass.ds(it * TPI + t, 1)], min_val=0, max_val=(SLOTS - 1) * 2 * EW)
                loaded = pe.value_load(tw_i[0:1, bass.ds(it * TPI + t, 1)], min_val=32, max_val=32 * NE)
                return w0, loaded

            def column_at(it, t):
                if not inside(it, TPI, t, NT):
                    return None
                return pe.value_load(te_i[0:1, bass.ds(it * TPI + t, 1)], min_val=0, max_val=(SLOTS - 1) * 2 * EW),

            held = {}

            def step(it, loc):
                if loc == 0:
                    held[-2] = column_at(it, -2)
                    if inside(it, TPI, 0, NT):
                        held[0] = ring_at(it, 0)
                    else:
                        held[-1] = column_at(it, -1)
                t = loc + 1
                if inside(it, TPI, t, NT):
                    pe.wait_ge(xs_in[t % TPI], it * 16 + 16 * (t // TPI + 1))
                    if inside(it, TPI, t - 1, NT):
                        pe.wait_ge(xst_ready, it * TPI + t)
                    for k in range(KC):
                        ins = pe.transpose(bank(4)[:, k * P:(k + 1) * P], XS[:, t % TPI, k * P:(k + 1) * P], ident[:, :])
                    ins.then_inc(xs_turned, 1)
                t = loc
                if inside(it, TPI, t, NT):
                    w0, loaded = held[loc]
                    pe.wait_ge(weights_in, loaded)
                    pe.wait_ge(xst_ready, it * TPI + t + 1)
                    if inside(it, TPI, t - 2, NT):
                        pe.wait_ge(h_ready, it * TPI + t - 1)
                    for n in range(2):
                        for k in range(KC):
                            for i, (a, b) in enumerate(SPLIT):
                                ins = pe.matmul(bank(2 * (t % 2) + n), XST[a][:, t % 2, k * P:(k + 1) * P],
                                                W[:, bass.ds(w0 + (b * EW + (2 * k + n) * F), F)],
                                                start=(k == 0 and i == 0), stop=(k == KC - 1 and i == 2))
                    ins.then_inc(gu_done, 1)
                    if loc == 0:
                        held[-1] = column_at(it, -1)
                    if loc + 1 < TPI:
                        held[loc + 1] = ring_at(it, t + 1)
                t = loc - 1
                if inside(it, TPI, t, NT):
                    pe.wait_ge(h_ready, it * TPI + t + 1)
                    if inside(it, TPI, t - 1, NT):
                        pe.wait_ge(ht_ready, it * TPI + t)
                    for c in range(FC):
                        ins = pe.transpose(bank(5)[:, c * P:(c + 1) * P], HS[:, t % 2, c * P:(c + 1) * P], ident[:, :])
                    ins.then_inc(h_turned, 1)
                t = loc - 2
                if inside(it, TPI, t, NT):
                    w0 = held[t][0]
                    pe.wait_ge(ht_ready, it * TPI + t + 1)
                    if inside(it, TPI, t - 1, NT):
                        pe.wait_ge(y_ready, it * TPI + t)
                    for c in range(FC):
                        for i, (a, b) in enumerate(SPLIT):
                            ins = pe.matmul(bank(6)[:, 0:D], HST[a][:, t % 2, c * P:(c + 1) * P],
                                            W[:, bass.ds(w0 + (b * EW + GUW + c * D), D)],
                                            start=(c == 0 and i == 0), stop=(c == FC - 1 and i == 2))
                    ins.then_inc(down_done, 1)

            tile_blocks(pe, step)

        waits_met = {nc.vector: sem("dve_waits_met"), nc.gpsimd: sem("pool_waits_met"),
                     nc.scalar: sem("act_waits_met"), nc.sync: sem("sp_waits_met")}

        def pass_waits(eng):
            eng.sem_inc(waits_met[eng], 1)

        block = stack.enter_context(nc.Block())

        def bank(i):
            return PS[:, i, :]

        def split_chunk(part, i):
            return W[:, part * EW + i * CHW:part * EW + (i + 1) * CHW]

        def weights_of(w):
            return w.rearrange("(c p) d -> p c d", p=P)

        N_SETUP = 2 + 3
        N_WEIGHTS = 5 + 1
        N_CLEARED = UB * 2 * KC

        def attention_blocks(eng, step):
            for it in (-1, 0, 1):
                for loc in range(SPI):
                    step(it, loc)
            with eng.Fori(2, NIT - 1) as it:
                for loc in range(SPI):
                    step(it, loc)
            for it in (NIT - 1, NIT):
                for loc in range(SPI):
                    step(it, loc)

        W_in = [w_raw[:, i * KC * D:(i + 1) * KC * D].rearrange("p (c d) -> p c d", c=KC) for i in range(4)]
        Wr_in = w_raw[0:NE, 4 * KC * D:4 * KC * D + D]

        @block.sync
        def _(sp):
            for w, t in zip((Wq, Wk, Wv, Wo), W_in):
                sp.dma_start(t, weights_of(w)).then_inc(setup_weights, 16)
            sp.dma_start(Wr_in, router).then_inc(setup_weights, 16)
            sp.dma_start(delta_in[:, :], delta).then_inc(setup_weights, 16)

            def step(it, loc):
                ul = loc // 8
                blocks_step(it, loc)
                weights_step(it, loc)
                if loc % 8 != 0:
                    return
                if inside(it, UPI, ul + 2, NU):
                    if inside(it, UPI, ul, NU):
                        sp.wait_ge(ln1_stats, it * UPI * 4 + 4 * (ul + 1))
                    b = it * (UPI * UB) + UB * (ul + 2)
                    dst = X1[:, bass.ds(b * D, UB * D)].rearrange("p (b d) -> p b d", b=UB)
                    sp.dma_start(dst, x_flat[:, bass.ds(b, UB), :]).then_inc(x_in[ul % 2], 16)
                if inside(it, UPI, ul + 2, NU):
                    if inside(it, UPI, ul, NU):
                        sp.wait_ge(pj_filled, it * UPI * FILLS + FILLS * ul + 2)
                    b = it * (UPI * UB) + UB * (ul + 2)
                    sp.dma_start(CTX[:, ul % 2, :, :], c_flat[:, bass.ds(b, UB), :]).then_inc(c_in[ul % 2], 16)
                if isinstance(it, int) and it * UPI + ul == -2:
                    for v, t in ((bv, bv_all), (bo, bo_all), (tau, tau_all)):
                        sp.dma_start(t[:, :], v.partition_broadcast(P)).then_inc(setup_in, 16)
                    for v, t in ((bq, bq_col), (bk, bk_col)):
                        sp.dma_start(t[:, :], v.rearrange("(c p) -> p c", p=P), allow_slow_non_contiguous=True
                                     ).then_inc(setup_in, 16)
                    sp.wait_ge(delta_high, 1)
                    sp.dma_start(delta_round, delta_r[:, :].bitcast(F32)).then_inc(delta_out, 16)
                    sp.wait_ge(delta_out, 16)

            def to_blocks(ul, b, n, arrived):
                pass_waits(sp)
                for i in range(HC):
                    rows = slice(E * i, E * (i + 1))
                    sp.dma_start(blocks[rows, b, n, :, i, :].bitcast(F32),
                                 tight[rows, ul % 2, n, :, b * L:(b + 1) * L]).then_inc(arrived[b], 16)

            def blocks_step(it, loc):
                ul, s = loc // 8, loc % 8
                if s == 0 and inside(it, UPI, ul, NU):
                    sp.wait_ge(k_rounded, it * UPI + ul + 1)
                    if inside(it, UPI, ul - 1, NU):
                        pass_waits(sp)
                        sp.wait_ge(s1_done, it * SPI + 8 * ul)
                    to_blocks(ul, 1, 1, keys_in)
                if s == 2 and inside(it, UPI, ul, NU):
                    sp.wait_ge(q_rounded, it * UPI + ul + 1)
                    if inside(it, UPI, ul - 1, NU):
                        pass_waits(sp)
                        sp.wait_ge(s2_done, it * SPI + 8 * ul)
                    to_blocks(ul, 1, 0, queries_in)
                if s == 4 and inside(it, UPI, ul + 1, NU):
                    if isinstance(it, int) and it * UPI + ul + 1 == 0:
                        sp.wait_ge(blocks_cleared, N_CLEARED)
                    sp.wait_ge(k_rounded, it * UPI + ul + 2)
                    if inside(it, UPI, ul, NU):
                        pass_waits(sp)
                        sp.wait_ge(s1_done, it * SPI + 8 * ul + 4)
                    to_blocks(ul + 1, 0, 1, keys_in)
                    b = it * (UPI * UB) + UB * (ul + 1)
                    sp.dma_start(DR[:, (ul + 1) % 2, :].rearrange("o (b s) -> o b s", b=UB).bitcast(F32),
                                 delta_round[bass.ds(b, UB), :].unsqueeze(0)).then_inc(delta_row_in[(ul + 1) % 2], 16)
                if s == 6 and inside(it, UPI, ul + 1, NU):
                    sp.wait_ge(q_rounded, it * UPI + ul + 2)
                    if inside(it, UPI, ul, NU):
                        pass_waits(sp)
                        sp.wait_ge(s2_done, it * SPI + 8 * ul + 4)
                    to_blocks(ul + 1, 0, 0, queries_in)

            def weights_step(it, loc):
                if loc < 5 and inside(it, 1, 0, NE):
                    if not isinstance(it, int) or it * SPI + loc > 0:
                        sp.wait_ge(s1_done, it * SPI + loc)
                        pass_waits(sp)
                if loc < 2 and inside(it, 1, -1, NE - 1):
                    sp.wait_ge(low_ready, it * 6)
                    pass_waits(sp)
                    c0, c1 = loc * EW, (loc + 1) * EW
                    sp.dma_start(split_w[bass.ds((it - 1) * P, P), c0:c1], W[:, c0:c1].bitcast(F32)).then_inc(split_out, 16)
                if 2 <= loc < 5 and inside(it, 1, 0, NE):
                    if isinstance(it, int) and it == 0 and loc == 2:
                        sp.wait_ge(wt_turned, 5)
                    pass_waits(sp)
                    if loc < 4:
                        n = loc - 2
                        dst = w_raw[:, 0:GUW].rearrange("p (k n f) -> p k n f", k=KC, n=2)
                        src = (w_gate, w_up)[n][bass.ds(it, 1), :, :].rearrange("o (k p) f -> p (o k) f", p=P)
                        sp.dma_start(dst[:, :, n, :], src).then_inc(raw_in, 16)
                    else:
                        dst = w_raw[:, GUW:EW].rearrange("p (c d) -> p c d", c=FC)
                        src = w_down[bass.ds(it, 1), :, :].rearrange("o (c p) d -> p (o c) d", p=P)
                        sp.dma_start(dst, src).then_inc(raw_in, 16)

            attention_blocks(sp, step)

            sp.wait_ge(pool_const, 13)
            for t in range(NE):
                sp.dma_start(routed[NE * REG + t * P:NE * REG + (t + 1) * P, :], PAD[:, :]).then_inc(dead_in, 16)
            pad_regions(sp, range(0, NE // 2))
            experts_sync(sp)

        @block.gpsimd
        def _(pool):
            def const(ins):
                ins.then_inc(pool_const, 1)

            const(pool.memset(ident[:, :], 0.0))
            const(pool.memset(before, 1.0))
            const(pool.memset(minus_half[:, :], -0.5))
            const(pool.memset(PAD[:, :], 0.0))
            const(pool.iota(expert_i[:, :], [[1, NE]], base=0, channel_multiplier=0))
            const(pool.iota(base_i[:, :], [[REG, NE]], base=0, channel_multiplier=0))
            const(pool.iota(out_rows[:, :], [[TOK, 2], [L, NB]], base=0, channel_multiplier=1))
            const(pool.iota(j_i[:, :], [[P, NB]], base=0, channel_multiplier=0))
            const(pool.iota(t_i[:, :], [[1, NT]], base=0, channel_multiplier=0))
            pool.wait_ge(pool_const, 9)
            const(pool.affine_select(out=ident[:, :], in_=ident[:, :], compare_op=ALU.not_equal, fill=1.0,
                                     base=0, pattern=[[-1, P]], channel_multiplier=1))
            const(pool.affine_select(out=before, in_=before, compare_op=ALU.is_gt, fill=0.0,
                                     base=0, pattern=[[1, P]], channel_multiplier=-1))
            const(pool.iota(PAD[:, D + 1:D + 2].bitcast(I32), [[0, 1]], base=2 * TOK, channel_multiplier=1))
            const(pool.memset(V[:, :, :, :, :], 0.0))
            pool.wait_ge(pool_const, 13)
            const(pool.memset(V[:, :, :, :, E:E + 1], 1.0))

            def step(it, loc):
                ul, s, j = loc // 8, loc % 8, loc % G
                if s == 3 and inside(it, UPI, ul + 2, NU):
                    pool.wait_ge(ln1_stats, it * UPI * 4 + 4 * (ul + 3))
                    if inside(it, UPI, ul + 1, NU):
                        pool.wait_ge(xn_ready, it * UPI * UB + UB * (ul + 2))
                    pass_waits(pool)
                    pool.tensor_scalar(ln_rstd[:, :], ln_mv[:, :, 1], LN_EPS, None, ALU.add).then_inc(ln1_rstd, 1)
                    pool.wait_ge(ln1_rstd, it * UPI * 2 + 2 * (ul + 2) + 1)
                    pool.tensor_tensor(ln_rstd[:, :], ln_rstd[:, :], minus_half[:, :], ALU.pow).then_inc(ln1_rstd, 1)
                if s == 7 and inside(it, UPI, ul + 2, NU):
                    pool.wait_ge(xn_ready, it * UPI * UB + UB * (ul + 3))
                    if isinstance(it, int) and it * UPI + ul + 2 == 0:
                        pool.wait_ge(setup_in, 16 * N_SETUP)
                    for b in range(UB):
                        xb = X1[:, bass.ds((it * (UPI * UB) + UB * (ul + 2) + b) * D, D)]
                        pool.tensor_tensor(xb, xb, bo_all[:, :], ALU.add).then_inc(x_biased, 1)
                if j == 1:
                    bl = (loc - 9) // G
                    if inside(it, BPI, bl, NB):
                        pool.wait_ge(ln2_step, it * BPI * 3 + 3 * (bl + 1))
                        if inside(it, BPI, bl - 1, NB):
                            pool.wait_ge(xp_ready, it * BPI + bl)
                        pass_waits(pool)
                        pool.tensor_scalar(rstd2[:, :], mv2[:, 1:2], LN_EPS, None, ALU.add).then_inc(ln2_rstd, 1)
                        pool.wait_ge(ln2_rstd, it * BPI * 2 + 2 * bl + 1)
                        pool.tensor_tensor(rstd2[:, :], rstd2[:, :], minus_half[:, 0:1], ALU.pow).then_inc(ln2_rstd, 1)
                if j == 2:
                    bl = (loc - 10) // G
                    if inside(it, BPI, bl, NB):
                        if inside(it, BPI, bl - 4, NB):
                            pool.wait_ge(scattered[bl % 4], it * 32 + 32 * (bl // 4))
                        pool.wait_ge(xp_ready, it * BPI + bl + 1)
                        pass_waits(pool)
                        pool.tensor_copy(XP[:, bl % 4, 1, 0:D], XP[:, bl % 4, 0, 0:D]).then_inc(xp_copied, 1)
                        for k in range(2):
                            pool.tensor_copy(XP[:, bl % 4, k, D + 1:D + 2].bitcast(I32),
                                             out_rows[:, bass.ds(it * BPI + bl + k * NB, 1)]).then_inc(xp_copied, 1)
                if j == 2:
                    bl = (loc - 18) // G
                    if inside(it, BPI, bl, NB):
                        pool.wait_ge(route_step, it * BPI * 17 + 17 * (bl + 1))
                        pool.wait_ge(xp_copied, it * BPI * 3 + 3 * (bl + 1))
                        pass_waits(pool)
                        for k in range(2):
                            pool.indirect_dma_start(
                                routed[:, :], bass.IndirectOffsetOnAxis(ap=slot[:, bl % 4, k:k + 1].bitcast(U32), axis=0),
                                XP[:, bl % 4, k, :], None).then_inc(scattered[bl % 4], 16)

                if 10 <= loc and inside(it, 1, 0, NE):
                    i = loc - 10
                    pool.wait_ge(high_ready, it * 6 + i + 1)
                    pool.tensor_tensor(split_chunk(1, i), w_raw[:, i * CHW:(i + 1) * CHW],
                                       split_chunk(0, i).bitcast(F32), ALU.subtract).then_inc(low_ready, 1)

            attention_blocks(pool, step)
            experts_pool(pool)

        @block.vector
        def _(dve):
            def const(ins):
                ins.then_inc(dve_const, 1)

            const(dve.memset(ones_b[:, :], 1.0))
            dve.wait_ge(pool_const, 9)
            const(dve.tensor_copy(expert_f[:, :], expert_i[:, :]))
            const(dve.tensor_copy(counts[:, :], base_i[:, :]))
            const(dve.tensor_copy(start_f[:, :], base_i[0:1, :]))
            const(dve.tensor_copy(j_f[:, :], j_i[:, :]))
            const(dve.tensor_copy(t_f[:, :], t_i[:, :]))
            const(dve.memset(ones8[:, :], 1.0))
            dve.wait_ge(pool_const, 11)
            const(dve.tensor_scalar(ones_r[:, :], ident[:, :], 0.0, 1.0, ALU.mult, ALU.add))
            const(dve.tensor_copy(before_b[:, :], before))
            for n, w in enumerate((WqT, WkT, WvT, WoT)):
                dve.wait_ge(wt_rounded, n + 1)
                high, low = (t[:, :, :].rearrange("p k d -> p (k d)") for t in w)
                dve.tensor_tensor(low, bank(n), high.bitcast(F32), ALU.subtract).then_inc(wt_ready, 1)
            dve.wait_ge(wt_turned, 5)
            dve.tensor_copy(WrT[:, :, :].rearrange("p k e -> p (k e)"), bank(4)[:, 0:KC * NE]).then_inc(wt_ready, 1)
            dve.tensor_scalar(delta_col[:, :], bank(4)[:, P:P + NB], SCALE, None, ALU.mult).then_inc(wt_ready, 1)

            def clear_blocks(k):
                dve.tensor_scalar(blocks[:, k // 4, (k // 2) % 2, k % 2, :, :], ident[:, :].unsqueeze(1)
                                  .to_broadcast([P, HC, L]), 0.0, None, ALU.mult).then_inc(blocks_cleared, 1)

            def route(k, ins):
                ins.then_inc(route_step, 1)

            def step(it, loc):
                ul, s, j = loc // 8, loc % 8, loc % G
                u = it * UPI
                if inside(it, SPI, loc, NSTEP):
                    dve.wait_ge(s1_done, it * SPI + loc + 1)
                    if inside(it, SPI, loc - 2, NSTEP):
                        dve.wait_ge(max_ready, it * SPI + loc - 1)
                    dve.tensor_reduce(NM[:, loc % 2, :], bank(loc % 2).rearrange("p (g s) -> p g s", g=G),
                                      AX.X, ALU.max, negate=True).then_inc(max_found, 1)
                if s == 3 and inside(it, UPI, ul + 2, NU):
                    dve.wait_ge(x_in[ul % 2], it * 16 * UPI // 2 + 16 * ((ul + 2) // 2 + 1))
                    if inside(it, UPI, ul + 1, NU):
                        dve.wait_ge(ln1_rstd, it * UPI * 2 + 2 * (ul + 2))
                        dve.wait_ge(xn_ready, it * UPI * UB + UB * (ul + 2))
                    base = it * (UPI * UB * D) + UB * (ul + 2) * D
                    pass_waits(dve)
                    for b in range(UB):
                        dve.bn_stats(ln_stats[:, b, :], X1[:, bass.ds(base + b * D, D)]).then_inc(ln1_stats, 1)
                    dve.wait_ge(ln1_stats, it * UPI * 4 + 4 * (ul + 2) + 2)
                    pass_waits(dve)
                    for b in range(UB):
                        dve.bn_aggr(ln_mv[:, b, :], ln_stats[:, b, :]).then_inc(ln1_stats, 1)
                if s == 6 and inside(it, UPI, ul + 2, NU):
                    dve.wait_ge(ln1_rstd, it * UPI * 2 + 2 * (ul + 3))
                    if inside(it, UPI, ul, NU):
                        dve.wait_ge(pj_filled, it * UPI * FILLS + FILLS * ul + 1)
                    base = it * (UPI * UB * D) + UB * (ul + 2) * D
                    for b in range(UB):
                        dve.tensor_scalar(XN[:, ul % 2, b, :], X1[:, bass.ds(base + b * D, D)], ln_mv[:, b, 0:1],
                                          ln_rstd[:, b:b + 1], ALU.subtract, ALU.mult).then_inc(xn_ready, 1)
                if s in (0, 1) and inside(it, UPI, ul + 1, NU):
                    dve.wait_ge(tokens_high, it * UPI * 2 + 2 * (ul + 1) + s + 1)
                    high, low = (t[:, :, :].rearrange("p k t -> p (k t)") for t in (XNT, CT)[s])
                    dve.tensor_tensor(low, bank(5), high.bitcast(F32), ALU.subtract).then_inc(pj_free, 1)
                if s == 2 and inside(it, UPI, ul + 1, NU):
                    dve.wait_ge(pj_filled, it * UPI * FILLS + FILLS * (ul + 1) + s + 1)
                    if inside(it, UPI, ul - 1, NU):
                        for b in range(UB):
                            dve.wait_ge(queries_in[b], (it * UPI + ul) * (16 * HC))
                        dve.wait_ge(s2_done, it * SPI + 8 * ul)
                    if isinstance(it, int) and it * UPI + ul + 1 == 0:
                        dve.wait_ge(setup_in, 16 * N_SETUP)
                    for c in range(KC):
                        ts = tau_all[:, bass.ds(it * (UPI * UB) + UB * (ul + 1), UB)]
                        ins = dve.scalar_tensor_tensor(
                            out=tight[:, (ul + 1) % 2, 0, c, :].rearrange("p (b l) -> p b l", b=UB),
                            in0=bank(5)[:, c * UT:(c + 1) * UT].rearrange("p (b l) -> p b l", b=UB),
                            scalar=bq_col[:, c:c + 1], in1=ts.unsqueeze(2).to_broadcast([P, UB, L]),
                            op0=ALU.add, op1=ALU.mult)
                    ins.then_inc(pj_free, 1)
                if isinstance(it, int) and it == -1 and 8 <= loc < 8 + N_CLEARED // 2:
                    clear_blocks(loc - 8)
                if s == 4 and inside(it, UPI, ul + 1, NU):
                    dve.wait_ge(pj_filled, it * UPI * FILLS + FILLS * (ul + 1) + s + 1)
                    if isinstance(it, int) and it * UPI + ul + 1 == 0:
                        dve.wait_ge(pool_const, 14)
                    if inside(it, UPI, ul - 1, NU):
                        dve.wait_ge(av_done, it * SPI + 8 * ul)
                    for b in range(UB):
                        ins = dve.tensor_tensor(
                            V[:, (ul + 1) % 2, b, :, 0:E],
                            bank(5)[:, b * D:(b + 1) * D].rearrange("p (h e) -> p h e", h=H),
                            bv_all[:, :].rearrange("p (h e) -> p h e", h=H), ALU.add)
                    ins.then_inc(pj_free, 1)
                if j == 3:
                    bl = (loc - 7) // G
                    if inside(it, BPI, bl, NB):
                        dve.wait_ge(ott_done, it * BPI + bl + 1)
                        by_head = bank(7).rearrange("p (h r) -> p h r", r=PADH)
                        if inside(it, BPI, bl - 1, NB):
                            dve.wait_ge(on_step, it * BPI * 2 + 2 * bl)
                        dve.reciprocal(rden[:, :], by_head[:, :, E]).then_inc(on_step, 1)
                        dve.wait_ge(on_step, it * BPI * 2 + 2 * bl + 1)
                        if inside(it, BPI, bl - 1, NB):
                            dve.wait_ge(ot2_done, it * BPI + bl)
                        dve.tensor_tensor(ON[:, :].rearrange("p (h r) -> p h r", r=E), by_head[:, :, 0:E],
                                          rden[:, :].unsqueeze(2).to_broadcast([P, H, E]), ALU.mult
                                          ).then_inc(on_step, 1)
                if j == 0:
                    bl = (loc - 8) // G
                    if inside(it, BPI, bl, NB):
                        dve.wait_ge(ont_high, it * BPI + bl + 1)
                        high, low = (t[:, :, :].rearrange("p k l -> p (k l)") for t in ONT)
                        dve.tensor_tensor(low, bank(7)[:, 0:KC * P], high.bitcast(F32), ALU.subtract
                                          ).then_inc(ont_ready, 1)
                if j == 1:
                    bl = (loc - 9) // G
                    if inside(it, BPI, bl, NB):
                        dve.wait_ge(wo_done, it * BPI + bl + 1)
                        dve.wait_ge(x_biased, it * BPI + bl + 1)
                        xb = X1[:, bass.ds((it * BPI + bl) * D, D)]
                        dve.tensor_tensor(xb, bank(7)[:, 0:D], xb, ALU.add).then_inc(ln2_step, 1)
                        dve.wait_ge(ln2_step, it * BPI * 3 + 3 * bl + 1)
                        pass_waits(dve)
                        dve.bn_stats(st2[:, :], xb).then_inc(ln2_step, 1)
                        dve.wait_ge(ln2_step, it * BPI * 3 + 3 * bl + 2)
                        if inside(it, BPI, bl - 1, NB):
                            dve.wait_ge(ln2_rstd, it * BPI * 2 + 2 * bl)
                            dve.wait_ge(xp_ready, it * BPI + bl)
                        pass_waits(dve)
                        dve.bn_aggr(mv2[:, :], st2[:, :]).then_inc(ln2_step, 1)
                if j == 2:
                    bl = (loc - 10) // G
                    if inside(it, BPI, bl, NB):
                        dve.wait_ge(ln2_rstd, it * BPI * 2 + 2 * (bl + 1))
                        if inside(it, BPI, bl - 4, NB):
                            dve.wait_ge(scattered[bl % 4], it * 32 + 32 * (bl // 4))
                        dve.tensor_scalar(XP[:, bl % 4, 0, 0:D], X1[:, bass.ds((it * BPI + bl) * D, D)], mv2[:, 0:1],
                                          rstd2[:, 0:1], ALU.subtract, ALU.mult).then_inc(xp_ready, 1)
                if j == 2:
                    bl = (loc - 14) // G
                    if inside(it, BPI, bl, NB):
                        r0 = it * BPI * 17 + 17 * bl
                        if inside(it, BPI, bl - 1, NB):
                            dve.wait_ge(route_step, r0)
                        dve.wait_ge(logits_done, it * BPI + bl + 1)
                        route(1, dve.tensor_copy(lg[:, :], bank(7)[:, 0:NE]))
                        dve.wait_ge(route_step, r0 + 1)
                        pass_waits(dve)
                        route(2, dve.max(mx[:, :], lg[:, :]))
                        dve.wait_ge(route_step, r0 + 2)
                        pass_waits(dve)
                        route(3, dve.max_index(mi[:, :], mx[:, :], lg[:, :]))
                        dve.wait_ge(route_step, r0 + 3)
                        route(4, dve.tensor_copy(mif[:, :], mi[:, 0:2]))
                        dve.wait_ge(route_step, r0 + 4)
                        for k in range(2):
                            route(5 + k, dve.tensor_scalar(M[:, k, :], expert_f[:, :], mif[:, k:k + 1], None, ALU.is_equal))
                        dve.wait_ge(route_step, r0 + 6)
                        route(7, dve.tensor_tensor(Mb[:, :], M[:, 0, :], M[:, 1, :], ALU.add))
                if j == 3:
                    bl = (loc - 15) // G
                    if inside(it, BPI, bl, NB):
                        r0 = it * BPI * 17 + 17 * bl
                        dve.wait_ge(gate_exp, it * BPI + bl + 1)
                        route(8, dve.tensor_scalar(gp[:, :], ge[:, :], 1.0, None, ALU.add))
                        dve.wait_ge(route_step, r0 + 8)
                        route(9, dve.reciprocal(gs[:, :], gp[:, :]))
                        dve.wait_ge(route_step, r0 + 9)
                        route(10, dve.scalar_tensor_tensor(out=gsum[:, :], in0=gs[:, 0:1], scalar=1e-10,
                                                           in1=gs[:, 1:2], op0=ALU.add, op1=ALU.add))
                        dve.wait_ge(route_step, r0 + 10)
                        route(11, dve.reciprocal(grec[:, :], gsum[:, :]))
                        dve.wait_ge(route_step, r0 + 11)
                        route(12, dve.tensor_scalar(XP[:, bl % 4, :, D], gs[:, :], grec[:, 0:1], None, ALU.mult))
                if j == 1:
                    bl = (loc - 17) // G
                    if inside(it, BPI, bl, NB):
                        r0 = it * BPI * 17 + 17 * bl
                        dve.wait_ge(rank_done, it * BPI + bl + 1)
                        dve.wait_ge(route_step, r0 + 12)
                        route(13, dve.tensor_tensor(rank[:, :], bank(6)[:, 0:NE], counts[:, :], ALU.add))
                        dve.wait_ge(route_step, r0 + 13)
                        route(14, dve.tensor_tensor(counts[:, :], bank(6)[:, NE:2 * NE], counts[:, :], ALU.add))
                        route(15, dve.tensor_tensor(rsel[:, :, :], M[:, :, :],
                                                    rank[:, :].unsqueeze(1).to_broadcast([P, 2, NE]), ALU.mult))
                        dve.wait_ge(route_step, r0 + 15)
                        route(16, dve.tensor_reduce(slot_f[:, :], rsel[:, :, :], AX.X, ALU.add))
                        dve.wait_ge(route_step, r0 + 16)
                        route(17, dve.tensor_copy(slot[:, bl % 4, :], slot_f[:, :]))

            attention_blocks(dve, step)

            dve.wait_ge(route_step, 17 * NB)
            dve.tensor_copy(end_i[:, :], counts[0:1, :]).then_inc(table_step, 1)
            dve.tensor_tensor(cnt[:, :], counts[0:1, :], start_f[:, :], ALU.subtract).then_inc(table_step, 1)
            dve.wait_ge(table_step, 2)
            dve.tensor_tensor(over, cnt[:, :].unsqueeze(2).to_broadcast([1, NE, NB]),
                              j_f[:, :].unsqueeze(1).to_broadcast([1, NE, NB]), ALU.is_gt).then_inc(table_step, 1)
            dve.wait_ge(table_step, 3)
            dve.tensor_reduce(ntile[:, :], over, AX.X, ALU.add).then_inc(table_step, 1)
            dve.wait_ge(table_step, 4)
            dve.tensor_copy(tiles_placed[:, 0:1], ntile[:, NE - 1:NE]).then_inc(table_step, 1)
            dve.tensor_copy(tiles_placed[:, 1:NE], ntile[:, 0:NE - 1]).then_inc(table_step, 1)
            dve.wait_ge(table_step, 6)
            dve.tensor_tensor_scan(upto[:, :], ones8[:, :], tiles_placed[:, :], 0.0, ALU.mult, ALU.add).then_inc(table_step, 1)
            dve.tensor_scalar(jump[:, :], tiles_placed[:, :], -float(P), float(REG), ALU.mult, ALU.add).then_inc(table_step, 1)
            dve.wait_ge(table_step, 8)
            dve.tensor_scalar(jump[:, 0:1], jump[:, 0:1], -float(NE * REG), None, ALU.add).then_inc(table_step, 1)
            dve.tensor_scalar(jump[:, NE - 1:NE], jump[:, NE - 1:NE], float(REG), None, ALU.add).then_inc(table_step, 1)
            dve.tensor_tensor(past, t_f[:, :].unsqueeze(2).to_broadcast([1, NT, NE]),
                              upto[:, :].unsqueeze(1).to_broadcast([1, NT, NE]), ALU.is_ge).then_inc(table_step, 1)
            dve.tensor_scalar(upto_i[:, :], upto[:, :], 1.0, None, ALU.add).then_inc(table_step, 1)
            dve.wait_ge(table_step, 12)
            dve.tensor_tensor(pastj, past, jump[:, :].unsqueeze(1).to_broadcast([1, NT, NE]),
                              ALU.mult).then_inc(table_step, 1)
            dve.tensor_reduce(te_f[:, :], past, AX.X, ALU.add).then_inc(table_step, 1)
            dve.wait_ge(table_step, 14)
            dve.tensor_reduce(tr_f[:, :], pastj, AX.X, ALU.add).then_inc(table_step, 1)
            dve.tensor_scalar(place[:, :], te_f[:, :], float(NE - 1), None, ALU.min).then_inc(table_step, 1)
            dve.wait_ge(table_step, 16)
            dve.tensor_scalar(tr_f[:, :], tr_f[:, :], float(expert_at(0) * REG), None, ALU.add).then_inc(table_step, 1)
            dve.tensor_scalar(turn1[:, :], place[:, :], float(SLOTS), None, ALU.is_ge).then_inc(table_step, 1)
            dve.tensor_scalar(turn2[:, :], place[:, :], float(2 * SLOTS), None, ALU.is_ge).then_inc(table_step, 1)
            dve.tensor_scalar(tw_f[:, :], place[:, :], 1.0, None, ALU.add).then_inc(table_step, 1)
            dve.wait_ge(table_step, 20)
            dve.scalar_tensor_tensor(out=tr_i[:, :], in0=t_f[:, :], scalar=float(P), in1=tr_f[:, :],
                                     op0=ALU.mult, op1=ALU.add).then_inc(table_step, 1)
            dve.tensor_scalar(tw_i[:, :], tw_f[:, :], 32.0, None, ALU.mult).then_inc(table_step, 1)
            dve.tensor_tensor(turn1[:, :], turn1[:, :], turn2[:, :], ALU.add).then_inc(table_step, 1)
            dve.wait_ge(table_step, 23)
            dve.scalar_tensor_tensor(out=place[:, :], in0=turn1[:, :], scalar=-float(SLOTS), in1=place[:, :],
                                     op0=ALU.mult, op1=ALU.add).then_inc(table_step, 1)
            dve.wait_ge(table_step, 24)
            dve.tensor_scalar(te_i[:, :], place[:, :], float(2 * EW), None, ALU.mult).then_inc(table_step, 1)
            experts_vector(dve)

        @block.scalar
        def _(act):
            for n, w in enumerate((WqT, WkT, WvT, WoT)):
                act.wait_ge(wt_turned, n + 1)
                act.activation(w[0][:, :, :].rearrange("p k d -> p (k d)"), bank(n), ACT.Copy).then_inc(wt_rounded, 1)
            act.wait_ge(setup_weights, 16 * N_WEIGHTS)
            act.activation(delta_r[:, :], delta_in[:, :], ACT.Copy).then_inc(delta_high, 1)

            def step(it, loc):
                ul, s, j = loc // 8, loc % 8, loc % G
                if inside(it, SPI, loc - 1, NSTEP):
                    act.wait_ge(max_found, it * SPI + loc)
                    if inside(it, SPI, loc - 3, NSTEP):
                        act.wait_ge(max_used, it * SPI + loc - 2)
                    k = (loc - 1) % 2
                    for g in range(G):
                        ins = act.activation(NMD[:, k, g, :], ident[:, :], ACT.Copy, scale=NM[:, k, g:g + 1])
                    ins.then_inc(max_ready, 1)
                if inside(it, SPI, loc - 2, NSTEP):
                    act.wait_ge(s2_done, it * SPI + loc - 1)
                    if inside(it, SPI, loc - 4, NSTEP):
                        act.wait_ge(av_done, it * SPI + loc - 3)
                    k = loc % 2
                    pass_waits(act)
                    act.activation(AT[:, k, :], bank(2 + k), ACT.Exp, scale=SCALE,
                                   bias=delta_col[:, bass.ds(it * BPI + (loc - 2) // G, 1)]).then_inc(probs_ready, 1)
                if s in (0, 1) and inside(it, UPI, ul + 1, NU):
                    act.wait_ge(pj_filled, it * UPI * FILLS + FILLS * (ul + 1) + s + 1)
                    dst = (XNT, CT)[s]
                    act.activation(dst[0][:, :, :].rearrange("p k t -> p (k t)"), bank(5), ACT.Copy
                                   ).then_inc(tokens_high, 1)
                if s == 2 and inside(it, UPI, ul + 1, NU):
                    act.wait_ge(pj_free, it * UPI * FILLS + FILLS * (ul + 1) + s + 1)
                    if inside(it, UPI, ul - 1, NU):
                        act.wait_ge(s1_done, it * SPI + 8 * ul)
                    act.activation(QR[:, (ul + 1) % 2, :, :], tight[:, (ul + 1) % 2, 0, :, :],
                                   ACT.Copy).then_inc(q_rounded, 1)
                if s == 3 and inside(it, UPI, ul + 1, NU):
                    act.wait_ge(pj_filled, it * UPI * FILLS + FILLS * (ul + 1) + s + 1)
                    if inside(it, UPI, ul - 1, NU):
                        for b in range(UB):
                            act.wait_ge(keys_in[b], (it * UPI + ul) * (16 * HC))
                        act.wait_ge(s2_done, it * SPI + 8 * ul)
                    if isinstance(it, int) and it * UPI + ul + 1 == 0:
                        act.wait_ge(setup_in, 16 * N_SETUP)
                    for c in range(KC):
                        ins = act.activation(tight[:, (ul + 1) % 2, 2, c, :],
                                             bank(5)[:, c * UT:(c + 1) * UT], ACT.Identity, bias=bk_col[:, c:c + 1])
                    ins.then_inc(pj_free, 1)
                    act.wait_ge(pj_free, it * UPI * FILLS + FILLS * (ul + 1) + s + 1)
                    act.activation(tight[:, (ul + 1) % 2, 1, :, :].bitcast(F32R), tight[:, (ul + 1) % 2, 2, :, :],
                                   ACT.Copy).then_inc(k_rounded, 1)
                if isinstance(it, int) and it == -1 and 8 <= loc < 8 + N_CLEARED // 2:
                    k = N_CLEARED // 2 + loc - 8
                    act.activation(blocks[:, k // 4, (k // 2) % 2, k % 2, :, :],
                                   ident[:, :].unsqueeze(1).to_broadcast([P, HC, L]), ACT.Copy, scale=0.0
                                   ).then_inc(blocks_cleared, 1)
                if j == 2:
                    bl = (loc - 6) // G
                    if inside(it, BPI, bl, NB):
                        act.wait_ge(av_done, it * SPI + G * (bl + 1))
                        if inside(it, BPI, bl - 1, NB):
                            act.wait_ge(ott_done, it * BPI + bl)
                        act.activation(OT[:, :], bank(4), ACT.Copy).then_inc(ot_ready, 1)
                if j == 0:
                    bl = (loc - 8) // G
                    if inside(it, BPI, bl, NB):
                        act.wait_ge(ot2_done, it * BPI + bl + 1)
                        if inside(it, BPI, bl - 1, NB):
                            act.wait_ge(wo_done, it * BPI + bl)
                        act.activation(ONT[0][:, :, :].rearrange("p k l -> p (k l)"), bank(7)[:, 0:KC * P], ACT.Copy
                                       ).then_inc(ont_high, 1)
                if j == 3:
                    bl = (loc - 11) // G
                    if inside(it, BPI, bl, NB):
                        act.wait_ge(x2t_turned, it * BPI + bl + 1)
                        if inside(it, BPI, bl - 1, NB):
                            act.wait_ge(logits_done, it * BPI + bl)
                        act.activation(X2T[:, :, :].rearrange("p k l -> p (k l)"), bank(6)[:, 0:KC * P], ACT.Copy
                                       ).then_inc(x2t_ready, 1)
                if j == 3:
                    bl = (loc - 15) // G
                    if inside(it, BPI, bl, NB):
                        act.wait_ge(route_step, it * BPI * 17 + 17 * bl + 2)
                        act.activation(ge[:, :], mx[:, 0:2], ACT.Exp, scale=-1.0).then_inc(gate_exp, 1)

                if 9 <= loc < 15 and inside(it, 1, 0, NE):
                    i = loc - 9
                    if i == 0:
                        act.wait_ge(raw_in, it * 48 + 48)
                        if inside(it, 1, -1, NE):
                            act.wait_ge(split_out, it * 32)
                    act.activation(split_chunk(0, i), w_raw[:, i * CHW:(i + 1) * CHW], ACT.Copy).then_inc(high_ready, 1)

            attention_blocks(act, step)
            experts_scalar(act)

        @block.tensor
        def _(pe):
            pe.wait_ge(setup_weights, 16 * N_WEIGHTS)
            pe.wait_ge(pool_const, 11)
            for n in range(4):
                for k in range(KC):
                    for c in range(KC):
                        ins = pe.transpose(bank(n)[:, k * D + c * P:k * D + (c + 1) * P],
                                           W_in[n][:, c, k * P:(k + 1) * P], ident[:, :])
                ins.then_inc(wt_turned, 1)
            for k in range(KC):
                pe.transpose(bank(4)[:, k * NE:(k + 1) * NE], Wr_in[:, k * P:(k + 1) * P], ident[0:NE, 0:NE])
            ins = pe.transpose(bank(4)[:, P:P + NB], delta_in[:, :], ident[0:NB, 0:NB])
            ins.then_inc(wt_turned, 1)
            pe.wait_ge(wt_ready, 6)
            pe.wait_ge(dve_const, 9)

            def step(it, loc):
                ul, s, j = loc // 8, loc % 8, loc % G
                if inside(it, SPI, loc, NSTEP):
                    if s == 0:
                        pe.wait_ge(q_rounded, it * UPI + ul + 1)
                        pe.wait_ge(delta_row_in[ul % 2], (it + 1) * 16)
                    if j == 0:
                        pe.wait_ge(keys_in[s // G], (it * UPI + ul + 1) * (16 * HC))
                    if inside(it, SPI, loc - 2, NSTEP):
                        pe.wait_ge(max_ready, it * SPI + loc - 1)
                    b, c, i = s // G, j // 2, G * (j % 2)
                    pe.matmul(bank(loc % 2), QR[:, ul % 2, c, b * L:(b + 1) * L],
                              blocks[:, b, 1, c, i:i + G, :], start=True, stop=False)
                    pe.matmul(bank(loc % 2).rearrange("p (i s) -> p i s", i=G), ones_r[0:1, :],
                              DR[:, ul % 2, b * L:(b + 1) * L].unsqueeze(1).to_broadcast([1, G, L]),
                              start=False, stop=True).then_inc(s1_done, 1)
                if inside(it, SPI, loc - 2, NSTEP):
                    k = loc - 2
                    kj, ku, kb = k % G, (k // 8) % 2, ((k % 8) // G) * L
                    pe.wait_ge(max_ready, it * SPI + k + 1)
                    if inside(it, SPI, k - 2, NSTEP):
                        pe.wait_ge(probs_ready, it * SPI + k - 1)
                    pe.matmul(bank(2 + k % 2), ones_r[:, :], NMD[:, k % 2, :, :].rearrange("p g l -> p (g l)"),
                              start=True, stop=False).then_inc(max_used, 1)
                    if kj == 0:
                        pe.wait_ge(queries_in[(k % 8) // G], (it * UPI + k // 8 + 1) * (16 * HC))
                    if k % 8 == 0:
                        pe.wait_ge(k_rounded, it * UPI + k // 8 + 1)
                    c, i = kj // 2, G * (kj % 2)
                    ins = pe.matmul(bank(2 + k % 2), tight[:, ku, 2, c, kb:kb + L],
                                    blocks[:, (k % 8) // G, 0, c, i:i + G, :].bitcast(F32), start=False, stop=True)
                    ins.then_inc(s2_done, 1)
                if inside(it, SPI, loc - 3, NSTEP):
                    k = loc - 3
                    kj, ku, kb = k % G, (k // 8) % 2, (k % 8) // G
                    pe.wait_ge(probs_ready, it * SPI + k + 1)
                    if k % 8 == 0:
                        pe.wait_ge(pj_free, it * UPI * FILLS + FILLS * (k // 8 + 1))
                    if kj == 0 and inside(it, BPI, k // G - 1, NB):
                        pe.wait_ge(ot_ready, it * BPI + k // G)
                    for g in range(G):
                        ins = pe.matmul(PS[PADH * g:PADH * (g + 1), 4, kj * P:(kj + 1) * P],
                                        V[:, ku, kb, G * kj + g, :], AT[:, k % 2, g * P:(g + 1) * P],
                                        start=True, stop=True)
                    ins.then_inc(av_done, 1)
                if s < FILLS and inside(it, UPI, ul + 1, NU):
                    f = it * UPI * FILLS + FILLS * (ul + 1) + s
                    if not (isinstance(it, int) and it * UPI + ul + 1 == 0 and s == 0):
                        pe.wait_ge(pj_free, f)
                    ub = (ul + 1) % 2
                    if s == 0:
                        pe.wait_ge(xn_ready, it * UPI * UB + UB * (ul + 2))
                    if s == 1:
                        pe.wait_ge(c_in[ub], it * 16 + 16 * ((ul + 1) // 2 + 1))
                    if s in (0, 1):
                        src = (XN, CTX)[s]
                        for k in range(KC):
                            for b in range(UB):
                                ins = pe.transpose(bank(5)[:, k * UT + b * L:k * UT + (b + 1) * L],
                                                   src[:, ub, b, k * P:(k + 1) * P], ident[:, :])
                    elif s < 4:
                        w, src = ((WqT, XNT), (WkT, CT))[s - 2]
                        for c in range(KC):
                            for k in range(KC):
                                for i, (a, b) in enumerate(SPLIT):
                                    ins = pe.matmul(bank(5)[:, c * UT:(c + 1) * UT], w[a][:, k, c * P:(c + 1) * P],
                                                    src[b][:, k, :], start=(k == 0 and i == 0),
                                                    stop=(k == KC - 1 and i == 2))
                    else:
                        for b in range(UB):
                            for k in range(KC):
                                for i, (a, c) in enumerate(SPLIT):
                                    ins = pe.matmul(bank(5)[:, b * D:(b + 1) * D], CT[a][:, k, b * L:(b + 1) * L],
                                                    WvT[c][:, k, :], start=(k == 0 and i == 0),
                                                    stop=(k == KC - 1 and i == 2))
                    ins.then_inc(pj_filled, 1)
                if j == 3:
                    bl = (loc - 7) // G
                    if inside(it, BPI, bl, NB):
                        pe.wait_ge(ot_ready, it * BPI + bl + 1)
                        if inside(it, BPI, bl - 1, NB):
                            pe.wait_ge(ln2_step, it * BPI * 3 + 3 * (bl - 1) + 1)
                        if inside(it, BPI, bl - 2, NB):
                            pe.wait_ge(route_step, it * BPI * 17 + 17 * (bl - 2) + 1)
                        for q in range(G):
                            ins = pe.transpose(bank(7)[:, q * P:(q + 1) * P], OT[:, q * P:(q + 1) * P], ident[:, :])
                        ins.then_inc(ott_done, 1)
                if j == 0:
                    bl = (loc - 8) // G
                    if inside(it, BPI, bl, NB):
                        pe.wait_ge(on_step, it * BPI * 2 + 2 * (bl + 1))
                        for k in range(KC):
                            ins = pe.transpose(bank(7)[:, k * P:(k + 1) * P], ON[:, k * P:(k + 1) * P], ident[:, :])
                        ins.then_inc(ot2_done, 1)
                if j == 1:
                    bl = (loc - 9) // G
                    if inside(it, BPI, bl, NB):
                        pe.wait_ge(ont_ready, it * BPI + bl + 1)
                        for k in range(KC):
                            for i, (a, c) in enumerate(SPLIT):
                                ins = pe.matmul(bank(7)[:, 0:D], ONT[a][:, k, :], WoT[c][:, k, :],
                                                start=(k == 0 and i == 0), stop=(k == KC - 1 and i == 2))
                        ins.then_inc(wo_done, 1)
                if j == 2:
                    bl = (loc - 14) // G
                    if inside(it, BPI, bl, NB):
                        pe.wait_ge(x2t_ready, it * BPI + bl + 1)
                        if inside(it, BPI, bl + 1, NB):
                            pe.wait_ge(ln2_step, it * BPI * 3 + 3 * (bl + 1) + 1)
                        for k in range(KC):
                            ins = pe.matmul(bank(7)[:, 0:NE], X2T[:, k, :], WrT[:, k, :], start=(k == 0),
                                            stop=(k == KC - 1))
                        ins.then_inc(logits_done, 1)
                if j == 3:
                    bl = (loc - 11) // G
                    if inside(it, BPI, bl, NB):
                        pe.wait_ge(xp_ready, it * BPI + bl + 1)
                        if inside(it, BPI, bl - 2, NB):
                            pe.wait_ge(route_step, it * BPI * 17 + 17 * (bl - 2) + 14)
                        for k in range(KC):
                            ins = pe.transpose(bank(6)[:, k * P:(k + 1) * P], XP[:, bl % 4, 0, k * P:(k + 1) * P],
                                               ident[:, :])
                        ins.then_inc(x2t_turned, 1)
                if j == 1:
                    bl = (loc - 17) // G
                    if inside(it, BPI, bl, NB):
                        pe.wait_ge(route_step, it * BPI * 17 + 17 * bl + 7)
                        if inside(it, BPI, bl + 1, NB):
                            pe.wait_ge(x2t_ready, it * BPI + bl + 2)
                        pe.matmul(bank(6)[:, 0:NE], before_b[:, :], Mb[:, :], start=True, stop=True)
                        pe.matmul(bank(6)[:, NE:2 * NE], ones_b[:, :], Mb[:, :], start=True, stop=True
                                  ).then_inc(rank_done, 1)

            attention_blocks(pe, step)
            experts_tensor(pe)


_INS = ['x', 'ctx_1024', 'condB_tau', 'fside_BxS2_0', 'L0_xcond_Wq', 'L0_xcond_bq', 'L0_xcond_Wk', 'L0_xcond_bk',
        'L0_xcond_Wv', 'L0_xcond_bv', 'L0_xcond_Wo', 'L0_xcond_bo', 'L0_ffn_router_w', 'L0_ffn_w_gate',
        'L0_ffn_w_up', 'L0_ffn_w_down']
_OUTS = [((NB, L, D), 'float32')]


def kernel(**inputs):
    import numpy as _np
    import concourse.bacc as _bacc
    from concourse import mybir as _mybir
    from concourse.bass_utils import run_bass_kernel_spmd as _run

    nc = _bacc.Bacc("TRN2", target_bir_lowering=False, num_devices=1)
    arrays, args = {}, []
    for name in _INS:
        a = _np.ascontiguousarray(inputs[name])
        arrays[f"in_{name}_dram"] = a
        args.append(nc.dram_tensor(f"in_{name}_dram", a.shape, _mybir.dt.from_np(a.dtype), kind="ExternalInput").ap())
    for i, (shape, dtype) in enumerate(_OUTS):
        dt = _mybir.dt.from_np(_np.dtype(dtype))
        args.append(nc.dram_tensor(f"out_{i}_dram", shape, dt, kind="ExternalOutput").ap())
    build(nc, *args)
    r = _run(nc, [arrays], core_ids=[0])
    got = tuple(r.results[0][f"out_{i}_dram"] for i in range(len(_OUTS)))
    return got[0]
```
